# Optimizing a Trainium2 kernel written in Bass

```python
import numpy as np
import jax
import jax.numpy as jnp

def _softmax(x, axis=-1):
    return jax.nn.softmax(x, axis=axis)

def _gelu(x):
    return jax.nn.gelu(x, approximate=True)

def _silu(x):
    return jax.nn.silu(x)

def _sigmoid(x):
    return jax.nn.sigmoid(x)

def _layernorm(x, axis=-1, eps=1e-05):
    m = jnp.mean(x, axis=axis, keepdims=True)
    v = jnp.var(x, axis=axis, keepdims=True)
    return (x - m) / jnp.sqrt(v + eps)

def _scatter_add(tgt, idx, src, axis=0):
    return tgt.at[idx].add(src)

def _segment_sum(src, seg, n):
    return jax.ops.segment_sum(src, seg, n)
kernel_name = 'mk_gnn_resnorm_d4_gnn_r8_f40502'

def setup_inputs(seed: int=0):
    np.random.seed(seed)
    _w = jnp.asarray

    def _rec_inputs():
        import jax
        import jax.numpy as jnp
        _gk = jax.random.key(seed)
        x = -0.0001126 + 1 * jax.random.normal(jax.random.fold_in(_gk, 1), (1250, 768), jnp.float32)
        src = jax.random.randint(jax.random.fold_in(_gk, 2), (20000,), 0, 1250, jnp.int32)
        dst = jnp.minimum((1250 * jax.random.uniform(jax.random.fold_in(_gk, 3), (20000,)) ** 2.0).astype(jnp.int32), 9999)
        _o = jnp.argsort(dst, stable=True)
        src = src[_o]
        dst = dst[_o]
        edge_type_8 = jax.random.randint(jax.random.fold_in(_gk, 13), (20000,), 0, 8, jnp.int32)
        edge_weight = jax.random.uniform(jax.random.fold_in(_gk, 14), (20000,), jnp.float32, 0.0, 0.999998)
        return (x, src, dst, edge_type_8, edge_weight)
    x, src, dst, edge_type_8, edge_weight = _rec_inputs()

    def _L0_gnn_setup():
        import jax, jax.numpy as jnp
        import numpy as np
        N_NODES = 1250
        N_EDGES = 20000
        NEG_SLOPE = 0.2

        def _gat_layer(x, src, dst, W, a_src, a_dst, bias, concat):
            N = x.shape[0]
            H, C = a_src.shape
            h = (x @ W).reshape(N, H, C)
            al_s = jnp.einsum('nhc,hc->nh', h, a_src)
            al_d = jnp.einsum('nhc,hc->nh', h, a_dst)
            e = jax.nn.leaky_relu(al_s[src] + al_d[dst], NEG_SLOPE)
            m = jax.ops.segment_max(e, dst, num_segments=N)
            ex = jnp.exp(e - m[dst])
            denom = jax.ops.segment_sum(ex, dst, num_segments=N)
            alpha = ex / (denom[dst] + 1e-16)
            msg = h[src] * alpha[:, :, None]
            out = jax.ops.segment_sum(msg, dst, num_segments=N)
            out = out.reshape(N, H * C) if concat else out.mean(axis=1)
            return out + bias
        key = jax.random.key(seed)
        ks = jax.random.split(key, 10)
        in_dim, hid, out_dim, heads = (768, 512, 768, 4)
        x = jax.random.normal(ks[0], (N_NODES, in_dim), dtype=jnp.float32)
        edge_index = jax.random.randint(ks[1], (2, N_EDGES), 0, N_NODES, dtype=jnp.int64)
        g = lambda k, shape, fan: jax.random.normal(k, shape, jnp.float32) / np.sqrt(fan)
        return {'x': x, 'edge_index': edge_index, 'W1': g(ks[2], (in_dim, heads * hid), in_dim), 'att_src1': g(ks[3], (heads, hid), hid), 'att_dst1': g(ks[4], (heads, hid), hid), 'b1': jnp.zeros((heads * hid,), jnp.float32), 'W2': g(ks[5], (heads * hid, out_dim), heads * hid), 'att_src2': g(ks[6], (1, out_dim), out_dim), 'att_dst2': g(ks[7], (1, out_dim), out_dim), 'b2': jnp.zeros((out_dim,), jnp.float32)}
    _L0_gnn_all = _L0_gnn_setup()
    _L0_gnn_in = {k: v for k, v in _L0_gnn_all.items() if k in ('W1', 'att_src1', 'att_dst1', 'b1', 'W2', 'att_src2', 'att_dst2', 'b2')}
    del _L0_gnn_all

    def _L1_gnn_setup():
        import jax, jax.numpy as jnp
        import numpy as np
        N, IN, OUT, R, E = (2500, 768, 768, 8, 40000)

        def _rgcn_conv(x, src, dst, etype, W, root, b):
            num_nodes = x.shape[0]
            num_rel = W.shape[0]
            x_src = x[src]
            seg = dst * num_rel + etype
            sums = jax.ops.segment_sum(x_src, seg, num_segments=num_nodes * num_rel)
            cnt = jax.ops.segment_sum(jnp.ones((src.shape[0],), dtype=x.dtype), seg, num_segments=num_nodes * num_rel)
            mean = sums / jnp.maximum(cnt, 1.0)[:, None]
            mean = mean.reshape(num_nodes, num_rel, -1)
            out = jnp.einsum('nri,rio->no', mean, W)
            return out + x @ root + b
        key = jax.random.key(seed)
        ks = jax.random.split(key, 9)
        x = jax.random.normal(ks[0], (N, IN), dtype=jnp.float32)
        edge_index = jax.random.randint(ks[1], (2, E), 0, N, dtype=jnp.int64)
        edge_type = jax.random.randint(ks[2], (E,), 0, R, dtype=jnp.int64)
        s1 = 1.0 / np.sqrt(IN)
        s2 = 1.0 / np.sqrt(OUT)
        W1 = jax.random.normal(ks[3], (R, IN, OUT), dtype=jnp.float32) * s1
        root1 = jax.random.normal(ks[4], (IN, OUT), dtype=jnp.float32) * s1
        b1 = jnp.zeros((OUT,), dtype=jnp.float32)
        W2 = jax.random.normal(ks[5], (R, OUT, OUT), dtype=jnp.float32) * s2
        root2 = jax.random.normal(ks[6], (OUT, OUT), dtype=jnp.float32) * s2
        b2 = jnp.zeros((OUT,), dtype=jnp.float32)
        return {'x': x, 'edge_index': edge_index, 'edge_type': edge_type, 'W1': W1, 'root1': root1, 'b1': b1, 'W2': W2, 'root2': root2, 'b2': b2}
    _L1_gnn_all = _L1_gnn_setup()
    _L1_gnn_in = {k: v for k, v in _L1_gnn_all.items() if k in ('W1', 'root1', 'b1', 'W2', 'root2', 'b2')}
    del _L1_gnn_all

    def _L2_gnn_setup():
        import jax, jax.numpy as jnp
        import numpy as np
        N = 6250
        E = 62500
        D = 768
        H = 256
        R = 32

        def _gcn(x, W, b, row, col, ew):
            x = x @ W
            n = x.shape[0]
            deg = jax.ops.segment_sum(ew, col, num_segments=n) + 1.0
            dinv = jax.lax.rsqrt(deg)
            norm = dinv[row] * ew * dinv[col]
            agg = jax.ops.segment_sum(norm[:, None] * x[row], col, num_segments=n)
            return agg + (dinv * dinv)[:, None] * x + b
        key = jax.random.key(seed)
        ks = jax.random.split(key, 8)
        d = D // R
        w = lambda k, sh: jax.random.normal(k, sh, jnp.float32) * 0.05
        return {'x': jax.random.normal(ks[0], (N, D), jnp.float32), 'edge_index': jax.random.randint(ks[1], (2, E), 0, N), 'edge_weight': jax.random.uniform(ks[2], (E,), jnp.float32), 'Wd': w(ks[3], (D, d)), 'bd': jnp.zeros((d,), jnp.float32), 'Wu': w(ks[4], (d, D)), 'bu': jnp.zeros((D,), jnp.float32), 'W1': w(ks[5], (D, H)), 'b1': jnp.zeros((H,), jnp.float32), 'W2': w(ks[6], (H, D)), 'b2': jnp.zeros((D,), jnp.float32)}
    _L2_gnn_all = _L2_gnn_setup()
    _L2_gnn_in = {k: v for k, v in _L2_gnn_all.items() if k in ('Wd', 'bd', 'Wu', 'bu', 'W1', 'b1', 'W2', 'b2')}
    del _L2_gnn_all

    def _L3_gnn_setup():
        import jax, jax.numpy as jnp
        import numpy as np
        N = 2500
        DEG = 16
        E = N * DEG
        H = 12
        DIN = 64
        DOUT = 64
        NEG_SLOPE = 0.2
        key = jax.random.key(seed)
        k_h, k_src, k_w, k_al, k_ar, k_wr = jax.random.split(key, 6)
        std = 1.414 * np.sqrt(2.0 / (DIN + DOUT))
        h = jax.random.normal(k_h, (N, H * DIN), dtype=jnp.float32)
        src = jax.random.randint(k_src, (E,), 0, N, dtype=jnp.int64)
        dst = jnp.repeat(jnp.arange(N, dtype=jnp.int64), DEG)
        W = jax.random.normal(k_w, (DOUT, DIN), dtype=jnp.float32) * std
        attn_l = jax.random.normal(k_al, (1, H, DOUT), dtype=jnp.float32) * std
        attn_r = jax.random.normal(k_ar, (1, H, DOUT), dtype=jnp.float32) * std
        W_res = jax.random.normal(k_wr, (DOUT, DIN), dtype=jnp.float32) * std
        return {'h': h, 'src': src, 'dst': dst, 'W': W, 'attn_l': attn_l, 'attn_r': attn_r, 'W_res': W_res}
    _L3_gnn_all = _L3_gnn_setup()
    _L3_gnn_in = {k: v for k, v in _L3_gnn_all.items() if k in ('W', 'attn_l', 'attn_r', 'W_res')}
    del _L3_gnn_all
    return {'x': x, 'src': src, 'dst': dst, 'edge_type_8': edge_type_8, 'edge_weight': edge_weight, 'L0_gnn_W1': _L0_gnn_in['W1'], 'L0_gnn_att_src1': _L0_gnn_in['att_src1'], 'L0_gnn_att_dst1': _L0_gnn_in['att_dst1'], 'L0_gnn_b1': _L0_gnn_in['b1'], 'L0_gnn_W2': _L0_gnn_in['W2'], 'L0_gnn_att_src2': _L0_gnn_in['att_src2'], 'L0_gnn_att_dst2': _L0_gnn_in['att_dst2'], 'L0_gnn_b2': _L0_gnn_in['b2'], 'L1_gnn_W1': _L1_gnn_in['W1'], 'L1_gnn_root1': _L1_gnn_in['root1'], 'L1_gnn_b1': _L1_gnn_in['b1'], 'L1_gnn_W2': _L1_gnn_in['W2'], 'L1_gnn_root2': _L1_gnn_in['root2'], 'L1_gnn_b2': _L1_gnn_in['b2'], 'L2_gnn_Wd': _L2_gnn_in['Wd'], 'L2_gnn_bd': _L2_gnn_in['bd'], 'L2_gnn_Wu': _L2_gnn_in['Wu'], 'L2_gnn_bu': _L2_gnn_in['bu'], 'L2_gnn_W1': _L2_gnn_in['W1'], 'L2_gnn_b1': _L2_gnn_in['b1'], 'L2_gnn_W2': _L2_gnn_in['W2'], 'L2_gnn_b2': _L2_gnn_in['b2'], 'L3_gnn_W': _L3_gnn_in['W'], 'L3_gnn_attn_l': _L3_gnn_in['attn_l'], 'L3_gnn_attn_r': _L3_gnn_in['attn_r'], 'L3_gnn_W_res': _L3_gnn_in['W_res']}

def reference(x, src, dst, edge_type_8, edge_weight, L0_gnn_W1, L0_gnn_att_src1, L0_gnn_att_dst1, L0_gnn_b1, L0_gnn_W2, L0_gnn_att_src2, L0_gnn_att_dst2, L0_gnn_b2, L1_gnn_W1, L1_gnn_root1, L1_gnn_b1, L1_gnn_W2, L1_gnn_root2, L1_gnn_b2, L2_gnn_Wd, L2_gnn_bd, L2_gnn_Wu, L2_gnn_bu, L2_gnn_W1, L2_gnn_b1, L2_gnn_W2, L2_gnn_b2, L3_gnn_W, L3_gnn_attn_l, L3_gnn_attn_r, L3_gnn_W_res):
    import jax
    import jax.numpy as jnp

    def _L0_gnn_ref(x, edge_index, W1, att_src1, att_dst1, b1, W2, att_src2, att_dst2, b2):
        import jax, jax.numpy as jnp
        import numpy as np
        N_NODES = 1250
        N_EDGES = 20000
        NEG_SLOPE = 0.2

        def _gat_layer(x, src, dst, W, a_src, a_dst, bias, concat):
            N = x.shape[0]
            H, C = a_src.shape
            h = (x @ W).reshape(N, H, C)
            al_s = jnp.einsum('nhc,hc->nh', h, a_src)
            al_d = jnp.einsum('nhc,hc->nh', h, a_dst)
            e = jax.nn.leaky_relu(al_s[src] + al_d[dst], NEG_SLOPE)
            m = jax.ops.segment_max(e, dst, num_segments=N)
            ex = jnp.exp(e - m[dst])
            denom = jax.ops.segment_sum(ex, dst, num_segments=N)
            alpha = ex / (denom[dst] + 1e-16)
            msg = h[src] * alpha[:, :, None]
            out = jax.ops.segment_sum(msg, dst, num_segments=N)
            out = out.reshape(N, H * C) if concat else out.mean(axis=1)
            return out + bias
        N = x.shape[0]
        loops = jnp.arange(N, dtype=edge_index.dtype)
        src = jnp.concatenate([edge_index[0], loops])
        dst = jnp.concatenate([edge_index[1], loops])
        h = jax.nn.elu(_gat_layer(x, src, dst, W1, att_src1, att_dst1, b1, concat=True))
        out = _gat_layer(h, src, dst, W2, att_src2, att_dst2, b2, concat=False)
        return out

    def _L1_gnn_ref(x, edge_index, edge_type, W1, root1, b1, W2, root2, b2):
        import jax, jax.numpy as jnp
        import numpy as np
        N, IN, OUT, R, E = (2500, 768, 768, 8, 40000)

        def _rgcn_conv(x, src, dst, etype, W, root, b):
            num_nodes = x.shape[0]
            num_rel = W.shape[0]
            x_src = x[src]
            seg = dst * num_rel + etype
            sums = jax.ops.segment_sum(x_src, seg, num_segments=num_nodes * num_rel)
            cnt = jax.ops.segment_sum(jnp.ones((src.shape[0],), dtype=x.dtype), seg, num_segments=num_nodes * num_rel)
            mean = sums / jnp.maximum(cnt, 1.0)[:, None]
            mean = mean.reshape(num_nodes, num_rel, -1)
            out = jnp.einsum('nri,rio->no', mean, W)
            return out + x @ root + b
        src, dst = (edge_index[0], edge_index[1])
        h = _rgcn_conv(x, src, dst, edge_type, W1, root1, b1)
        h = jax.nn.relu(h)
        out = _rgcn_conv(h, src, dst, edge_type, W2, root2, b2)
        return out

    def _L2_gnn_ref(x, edge_index, edge_weight, Wd, bd, Wu, bu, W1, b1, W2, b2):
        import jax, jax.numpy as jnp
        import numpy as np
        N = 6250
        E = 62500
        D = 768
        H = 256
        R = 32

        def _gcn(x, W, b, row, col, ew):
            x = x @ W
            n = x.shape[0]
            deg = jax.ops.segment_sum(ew, col, num_segments=n) + 1.0
            dinv = jax.lax.rsqrt(deg)
            norm = dinv[row] * ew * dinv[col]
            agg = jax.ops.segment_sum(norm[:, None] * x[row], col, num_segments=n)
            return agg + (dinv * dinv)[:, None] * x + b
        h = jax.nn.relu(x @ Wd + bd) @ Wu + bu + x
        row, col = (edge_index[0], edge_index[1])
        h = jax.nn.relu(_gcn(h, W1, b1, row, col, edge_weight))
        h = _gcn(h, W2, b2, row, col, edge_weight)
        return h

    def _L3_gnn_ref(h, src, dst, W, attn_l, attn_r, W_res):
        import jax, jax.numpy as jnp
        import numpy as np
        N = 2500
        DEG = 16
        E = N * DEG
        H = 12
        DIN = 64
        DOUT = 64
        NEG_SLOPE = 0.2
        n = h.shape[0]
        hv = h.reshape(n, H, DIN)
        ft = jnp.einsum('nhd,od->nho', hv, W)
        a1 = jnp.sum(ft * attn_l, axis=-1)
        a2 = jnp.sum(ft * attn_r, axis=-1)
        e = jax.nn.leaky_relu(a1[src] + a2[dst], negative_slope=NEG_SLOPE)
        m = jax.ops.segment_max(e, dst, num_segments=n)
        m = jnp.where(jnp.isfinite(m), m, 0.0)
        w = jnp.exp(e - m[dst])
        denom = jax.ops.segment_sum(w, dst, num_segments=n)
        alpha = w / jnp.maximum(denom[dst], 1e-16)
        msg = alpha[:, :, None] * ft[src]
        agg = jax.ops.segment_sum(msg, dst, num_segments=n)
        res = jnp.einsum('nhd,od->nho', hv, W_res)
        out = jax.nn.relu((agg + res).reshape(n, H * DOUT))
        return out
    edge_index = jnp.stack([src, dst])
    x = _layernorm(x + _L0_gnn_ref(x, edge_index, L0_gnn_W1, L0_gnn_att_src1, L0_gnn_att_dst1, L0_gnn_b1, L0_gnn_W2, L0_gnn_att_src2, L0_gnn_att_dst2, L0_gnn_b2), axis=-1)
    x = _layernorm(x + _L1_gnn_ref(x, edge_index, edge_type_8, L1_gnn_W1, L1_gnn_root1, L1_gnn_b1, L1_gnn_W2, L1_gnn_root2, L1_gnn_b2), axis=-1)
    x = _layernorm(x + _L2_gnn_ref(x, edge_index, edge_weight, L2_gnn_Wd, L2_gnn_bd, L2_gnn_Wu, L2_gnn_bu, L2_gnn_W1, L2_gnn_b1, L2_gnn_W2, L2_gnn_b2), axis=-1)
    x = _layernorm(x + _L3_gnn_ref(x, src, dst, L3_gnn_W, L3_gnn_attn_l, L3_gnn_attn_r, L3_gnn_W_res), axis=-1)
    return x

_drawn_inputs = setup_inputs


def setup_inputs(seed=0):
    import zlib

    import numpy as np

    out = dict(_drawn_inputs(seed))
    spreads = {'L0_gnn_b1': (0.0, 0.1),
     'L0_gnn_b2': (0.0, 0.1),
     'L1_gnn_b1': (0.0, 0.1),
     'L1_gnn_b2': (0.0, 0.1),
     'L2_gnn_bd': (0.0, 0.638),
     'L2_gnn_bu': (0.0, 0.1),
     'L2_gnn_b1': (0.0, 0.1),
     'L2_gnn_b2': (0.0, 0.1)}
    factors = {'L0_gnn_att_dst1': 2.994, 'L0_gnn_att_dst2': 7.962}
    for name, (base, spread) in spreads.items():
        noise = np.random.default_rng([zlib.crc32(name.encode()), seed]).standard_normal(out[name].shape)
        drawn = base * np.exp(spread * noise) if base else spread * noise
        out[name] = jnp.asarray(drawn.astype(out[name].dtype))
    for name, factor in factors.items():
        out[name] = (out[name] * factor).astype(out[name].dtype)
    return out
```

```python
from contextlib import ExitStack

import concourse.bass as bass
from concourse import mybir

F32 = mybir.dt.float32
BF16 = mybir.dt.bfloat16
I32 = mybir.dt.int32
ALU = mybir.AluOpType
ACT = mybir.ActivationFunctionType
AX_X = mybir.AxisListType.X

P = 125
NEVER = 30000.0



class Chain:

    def __init__(self, eng, done):
        self.eng, self.done, self.base, self.k = eng, done, 0, 0

    def mark(self, ins):
        ins.then_inc(self.done, 1)
        self.k += 1

    def wait(self):
        self.eng.wait_ge(self.done, self.base + self.k)

    def __call__(self, ins):
        self.mark(ins)
        self.wait()

    def loop(self, i, per):
        self.before = self.base + self.k
        self.base, self.k = self.before + i * per, 0

    def end(self, trips, per):
        assert self.k == per, f"{self.k} signals an iteration, not {per}"
        self.base, self.k = self.before + trips * per, 0


def build(nc, a, out):
    N, D = a["x"].shape
    E, = a["src"].shape
    NT = N // P
    KD = D // 128
    HD = D // 2
    GT = 5
    NG = -(-E // (128 * GT))
    ET = NG * GT
    R = a["L1_gnn_W1"].shape[0]
    FULL = E // 128
    TAIL = E - FULL * 128
    ROWS1 = ET - 128
    CW = [417, 417, 416]
    CO = [0, 417, 834]
    H0, C0 = a["L0_gnn_att_src1"].shape
    KC0 = C0 // 128
    _, H3, C3 = a["L3_gnn_attn_l"].shape
    BOT = a["L2_gnn_Wd"].shape[1]
    G2 = a["L2_gnn_W1"].shape[1]
    KG2 = G2 // 128
    PRE = 4
    SLOPE = 0.2
    ABSENT = -1e30
    FLOOR = -1e29
    TINY = 1e-16
    EPS = 1e-5
    PARTS = [(0, 4), (4, 4), (8, NT - 8)]

    with ExitStack() as ctx:
        def sb(name, shape, dt=F32):
            return ctx.enter_context(nc.sbuf_tensor(name, shape, dt))

        def sem(name):
            return ctx.enter_context(nc.semaphore(name))

        def dram(name, shape, dt=F32):
            return nc.dram_tensor(name, shape, dt).ap()

        bank = [ctx.enter_context(nc.psum_tensor(f"bank{i}", [128, 512], F32)) for i in range(8)]

        ident = sb("ident", [128, 128])
        ones = sb("ones", [128, 128])
        zeros = sb("zeros", [128, 128])
        iota_row = sb("iota_row", [128, N])
        tile_start = sb("tile_start", [128, 1])
        start_i = sb("start_i", [128, 1], I32)[:]
        table = sb("table", [1, 2 * NT + 1], I32)
        edge = sb("edge", [128, 6, ET])
        DST, SRC, TYP, EW, REL_W, TMP = range(6)
        idx_y = sb("idx_y", [128, ET], I32)
        idx_src = sb("idx_src", [128, ET], I32)
        idx_cnt = sb("idx_cnt", [128, ET], I32)
        idx_slot = sb("idx_slot", [128, GT], I32)
        w_slot = sb("w_slot", [128, GT])
        degree = sb("degree", [P, NT, 16])
        inv_count = sb("inv_count", [P, NT, R])
        dinv = sb("dinv", [P, NT])
        stats = sb("stats", [P, NT, 2, 6])
        moments = sb("moments", [P, NT, 2])
        rstd = sb("rstd", [P, NT])

        node = N // P * D
        fixed = 2 * node + KD * N
        REST = 26300
        arena = sb("arena", [128, fixed + REST])

        def cut(at, *shape, dt=F32, parts=128):
            n = 1
            for k in shape:
                n *= k
            if dt == BF16:
                n //= 2
            v = arena[0:parts, at:at + n]
            if dt != F32:
                v = v.bitcast(dt)
            names = "abcd"[:len(shape)]
            if len(shape) > 1:
                v = v.rearrange(f"p ({' '.join(names)}) -> p {' '.join(names)}", **dict(zip(names, shape)))
            return v

        node_a = cut(0, NT, D, parts=P)
        node_b = cut(node, NT, D, parts=P)
        xT = cut(2 * node, KD, N)
        rest = fixed

        lncount = cut(rest, NT, N, parts=P)
        at = rest + NT * N
        raw = cut(at, 4, 2, 128, dt=I32)
        rows = cut(at + 1024, 4, 2, 128)
        dst_low = cut(at + 2048, 2, 128)
        diags = cut(at + 2304, 4, 128)
        iota_i = cut(at + 2816, N, dt=I32)
        at += 2816 + N
        span = cut(at, 4)
        group_lo = cut(at + 4, NG, parts=NT)
        group_hi = cut(at + 4 + NG, NG, parts=NT)
        touch = cut(at + 4 + 2 * NG, 4, NG, parts=NT)
        reach = cut(at + 4 + 6 * NG, 8, parts=NT)
        tri = cut(at + 12 + 6 * NG, NT + 1, parts=NT)
        ew_parts = cut(at + 24 + 6 * NG, 3, ET, dt=BF16)
        at += 24 + 6 * NG + 2 * ET
        hot_dst = cut(at, GT, P + 1, dt=BF16)[:, :, 0:P]
        hot_src = cut(at + GT * (P + 1) // 2 + 1, GT, N, dt=BF16)
        feat = cut(at + GT * (P + 1) // 2 + 1 + GT * N // 2, GT, 16, dt=BF16)

        at = rest + NT * N
        score = cut(at, 2, N, parts=P)
        turned_score = cut(at + 2 * N, 2, NT, P, parts=P)
        w_in = cut(at + 4 * N, KD, C0)
        w_out = cut(at + 4 * N + KD * C0, KC0, D)
        hT = cut(at + 4 * N + 2 * KD * C0, 2, KC0, P)
        at += 4 * N + 2 * KD * C0 + 2 * KC0 * P
        s_row = cut(at, N, parts=P)
        s_diag = cut(at + N, 2, P + 3, parts=P)[:, :, 0:P]
        assert at + N + 256 <= rest + REST, at + N + 256 - rest
        h_head = cut(node, NT, C0, parts=P)
        hidden = cut(node + NT * C0, 2, C0, parts=P)
        att_rows = cut(node + NT * C0 + 2 * C0, 2, C0, parts=P)
        b1_row = cut(node + NT * C0 + 4 * C0, C0, parts=P)
        wide_rows = cut(rest + NT * N + 4 * N, 2, D, parts=P)
        b2_row = cut(rest + NT * N + 4 * N + 2 * D, D, parts=P)
        x_slot = cut(rest + NT * N + 4 * N + 3 * D, 2, D, parts=P)
        res3 = cut(rest + NT * N, NT, D, parts=P)
        score3 = cut(2 * node, 2, N, parts=P)
        turned3 = cut(2 * node + 2 * N, 2, NT, P, parts=P)
        s_row3 = cut(2 * node + 4 * N, N, parts=P)
        s_diag3 = cut(2 * node + 5 * N, 2, P + 3, parts=P)[:, :, 0:P]
        al3 = cut(rest + NT * N + node, 2, NT, H3, parts=P)
        att3 = cut(rest + NT * N + node + 2 * NT * H3, 2, D, parts=P)
        w3 = cut(rest + NT * N + node + 2 * NT * H3 + 2 * D, 2, 128)
        w3T = cut(rest + NT * N + node + 2 * NT * H3 + 2 * D + 256, 2, 128)
        scratch3 = cut(rest + NT * N + node + 2 * NT * H3 + 2 * D + 512, D, parts=P)
        ln_tmp3 = cut(rest + NT * N + node + 2 * NT * H3 + 3 * D + 512, 2, N, parts=P)
        s_row_low = iota_row[0:P, :]
        mx = sb("mx", [P, 4])
        neg_mx = sb("neg_mx", [P, 4])
        den = sb("den", [P, 4])
        rden = sb("rden", [P, 4])
        al_s = sb("al_s", [P, NT])
        al_d = sb("al_d", [P, NT])

        w_rel = cut(rest, 2, KD, D)
        at = rest + 2 * KD * D
        gathered = cut(at, GT, D)
        pick = cut(at + GT * D, GT, P + 3)[:, :, 0:P]
        y_stage = cut(at + GT * (D + 128), 4, D, parts=P)
        bias_row = cut(at + GT * (D + 128) + 4 * D, D, parts=P)
        assert at + GT * (D + 128) + 5 * D <= rest + REST
        wd = cut(rest, KD, BOT)
        wu = cut(rest + 256, D, parts=BOT)
        bd_col = cut(rest + 256 + D, 1, parts=BOT)
        bu_row = cut(rest + 260 + D, D, parts=P)
        tT = cut(rest + 260 + 2 * D, N, parts=BOT)
        gw1 = cut(rest + 260 + 2 * D + N, KD, G2)
        gb1_row = cut(rest + 260 + 2 * D + N + KD * G2, G2, parts=P)
        gcn_at = rest + 260 + 2 * D + N + KD * G2 + G2
        assert gcn_at <= rest + 2 * KD * D
        gw2 = cut(rest, KG2, D)
        zT = cut(rest + KG2 * D, KG2, N)
        gb2_row = cut(rest + KG2 * D + KG2 * N, D, parts=P)
        at += GT * (D + 128) + 5 * D
        xs = cut(at, NT, G2, parts=P)
        assert at + NT * G2 <= rest + REST, at + NT * G2 - rest
        agg2 = cut(2 * node, NT, G2, parts=P)

        count_d = dram("count_d", [N, N])
        inv_d = dram("inv_d", [N * R, 1])
        y_d = dram("y_d", [R * N, D])
        xs_d = dram("xs_d", [N, G2])

        consts = sem("consts")
        phase_end, gate = sem("phase_end"), sem("gate")
        loaded = sem("loaded")
        dve_step = sem("dve_step")
        rows_ready, diag_ready, spans_spread = sem("rows_ready"), sem("diag_ready"), sem("spans_spread")
        reach_ready, table_made, table_ready = sem("reach_ready"), sem("table_made"), sem("table_ready")
        edges_turned, edges_taken = sem("edges_turned"), sem("edges_taken")
        hot_ready, hot_used = sem("hot_ready"), sem("hot_used")
        tile_counted, tile_taken = sem("tile_counted"), sem("tile_taken")
        count_stored, inv_ready, inv_stored = sem("count_stored"), sem("inv_ready"), sem("inv_stored")
        pool_step, w_landed = sem("pool_step"), sem("w_landed")
        piece_made, piece_taken = sem("piece_made"), sem("piece_taken")
        score_masked, weight_made = sem("score_masked"), sem("weight_made")
        score_turned, turned_taken = sem("score_turned"), sem("turned_taken")
        agg_made, agg_taken = sem("agg_made"), sem("agg_taken")
        elu_in, elu_exp, hidden_ready = sem("elu_in"), sem("elu_exp"), sem("hidden_ready")
        hidden_turned, hT_ready, part_made, part_taken = sem("hidden_turned"), sem("hT_ready"), sem("part_made"), sem("part_taken")
        h_made, h_ready = sem("h_made"), sem("h_ready")
        diag_made, s_spread, s_row_ready = sem("diag_made"), sem("s_spread"), sem("s_row_ready")
        w3_cleared, w3_turned, w3T_ready = sem("w3_cleared"), sem("w3_turned"), sem("w3T_ready")
        iota_ready, bias_loaded = sem("iota_ready"), sem("bias_loaded")
        acc_cleared, ln_in, ln_out = sem("acc_cleared"), sem("ln_in"), sem("ln_out")
        f_made, f_taken, r_taken = sem("f_made"), sem("f_taken"), sem("r_taken")
        t_made, t_taken = sem("t_made"), sem("t_taken")
        w_in_loaded, w_out_loaded = sem("w_in_loaded"), sem("w_out_loaded")
        att_loaded, b1_loaded = sem("att_loaded"), sem("b1_loaded")
        x_loaded = [sem(f"x_loaded{i}") for i in range(2)]
        x_used = sem("x_used")
        bulk_loaded = sem("bulk_loaded")
        slab_loaded = [sem(f"slab_loaded{i}") for i in range(2)]
        slab_used = sem("slab_used")
        y_made, y_staged = sem("y_made"), sem("y_staged")
        y_stored = [sem(f"y_stored{i}") for i in range(4)]
        root_made, root_taken = sem("root_made"), sem("root_taken")
        pick_ready = [sem(f"pick_ready{i}") for i in range(GT)]
        row_landed = [sem(f"row_landed{i}") for i in range(GT)]
        slot_used = [sem(f"slot_used{i}") for i in range(GT)]
        sum_made, sum_taken = sem("sum_made"), sem("sum_taken")
        mm_made, mm_taken = sem("mm_made"), sem("mm_taken")
        sqrt_in, sqrt_done = sem("sqrt_in"), sem("sqrt_done")
        xs_ready, xs_stored = sem("xs_ready"), sem("xs_stored")
        stored = [sem(f"stored{i}") for i in range(2)]
        ln_done = sem("ln_done")

        def spread(v, n):
            return v.partition_broadcast(n)

        def settle(eng):
            eng.sem_inc(gate, 1)

        phases = {}

        def next_phase(eng):
            n = phases[eng] = phases.get(eng, 0) + 1
            eng.drain().then_inc(phase_end, 1)
            eng.wait_ge(phase_end, 5 * n)

        def unit(u):
            return u + 1 + PRE

        counts = {}

        def tick(name, by=1):
            counts[name] = counts.get(name, 0) + by
            return counts[name]

        PIECES = [(k, c) for k in range(KD) for c in range(3)]

        def pe_turn(pe, name, src, kd):
            for k in range(kd):
                for c, (t0, nt) in enumerate(PARTS):
                    q = tick(name) - 1
                    if q >= 6:
                        pe.wait_ge(piece_taken, q - 5)
                    for t in range(nt):
                        ins = pe.transpose(bank[q % 6][:, t * P:(t + 1) * P], src[:, t0 + t, k * 128:(k + 1) * 128], ident[0:P, 0:P])
                    ins.then_inc(piece_made, 1)

        def act_turn(act, name, dst, kd):
            for k in range(kd):
                for c, (t0, nt) in enumerate(PARTS):
                    q = tick(name) - 1
                    act.wait_ge(piece_made, q + 1)
                    act.copy(dst[:, k, t0 * P:(t0 + nt) * P], bank[q % 6][:, 0:nt * P]).then_inc(piece_taken, 1)

        def dve_norm(dve, chain, t, to):
            for d in range(NT):
                for h in range(2):
                    chain.mark(dve.bn_stats(stats[:, d, h], t[:, d, h * HD:(h + 1) * HD]))
            chain.wait()
            for d in range(NT):
                chain.mark(dve.bn_aggr(moments[:, d], stats[:, d].rearrange("p a b -> p (a b)")))
            chain.wait()
            dve.tensor_scalar(rstd[:], moments[:, :, 1], EPS, None, op0=ALU.add).then_inc(sqrt_in, 1)
            dve.wait_ge(sqrt_done, tick("sqrt_dve"))
            chain(dve.reciprocal(rstd[:], rstd[:]))
            for d in range(NT):
                dve.tensor_scalar(to[:, d], t[:, d], moments[:, d, 0:1], rstd[:, d:d + 1], op0=ALU.subtract, op1=ALU.mult).then_inc(ln_done, 1)

        def act_sqrt(act, name, v):
            act.wait_ge(sqrt_in, tick(name))
            act.activation(v, v, ACT.Sqrt).then_inc(sqrt_done, 1)

        def act_units(act, uh, sc, tsc, elu):
            for s in range(0, NT + 2):
                if s < NT:
                    act_unit_exp(act, uh * NT + s, s, sc)
                    act_unit_take(act, uh * NT + s, s, tsc)
                if elu and 0 <= s - 2:
                    u, d = uh * NT + (s - 2), s - 2
                    act.wait_ge(elu_in, u + 1)
                    b = bank[3 + d % 2][0:P, 0:C0]
                    act.activation(b, b, ACT.Exp).then_inc(elu_exp, 1)
                    act.wait_ge(hidden_turned, unit(u))
                    act.wait_ge(part_made, unit(u - 2))
                    act.copy(hT[:, d % 2].rearrange("p k n -> p (k n)"), bank[5][:, 0:KC0 * P]).then_inc(hT_ready, 1)

        def pe_units(pe, uh, sc, tsc, banks, feats, elu):
            for s in range(0, NT + 2):
                if s < NT:
                    pe_unit_turn(pe, uh * NT + s, s, sc)
                if 0 <= s - 1 < NT:
                    pe_unit_sum(pe, uh * NT + (s - 1), s - 1, tsc, banks(s - 1), feats)
                if elu and 0 <= s - 2:
                    u, d = uh * NT + (s - 2), s - 2
                    pe.wait_ge(hidden_ready, unit(u))
                    pe.wait_ge(hT_ready, unit(u - 1))
                    for k in range(KC0):
                        ins = pe.transpose(bank[5][:, k * P:(k + 1) * P], hidden[:, d % 2, k * 128:(k + 1) * 128], ident[0:P, 0:P])
                    ins.then_inc(hidden_turned, 1)
                    pe.wait_ge(hT_ready, unit(u))
                    pe.wait_ge(part_taken, unit(u - 1))
                    for g in range(2):
                        for k in range(KC0):
                            ins = pe.matmul(bank[6 + g][0:P, 0:HD], hT[:, d % 2, k], w_out[:, k, g * HD:(g + 1) * HD],
                                            start=(k == 0), stop=(k == KC0 - 1))
                    ins.then_inc(part_made, 1)

        def dve_units(dve, chain, uh, sc, srow, leave, late, part):
            dve.wait_ge(s_row_ready, uh + 1)
            for s in range(-1, NT + 3):
                if s + 1 < NT:
                    dve_unit_mask(dve, chain, uh * NT + (s + 1), s + 1, sc, srow)
                if 0 <= s - 2 < NT:
                    leave(uh * NT + (s - 2), s - 2)
                if late and 0 <= s - 2 < NT:
                    late(uh * NT + (s - 2), s - 2)
                if part and 0 <= s - 3:
                    part(uh * NT + (s - 3), s - 3)

        def act_ln(act, which, tmp):
            for d in range(NT):
                act.wait_ge(ln_in, which * NT + d + 1)
                act.activation(tmp[:, d % 2], tmp[:, d % 2], ACT.Ln).then_inc(ln_out, 1)

        def dve_ln(dve, chain, which, tmp):
            for d in range(NT + 1):
                if d < NT:
                    chain(dve.tensor_scalar(tmp[:, d % 2], lncount[:, d], 1.0, None, op0=ALU.max))
                    dve.tensor_scalar(lncount[:, d], lncount[:, d], 0.5, ABSENT, op0=ALU.is_lt, op1=ALU.mult).then_inc(ln_in, 1)
                if d:
                    dve.wait_ge(ln_out, which * NT + d)
                    chain(dve.tensor_tensor(lncount[:, d - 1], lncount[:, d - 1], tmp[:, (d - 1) % 2], op=ALU.add))

        def act_unit_exp(act, u, d, sc):
            act.wait_ge(score_masked, unit(u))
            act.activation(sc[:, d % 2], sc[:, d % 2], ACT.Exp, bias=neg_mx[:, d % 4:d % 4 + 1],
                           accum_out=den[:, d % 4:d % 4 + 1]).then_inc(weight_made, 1)

        def dve_unit_mask(dve, chain, u, d, sc, srow):
            dve.wait_ge(score_turned, unit(u - 2))
            chain(dve.scalar_tensor_tensor(sc[:, d % 2], srow, al_d[:, d:d + 1], s_row_low, op0=ALU.add, op1=ALU.max))
            settle(dve)
            chain(dve.tensor_tensor_reduce(out=sc[:, d % 2], in0=sc[:, d % 2], in1=lncount[:, d], scale=1.0, scalar=FLOOR,
                                           op0=ALU.add, op1=ALU.max, accum_out=mx[:, d % 4:d % 4 + 1]))
            dve.tensor_scalar(neg_mx[:, d % 4:d % 4 + 1], mx[:, d % 4:d % 4 + 1], -1.0, None, op0=ALU.mult).then_inc(score_masked, 1)

        def pe_unit_turn(pe, u, d, sc):
            pe.wait_ge(weight_made, unit(u))
            pe.wait_ge(turned_taken, unit(u - 1))
            for c, (t0, nt) in enumerate(PARTS):
                for t in range(nt):
                    ins = pe.transpose(bank[c][0:P, t * P:(t + 1) * P], sc[:, d % 2, (t0 + t) * P:(t0 + t + 1) * P], ident[0:P, 0:P])
            ins.then_inc(score_turned, 1)

        def act_unit_take(act, u, d, tsc):
            act.wait_ge(score_turned, unit(u))
            act.wait_ge(agg_made, unit(u - 2))
            for c, (t0, nt) in enumerate(PARTS):
                ins = act.copy(tsc[:, d % 2, t0:t0 + nt], bank[c][0:P, 0:nt * P].rearrange("p (t n) -> p t n", n=P))
            ins.then_inc(turned_taken, 1)

        def pe_unit_sum(pe, u, d, tsc, banks, feats):
            pe.wait_ge(turned_taken, unit(u))
            pe.wait_ge(agg_taken, unit(u - 2))
            for t in range(NT):
                for b, f in zip(banks, feats(t)):
                    w = f.shape[-1]
                    ins = pe.matmul(bank[b][0:P, 0:w], tsc[:, d % 2, t], f, start=(t == 0), stop=(t == NT - 1))
            ins.then_inc(agg_made, 1)

        def dve_unit_rden(dve, chain, u, d, add):
            dve.wait_ge(agg_made, unit(u))
            q = slice(d % 4, d % 4 + 1)
            chain(dve.tensor_scalar(rden[:, q], den[:, q], TINY, None, op0=ALU.add if add else ALU.max))
            chain(dve.reciprocal(rden[:, q], rden[:, q]))
            return rden[:, q]

        def dve_s_row(dve, uh, sd):
            for t in range(NT):
                dve.wait_ge(s_spread, unit(uh * NT + (t - 2)))
                dve.tensor_scalar(sd[:, t % 2], ident[0:P, 0:P], al_s[:, t:t + 1], None, op0=ALU.mult).then_inc(diag_made, 1)

        def pe_s_row(pe, uh, sd):
            pe.wait_ge(turned_taken, unit(uh * NT - 1))
            for t in range(NT):
                pe.wait_ge(diag_made, uh * NT + (t + 1))
                pe.matmul(bank[t // 4][0:P, (t % 4) * P:(t % 4 + 1) * P], ones[0:P, 0:P], sd[:, t % 2], start=True, stop=True).then_inc(s_spread, 1)

        def act_s_row(act, uh, srow):
            act.wait_ge(s_spread, unit(uh * NT + (NT - 1)))
            for c, (t0, nt) in enumerate(PARTS):
                v = slice(t0 * P, (t0 + nt) * P)
                act.copy(srow[:, v], bank[c][0:P, 0:nt * P])
                ins = act.activation(s_row_low[:, v], bank[c][0:P, 0:nt * P], ACT.Copy, scale=SLOPE)
            ins.then_inc(s_row_ready, 1)
        def run_of(eng, d):
            first = eng.value_load(table[0:1, d:d + 1], min_val=0, max_val=NT * NG)
            end = eng.value_load(table[0:1, d + 1:d + 2], min_val=0, max_val=NT * NG)
            return first, end

        def done_before(eng, p):
            return eng.value_load(table[0:1, NT:NT + 1], min_val=1, max_val=NT * NG) * p if p else 0

        def sum_pool(pool, p, src_d, width):
            past = done_before(pool, p)
            for d in range(NT):
                first, end = run_of(pool, d)
                with pool.Fori(first, end) as j:
                    for k in range(GT):
                        pool.wait_ge(pick_ready[k], j + past + 1)
                        settle(pool)
                        pool.indirect_dma_start(gathered[:, k, 0:width], None, src_d,
                                                bass.IndirectOffsetOnAxis(ap=idx_slot[:, k:k + 1], axis=0)).then_inc(row_landed[k], 16)

        def sum_dve(dve, p, idx, weight, take):
            past = done_before(dve, p)
            dve.wait_ge(iota_ready, 1)
            for d in range(NT):
                first, end = run_of(dve, d)
                shift = dve.value_load(table[0:1, NT + 1 + d:NT + 2 + d], min_val=-NT * NG, max_val=NG)
                with dve.Fori(first, end) as j:
                    group = nc.s_assert_within(j + shift, 0, NG - 1)
                    for k in range(GT):
                        t = group * GT + k
                        dve.wait_ge(slot_used[k], j + past + 1)
                        dve.tensor_copy(idx_slot[:, k:k + 1], idx[:, bass.ds(t, 1)])
                        dve.tensor_scalar(pick[:, k], iota_row[:, d * P:(d + 1) * P], edge[:, DST, bass.ds(t, 1)],
                                          edge[:, weight, bass.ds(t, 1)], op0=ALU.is_equal, op1=ALU.mult).then_inc(pick_ready[k], 1)
                q = tick("sum_dve")
                dve.wait_ge(sum_made, q)
                take(d).then_inc(sum_taken, 1)

        def sum_pe(pe, p, width):
            halves = [(h * HD, HD) for h in range(2)] if width == D else [(0, width)]
            past = done_before(pe, p)
            pe.wait_ge(iota_ready, 1)
            for d in range(NT):
                first, end = run_of(pe, d)
                acc = bank[2 * (d % 2):2 * (d % 2) + 2]
                q = tick("sum_pe")
                if q > 2:
                    pe.wait_ge(sum_taken, q - 2)
                for (o, w), b in zip(halves, acc):
                    pe.matmul(b[0:P, 0:w], zeros[0:1, 0:P], iota_row[0:1, 0:w], start=True, stop=False)
                with pe.Fori(first, end) as j:
                    for k in range(GT):
                        pe.wait_ge(pick_ready[k], j + past + 1)
                        pe.wait_ge(row_landed[k], (j + past + 1) * 16)
                        for (o, w), b in zip(halves, acc):
                            ins = pe.matmul(b[0:P, 0:w], pick[:, k], gathered[:, k, o:o + w], start=False, stop=False)
                        ins.then_inc(slot_used[k], 1)
                for (o, w), b in zip(halves, acc):
                    ins = pe.matmul(b[0:P, 0:w], zeros[0:1, 0:P], iota_row[0:1, 0:w], start=False, stop=True)
                ins.then_inc(sum_made, 1)

        block = ctx.enter_context(nc.Block())

        @block.sync
        def _(sp):
            for s in y_stored:
                sp.sem_inc(s, 16)
            sp.dma_start(node_a, a["x"].rearrange("(n p) d -> p n d", p=P)).then_inc(bulk_loaded, 16)
            sp.wait_ge(rows_ready, 1)
            for i, v in enumerate([a["dst"], a["src"], a["edge_type_8"], a["edge_weight"]]):
                to = raw[:, i] if i < 3 else rows[:, i]
                sp.dma_start(to[0:128, 0, :], v[0:128 * 128].rearrange("(t e) -> t e", e=128)).then_inc(loaded, 16)
                sp.dma_start(to[0:FULL - 128, 1, :], v[128 * 128:FULL * 128].rearrange("(t e) -> t e", e=128)).then_inc(loaded, 16)
                sp.dma_start(to[FULL - 128:FULL - 127, 1, 0:TAIL], v[FULL * 128:E].rearrange("(t e) -> t e", e=TAIL)).then_inc(loaded, 16)
            sp.wait_ge(tile_taken, NT)
            sp.dma_start(count_d.rearrange("(n p) s -> p n s", p=P), lncount).then_inc(count_stored, 16)
            sp.wait_ge(inv_ready, 1)
            sp.dma_start(inv_d.rearrange("(n p r) o -> p n (r o)", p=P, r=R), inv_count[:]).then_inc(inv_stored, 16)
            sp.wait_ge(count_stored, 16)
            next_phase(sp)
            with sp.Fori(0, H0) as h:
                sp.wait_ge(h_made, unit(h * NT - 1))
                sp.dma_start(w_in, a["L0_gnn_W1"].rearrange("(k p) c -> p k c", p=128)[:, :, bass.ds(h * C0, C0)]).then_inc(w_in_loaded, 16)
                sp.wait_ge(agg_taken, unit(h * NT - 1))
                sp.dma_start(att_rows[:, 0], spread(a["L0_gnn_att_src1"][bass.ds(h, 1), :].rearrange("o c -> (o c)"), P)).then_inc(att_loaded, 16)
                sp.dma_start(att_rows[:, 1], spread(a["L0_gnn_att_dst1"][bass.ds(h, 1), :].rearrange("o c -> (o c)"), P)).then_inc(att_loaded, 16)
                sp.dma_start(b1_row, spread(a["L0_gnn_b1"][bass.ds(h * C0, C0)], P)).then_inc(b1_loaded, 16)
                sp.wait_ge(part_made, unit(h * NT - 1))
                sp.dma_start(w_out, a["L0_gnn_W2"][bass.ds(h * C0, C0), :].rearrange("(k p) c -> p k c", p=128)).then_inc(w_out_loaded, 16)
            next_phase(sp)
            sp.dma_start(wide_rows[:, 0], spread(a["L0_gnn_att_src2"][0, :], P)).then_inc(att_loaded, 16)
            sp.dma_start(wide_rows[:, 1], spread(a["L0_gnn_att_dst2"][0, :], P)).then_inc(att_loaded, 16)
            sp.dma_start(b2_row, spread(a["L0_gnn_b2"], P)).then_inc(b1_loaded, 16)
            for d in range(NT):
                if d >= 2:
                    sp.wait_ge(x_used, d - 1)
                sp.dma_start(x_slot[:, d % 2], a["x"][d * P:(d + 1) * P, :]).then_inc(x_loaded[d % 2], 16)
            next_phase(sp)
            for c in range(2):
                with sp.Fori(0, R // 2) as q:
                    for s in range(2):
                        for n in range(NT):
                            i = (s * NT + n) % 4
                            sp.wait_ge(y_staged, unit((c * R + q * 2 + s) * NT + n))
                            sp.dma_start(y_d[bass.ds((q * 2 + s) * N + n * P, P), :], y_stage[:, i]).then_inc(y_stored[i], 16)
                next_phase(sp)
            for v, t in ((wd, a["L2_gnn_Wd"].rearrange("(k p) c -> p k c", p=128)), (wu, a["L2_gnn_Wu"]),
                         (bd_col, a["L2_gnn_bd"].rearrange("(p o) -> p o", o=1)), (bu_row, spread(a["L2_gnn_bu"], P)),
                         (gw1, a["L2_gnn_W1"].rearrange("(k p) c -> p k c", p=128)), (gb1_row, spread(a["L2_gnn_b1"], P))):
                sp.dma_start(v, t).then_inc(bulk_loaded, 16)
            for c in range(2):
                sp.wait_ge(xs_ready, c + 1)
                sp.dma_start(xs_d.rearrange("(n p) c -> p n c", p=P), xs).then_inc(xs_stored, 16)
            next_phase(sp)
            sp.dma_start(gw2, a["L2_gnn_W2"].rearrange("(k p) c -> p k c", p=128)).then_inc(bulk_loaded, 16)
            sp.dma_start(gb2_row, spread(a["L2_gnn_b2"], P)).then_inc(bulk_loaded, 16)
            next_phase(sp)
            sp.dma_start(lncount, count_d.rearrange("(n p) s -> p n s", p=P)).then_inc(bulk_loaded, 16)
            sp.dma_start(att3[:, 0], spread(a["L3_gnn_attn_l"][0].rearrange("h c -> (h c)"), P)).then_inc(bulk_loaded, 16)
            sp.dma_start(att3[:, 1], spread(a["L3_gnn_attn_r"][0].rearrange("h c -> (h c)"), P)).then_inc(bulk_loaded, 16)
            sp.wait_ge(w3_cleared, 1)
            for i, w in enumerate((a["L3_gnn_W"], a["L3_gnn_W_res"])):
                for q in range(2):
                    sp.dma_start(w3[q * C3:(q + 1) * C3, i, q * C3:(q + 1) * C3], w).then_inc(bulk_loaded, 16)
            next_phase(sp)
            for d in range(NT):
                sp.wait_ge(ln_done, 3 * NT + d + 1)
                sp.dma_start(out[d * P:(d + 1) * P, :], node_b[:, d]).then_inc(stored[d % 2], 16)
            for i in range(2):
                sp.wait_ge(stored[i], 16 * NT // 2)

        @block.gpsimd
        def _(pool):
            pool.memset(ident[:], 0.0).then_inc(consts, 1)
            pool.memset(ones[:], 1.0).then_inc(consts, 1)
            pool.memset(zeros[:], 0.0).then_inc(consts, 1)
            pool.memset(tri, 0.0).then_inc(consts, 1)
            pool.wait_ge(consts, 4)
            pool.affine_select(out=ident[:], in_=ident[:], compare_op=ALU.not_equal, fill=1.0, base=0,
                               pattern=[[-1, 128]], channel_multiplier=1).then_inc(consts, 1)
            pool.affine_select(out=tri, in_=tri, compare_op=ALU.is_ge, fill=1.0, base=0,
                               pattern=[[-1, NT + 1]], channel_multiplier=1).then_inc(consts, 1)
            pool.iota(iota_row[:], pattern=[[1, N]], base=0, channel_multiplier=0, allow_small_or_imprecise_dtypes=True).then_inc(consts, 1)
            pool.iota(start_i, pattern=[[1, 1]], base=0, channel_multiplier=P).then_inc(consts, 1)
            pool.wait_ge(inv_stored, 16)
            with pool.Fori(0, NG) as g:
                pool.tensor_copy(idx_slot[:], idx_cnt[:, bass.ds(g * GT, GT)]).then_inc(pool_step, 1)
                pool.wait_ge(pool_step, g * 2 + 1)
                settle(pool)
                for k in range(GT):
                    pool.indirect_dma_start(w_slot[:, k:k + 1], None, inv_d,
                                            bass.IndirectOffsetOnAxis(ap=idx_slot[:, k:k + 1], axis=0)).then_inc(w_landed, 16)
                pool.wait_ge(w_landed, (g + 1) * 16 * GT)
                pool.tensor_copy(edge[:, REL_W, bass.ds(g * GT, GT)], w_slot[:]).then_inc(pool_step, 1)
                pool.wait_ge(pool_step, g * 2 + 2)
            next_phase(pool)
            pool.memset(node_a, 0.0).then_inc(acc_cleared, 1)
            next_phase(pool)
            next_phase(pool)
            pool.iota(iota_row[:], pattern=[[1, N]], base=0, channel_multiplier=0, allow_small_or_imprecise_dtypes=True).then_inc(iota_ready, 1)
            for c in range(2):
                W, root, b = (a[f"L1_gnn_{n}{c + 1}"] for n in ("W", "root", "b"))
                pool.dma_start(w_rel[:, 0], root.rearrange("(k p) c -> p k c", p=128)).then_inc(slab_loaded[0], 16)
                pool.dma_start(bias_row, spread(b, P)).then_inc(bias_loaded, 16)
                with pool.Fori(0, R // 2) as q:
                    for s in range(2):
                        pool.wait_ge(slab_used, q * 2 + (c * (R + 1) + s + 1))
                        pool.dma_start(w_rel[:, 1 - s], W[bass.ds(q * 2 + s, 1), :, :].rearrange("o (k p) c -> p (o k) c", p=128)).then_inc(slab_loaded[1 - s], 16)
                for i in range(4):
                    pool.wait_ge(y_stored[i], 16 * (R * NT // 4 * (c + 1) + 1))
                sum_pool(pool, c, y_d, D)
                next_phase(pool)
            for c in range(2):
                pool.wait_ge(xs_stored, 16 * (c + 1))
                sum_pool(pool, 2 + c, xs_d, G2)
            next_phase(pool)
            next_phase(pool)
            pool.memset(w3, 0.0).then_inc(w3_cleared, 1)
            next_phase(pool)

        @block.scalar
        def _(act):
            for s in (y_staged, turned_taken, weight_made, hT_ready):
                act.sem_inc(s, PRE)
            act_turn(act, "turn_act", xT, KD)
            act_ln(act, 0, score)
            act_sqrt(act, "sqrt_act", dinv[:])
            next_phase(act)
            with act.Fori(0, H0) as h:
                for n in range(NT):
                    act.wait_ge(h_made, unit(h * NT + n))
                    if n == 0:
                        act.wait_ge(agg_made, unit(h * NT - 1))
                    act.copy(h_head[:, n], bank[5 + n % 2][0:P, 0:C0]).then_inc(h_ready, 1)
                act_s_row(act, h, s_row)
                act_units(act, h, score, turned_score, True)
            next_phase(act)
            act_s_row(act, H0, s_row)
            act_units(act, H0, score, turned_score, False)
            act_sqrt(act, "sqrt_act", rstd[:])
            next_phase(act)
            for c in range(2):
                act_turn(act, "turn_act", xT, KD)
                with act.Fori(0, R // 2) as q:
                    for s in range(2):
                        for n in range(NT):
                            i = (s * NT + n) % 4
                            act.wait_ge(y_made, unit((c * R + q * 2 + s) * NT + n))
                            act.wait_ge(y_stored[i], (q * 5 + (c * 5 * R // 2 + (s * NT + n) // 4 + 1)) * 16)
                            act.copy(y_stage[:, i, 0:HD], bank[2 * i][0:P, 0:HD])
                            act.copy(y_stage[:, i, HD:D], bank[2 * i + 1][0:P, 0:HD]).then_inc(y_staged, 1)
                if c == 1:
                    act_sqrt(act, "sqrt_act", rstd[:])
                next_phase(act)
            act_turn(act, "turn_act", xT, KD)
            act.wait_ge(bulk_loaded, 16 * 7)
            for c, (t0, nt) in enumerate(PARTS):
                act.wait_ge(t_made, c + 1)
                act.activation(tT[:, t0 * P:(t0 + nt) * P], bank[6][0:BOT, 0:nt * P], ACT.Relu, bias=bd_col).then_inc(t_taken, 1)
            act_turn(act, "turn_act", xT, KD)
            next_phase(act)
            act_turn(act, "turn_act", zT, KG2)
            act_sqrt(act, "sqrt_act", rstd[:])
            next_phase(act)
            act_ln(act, 1, ln_tmp3)
            act_turn(act, "turn_act", xT, KD)
            act.wait_ge(w3_turned, 1)
            act.copy(w3T.rearrange("p a b -> p (a b)"), bank[6][:, 0:256]).then_inc(w3T_ready, 1)
            for n in range(NT):
                for g in range(3):
                    q = 3 * n + g
                    act.wait_ge(f_made, q + 1)
                    act.copy(res3[:, n, g * 256:(g + 1) * 256].rearrange("p (c f) -> p c f", c=2),
                             bank[q % 6][0:P, :].rearrange("p (c i f) -> p c i f", c=2, i=2)[:, :, 1]).then_inc(r_taken, 1)
            next_phase(act)
            with act.Fori(0, H3) as h:
                act_s_row(act, h + (H0 + 1), s_row3)
                act_units(act, h + (H0 + 1), score3, turned3, False)
            act_sqrt(act, "sqrt_act", rstd[:])

        @block.tensor
        def _(pe):
            for s in (s_spread, score_turned, agg_made, h_made, part_made, y_made, hidden_turned):
                pe.sem_inc(s, PRE)
            pe.sem_inc(slab_used, 1)
            pe.sem_inc(hot_used, 1)
            for s in slot_used:
                pe.sem_inc(s, 1)
            pe.wait_ge(consts, 8)
            pe.wait_ge(diag_ready, 1)
            for i in range(4):
                w = 128 if i % 2 == 0 else ROWS1
                o = 256 * (i // 2) + 128 * (i % 2)
                ins = pe.matmul(bank[7][0:NT, o:o + w], ones[:, 0:NT], diags[:, i, 0:w], start=True, stop=True)
            ins.then_inc(spans_spread, 1)
            pe.wait_ge(reach_ready, 1)
            pe.matmul(bank[7][0:1, 448:448 + NT + 1], reach[:, 4:5], tri, start=True, stop=True)
            pe.matmul(bank[7][0:1, 449 + NT:449 + 2 * NT], reach[:, 2:3], ident[0:NT, 0:NT], start=True, stop=True).then_inc(table_made, 1)
            for i in range(4):
                pe.matmul(bank[i][:, 0:128], rows[:, i, 0, :], ident[:], start=True, stop=True)
                ins = pe.matmul(bank[i][:, 128:ET], rows[0:ROWS1, i, 1, :], ident[0:ROWS1, 0:ROWS1], start=True, stop=True)
            ins.then_inc(edges_turned, 1)
            pe.wait_ge(edges_taken, 1)
            pe.wait_ge(bulk_loaded, 16)
            pe_turn(pe, "turn_pe", node_a, KD)
            pe.wait_ge(piece_taken, counts["turn_pe"])
            pe.wait_ge(table_ready, 1)
            for d in range(NT):
                first, end = run_of(pe, d)
                acc = bank[4 * (d % 2):4 * (d % 2) + 4]
                widths = CW + [16]
                if d >= 2:
                    pe.wait_ge(tile_taken, d - 1)
                for b, w in zip(acc, widths):
                    pe.matmul(b[0:P, 0:w], zeros[0:1, 0:P], iota_row[0:1, 0:w], start=True, stop=False)
                with pe.Fori(first, end) as j:
                    pe.wait_ge(hot_ready, j + 1)
                    for k in range(GT):
                        for c in range(3):
                            pe.matmul(acc[c][0:P, 0:CW[c]], hot_dst[:, k], hot_src[:, k, CO[c]:CO[c] + CW[c]], start=False, stop=False)
                        ins = pe.matmul(acc[3][0:P, 0:16], hot_dst[:, k], feat[:, k], start=False, stop=False)
                    ins.then_inc(hot_used, 1)
                for b, w in zip(acc, widths):
                    ins = pe.matmul(b[0:P, 0:w], zeros[0:1, 0:P], iota_row[0:1, 0:w], start=False, stop=True)
                ins.then_inc(tile_counted, 1)
            next_phase(pe)
            with pe.Fori(0, H0) as h:
                pe.wait_ge(w_in_loaded, (h + 1) * 16)
                for n in range(NT):
                    if n < 2:
                        pe.wait_ge(hT_ready, unit(h * NT - 1))
                        pe.wait_ge(part_taken, unit(h * NT - 1))
                    else:
                        pe.wait_ge(h_ready, h * NT + (n - 1))
                    for k in range(KD):
                        ins = pe.matmul(bank[5 + n % 2][0:P, 0:C0], xT[:, k, n * P:(n + 1) * P], w_in[:, k], start=(k == 0), stop=(k == KD - 1))
                    ins.then_inc(h_made, 1)
                pe_s_row(pe, h, s_diag)
                pe.wait_ge(w_out_loaded, (h + 1) * 16)
                pe_units(pe, h, score, turned_score, lambda d: [3 + d % 2], lambda t: [h_head[:, t]], True)
            next_phase(pe)
            pe_s_row(pe, H0, s_diag)
            pe_units(pe, H0, score, turned_score, lambda d: [3 + 2 * (d % 2), 4 + 2 * (d % 2)],
                     lambda t: [node_a[:, t, 0:HD], node_a[:, t, HD:D]], False)
            next_phase(pe)
            for c in range(2):
                pe_turn(pe, "turn_pe", node_a if c else node_b, KD)
                pe.wait_ge(piece_taken, counts["turn_pe"])
                pe.wait_ge(slab_loaded[0], 16 * (c * (1 + R // 2) + 1))

                def product(n, i, slab):
                    for h in range(2):
                        for k in range(KD):
                            ins = pe.matmul(bank[2 * i + h][0:P, 0:HD], xT[:, k, n * P:(n + 1) * P],
                                            w_rel[:, slab, k, h * HD:(h + 1) * HD], start=(k == 0), stop=(k == KD - 1))
                    return ins

                for n in range(NT):
                    if n >= 4:
                        pe.wait_ge(root_taken, c * NT + n - 3)
                    product(n, n % 4, 0).then_inc(root_made, 1)
                pe.drain().then_inc(slab_used, 1)
                pe.wait_ge(root_taken, (c + 1) * NT)
                with pe.Fori(0, R // 2) as q:
                    for s in range(2):
                        pe.wait_ge(slab_loaded[1 - s], (q + (c * (1 + R // 2) + 2 if s else c * (R // 2) + 1)) * 16)
                        for n in range(NT):
                            u = (c * R + q * 2 + s) * NT + n
                            pe.wait_ge(y_staged, unit(u - 4))
                            product(n, (s * NT + n) % 4, 1 - s).then_inc(y_made, 1)
                        pe.drain().then_inc(slab_used, 1)
                pe.wait_ge(y_staged, unit((c + 1) * R * NT - 1))
                sum_pe(pe, c, D)
                next_phase(pe)
            pe_turn(pe, "turn_pe", node_b, KD)
            pe.wait_ge(piece_taken, counts["turn_pe"])
            pe.wait_ge(bulk_loaded, 16 * 7)
            for c, (t0, nt) in enumerate(PARTS):
                if c:
                    pe.wait_ge(t_taken, c)
                for k in range(KD):
                    ins = pe.matmul(bank[6][0:BOT, 0:nt * P], wd[:, k], xT[:, k, t0 * P:(t0 + nt) * P], start=(k == 0), stop=(k == KD - 1))
                ins.then_inc(t_made, 1)
            pe.wait_ge(t_taken, 3)
            for n in range(NT):
                if n >= 2:
                    pe.wait_ge(mm_taken, n - 1)
                for h in range(2):
                    ins = pe.matmul(bank[2 * (n % 2) + h][0:P, 0:HD], tT[:, n * P:(n + 1) * P], wu[:, h * HD:(h + 1) * HD], start=True, stop=True)
                ins.then_inc(mm_made, 1)
            pe.wait_ge(mm_taken, NT)
            pe_turn(pe, "turn_pe", node_a, KD)
            pe.wait_ge(piece_taken, counts["turn_pe"])
            for n in range(NT):
                if n >= 2:
                    pe.wait_ge(mm_taken, NT + n - 1)
                for k in range(KD):
                    ins = pe.matmul(bank[6 + n % 2][0:P, 0:G2], xT[:, k, n * P:(n + 1) * P], gw1[:, k], start=(k == 0), stop=(k == KD - 1))
                ins.then_inc(mm_made, 1)
            sum_pe(pe, 2, G2)
            sum_pe(pe, 3, G2)
            next_phase(pe)
            pe_turn(pe, "turn_pe", agg2, KG2)
            pe.wait_ge(piece_taken, counts["turn_pe"])
            pe.wait_ge(bulk_loaded, 16 * 9)
            for n in range(NT):
                if n >= 2:
                    pe.wait_ge(mm_taken, 2 * NT + n - 1)
                for h in range(2):
                    for k in range(KG2):
                        ins = pe.matmul(bank[2 * (n % 2) + h][0:P, 0:HD], zT[:, k, n * P:(n + 1) * P], gw2[:, k, h * HD:(h + 1) * HD],
                                        start=(k == 0), stop=(k == KG2 - 1))
                ins.then_inc(mm_made, 1)
            next_phase(pe)
            pe_turn(pe, "turn_pe", node_b, KD)
            pe.wait_ge(bulk_loaded, 16 * 16)
            for i in range(2):
                ins = pe.transpose(bank[6][:, i * 128:(i + 1) * 128], w3[:, i], ident[:])
            ins.then_inc(w3_turned, 1)
            pe.wait_ge(w3T_ready, 1)
            pe.wait_ge(piece_taken, counts["turn_pe"])
            for n in range(NT):
                for g in range(3):
                    q = 3 * n + g
                    if q >= 6:
                        pe.wait_ge(f_taken, q - 5)
                        pe.wait_ge(r_taken, q - 5)
                    for c in range(2):
                        ins = pe.matmul(bank[q % 6][0:P, c * 256:(c + 1) * 256], xT[:, 2 * g + c, n * P:(n + 1) * P],
                                        w3T.rearrange("p a b -> p (a b)"), start=True, stop=True)
                    ins.then_inc(f_made, 1)
            next_phase(pe)
            with pe.Fori(0, H3) as h:
                pe_s_row(pe, h + (H0 + 1), s_diag3)
                pe_units(pe, h + (H0 + 1), score3, turned3, lambda d: [3 + d % 2], lambda t: [node_a[:, t, bass.ds(h * C3, C3)]], False)

        @block.vector
        def _(dve):
            chain = Chain(dve, dve_step)
            for s in (score_masked, agg_taken, hidden_ready, part_taken):
                dve.sem_inc(s, PRE)
            chain.mark(dve.memset(raw[:, 0], int(NEVER)))
            chain.mark(dve.memset(raw[:, 1:3], 0))
            chain.mark(dve.memset(rows[:, 3], 0.0))
            chain.wait()
            dve.memset(feat, 0.0).then_inc(rows_ready, 1)
            dve.wait_ge(consts, 8)
            chain(dve.tensor_copy(tile_start[:], start_i))
            dve.wait_ge(loaded, 16 * 12)
            chain(dve.tensor_copy(rows[:, 0:3], raw[:, 0:3]))
            chain.mark(dve.tensor_reduce(span[:, 0:2], rows[:, 0], axis=AX_X, op=ALU.min))
            chain(dve.scalar_tensor_tensor(dst_low, rows[:, 0], NEVER, rows[:, 0], op0=ALU.is_lt, op1=ALU.mult))
            chain(dve.tensor_reduce(span[:, 2:4], dst_low, axis=AX_X, op=ALU.max))
            for i in range(4):
                ins = dve.tensor_scalar(diags[:, i], ident[:], span[:, i:i + 1], None, op0=ALU.mult)
            ins.then_inc(diag_ready, 1)
            dve.wait_ge(spans_spread, 1)
            chain.mark(dve.tensor_reduce(group_lo, bank[7][0:NT, 0:ET].rearrange("p (g t) -> p g t", t=GT), axis=AX_X, op=ALU.min))
            chain(dve.tensor_reduce(group_hi, bank[7][0:NT, 256:256 + ET].rearrange("p (g t) -> p g t", t=GT), axis=AX_X, op=ALU.max))
            chain.mark(dve.tensor_scalar(touch[:, 0], group_lo, tile_start[0:NT], float(P), op0=ALU.subtract, op1=ALU.is_lt))
            chain(dve.tensor_scalar(touch[:, 1], group_hi, tile_start[0:NT], None, op0=ALU.is_ge))
            chain(dve.tensor_tensor(touch[:, 2], touch[:, 0], touch[:, 1], op=ALU.mult))
            chain.mark(dve.scalar_tensor_tensor(touch[:, 0], iota_row[0:NT, 0:NG], 1.0, touch[:, 2], op0=ALU.add, op1=ALU.mult))
            chain(dve.tensor_scalar(touch[:, 3], iota_row[0:NT, 0:NG], -1.0, float(NG), op0=ALU.mult, op1=ALU.add))
            chain.mark(dve.tensor_tensor(touch[:, 1], touch[:, 3], touch[:, 2], op=ALU.mult))
            chain(dve.tensor_reduce(reach[:, 0:1], touch[:, 0], axis=AX_X, op=ALU.max))
            chain(dve.tensor_reduce(reach[:, 1:2], touch[:, 1], axis=AX_X, op=ALU.max))
            chain(dve.tensor_scalar(reach[:, 5:6], reach[:, 1:2], 1.0, -1.0, op0=ALU.max, op1=ALU.mult))
            chain(dve.tensor_scalar(reach[:, 2:3], reach[:, 5:6], float(NG), None, op0=ALU.add))
            chain(dve.tensor_tensor(reach[:, 3:4], reach[:, 0:1], reach[:, 2:3], op=ALU.subtract))
            dve.tensor_scalar(reach[:, 4:5], reach[:, 3:4], 1.0, None, op0=ALU.max).then_inc(reach_ready, 1)
            dve.wait_ge(table_made, 1)
            chain(dve.tensor_copy(diags[0:1, 0, 0:2 * NT + 1], bank[7][0:1, 448:448 + 2 * NT + 1]))
            chain.mark(dve.tensor_copy(table[:, 0:NT + 1], diags[0:1, 0, 0:NT + 1]))
            chain(dve.tensor_tensor(diags[0:1, 1, 0:NT], diags[0:1, 0, NT + 1:2 * NT + 1], diags[0:1, 0, 0:NT], op=ALU.subtract))
            dve.tensor_copy(table[:, NT + 1:], diags[0:1, 1, 0:NT]).then_inc(table_ready, 1)
            dve.wait_ge(edges_turned, 1)
            for i in range(4):
                chain.mark(dve.tensor_copy(edge[:, i], bank[i][:, 0:ET]))
            chain.wait()
            chain(dve.scalar_tensor_tensor(edge[:, TMP], edge[:, TYP], float(N), edge[:, SRC], op0=ALU.mult, op1=ALU.add))
            chain.mark(dve.tensor_copy(idx_y[:], edge[:, TMP]))
            chain(dve.tensor_copy(idx_src[:], edge[:, SRC]))
            chain(dve.tensor_scalar(edge[:, TMP], edge[:, DST], float(N - 1), float(R), op0=ALU.min, op1=ALU.mult))
            chain(dve.tensor_tensor(edge[:, TMP], edge[:, TMP], edge[:, TYP], op=ALU.add))
            chain.mark(dve.tensor_copy(idx_cnt[:], edge[:, TMP]))
            chain(dve.tensor_copy(ew_parts[:, 0], edge[:, EW]))
            chain(dve.tensor_tensor(edge[:, TMP], edge[:, EW], ew_parts[:, 0], op=ALU.subtract))
            chain(dve.tensor_copy(ew_parts[:, 1], edge[:, TMP]))
            chain(dve.tensor_tensor(edge[:, TMP], edge[:, TMP], ew_parts[:, 1], op=ALU.subtract))
            chain(dve.tensor_copy(ew_parts[:, 2], edge[:, TMP]))
            dve.drain().then_inc(edges_taken, 1)
            dve.wait_ge(table_ready, 1)
            for d in range(NT):
                first, end = run_of(dve, d)
                shift = dve.value_load(table[0:1, NT + 1 + d:NT + 2 + d], min_val=-NT * NG, max_val=NG)
                with dve.Fori(first, end) as j:
                    group = nc.s_assert_within(j + shift, 0, NG - 1)
                    dve.wait_ge(hot_used, j + 1)
                    for k in range(GT):
                        t = group * GT + k
                        dve.tensor_scalar(hot_dst[:, k], iota_row[:, d * P:(d + 1) * P], edge[:, DST, bass.ds(t, 1)], None, op0=ALU.is_equal)
                        dve.tensor_scalar(hot_src[:, k], iota_row[:], edge[:, SRC, bass.ds(t, 1)], None, op0=ALU.is_equal)
                        dve.tensor_scalar(feat[:, k, 0:R], iota_row[:, 0:R], edge[:, TYP, bass.ds(t, 1)], None, op0=ALU.is_equal)
                        ins = dve.tensor_copy(feat[:, k, R:R + 3], ew_parts[:, :, bass.ds(t, 1)].rearrange("p c o -> p (c o)"))
                    ins.then_inc(hot_ready, 1)
                dve.wait_ge(tile_counted, d + 1)
                for c in range(3):
                    dve.tensor_copy(lncount[:, d, CO[c]:CO[c] + CW[c]], bank[4 * (d % 2) + c][0:P, 0:CW[c]])
                chain.mark(dve.tensor_copy(degree[:, d], bank[4 * (d % 2) + 3][0:P, 0:16]))
                chain.wait()
                dve.drain().then_inc(tile_taken, 1)
            chain(dve.tensor_scalar(inv_count[:], degree[:, :, 0:R], 1.0, None, op0=ALU.max))
            dve.reciprocal(inv_count[:], inv_count[:]).then_inc(inv_ready, 1)
            chain(dve.tensor_tensor(dinv[:], degree[:, :, R], degree[:, :, R + 1], op=ALU.add))
            chain(dve.scalar_tensor_tensor(dinv[:], dinv[:], 1.0, degree[:, :, R + 2], op0=ALU.add, op1=ALU.add))
            dve.wait_ge(count_stored, 16)
            for d in range(NT):
                chain.mark(dve.tensor_tensor(lncount[:, d, d * P:(d + 1) * P], lncount[:, d, d * P:(d + 1) * P], ident[0:P, 0:P], op=ALU.add))
            chain.wait()
            dve_ln(dve, chain, 0, score)
            dve.drain().then_inc(sqrt_in, 1)
            dve.wait_ge(sqrt_done, tick("sqrt_dve"))
            chain(dve.reciprocal(dinv[:], dinv[:]))
            next_phase(dve)
            dve.wait_ge(acc_cleared, 1)
            A_STEPS = 8 * NT + 1
            with dve.Fori(0, H0) as h:
                chain.loop(h, A_STEPS)
                dve.wait_ge(att_loaded, (h + 1) * 32)
                dve.wait_ge(b1_loaded, (h + 1) * 16)
                for n in range(NT):
                    dve.wait_ge(h_ready, h * NT + (n + 1))
                    for i, al in enumerate((al_s, al_d)):
                        chain(dve.tensor_tensor_reduce(out=hidden[:, i], in0=h_head[:, n], in1=att_rows[:, i], scale=1.0, scalar=0.0,
                                                       op0=ALU.mult, op1=ALU.add, accum_out=al[:, n:n + 1]))
                chain(dve.tensor_scalar(al_d[:], al_d[:], 1.0 - SLOPE, None, op0=ALU.mult))
                dve_s_row(dve, h, s_diag)

                def leave_a(u, d):
                    r = dve_unit_rden(dve, chain, u, d, True)
                    dve.wait_ge(hidden_turned, unit(u - 2))
                    b = bank[3 + d % 2][0:P, 0:C0]
                    chain(dve.scalar_tensor_tensor(hidden[:, d % 2], b, r, b1_row, op0=ALU.mult, op1=ALU.add))
                    dve.tensor_scalar(b, hidden[:, d % 2], 0.0, None, op0=ALU.min).then_inc(elu_in, 1)

                def elu_a(u, d):
                    dve.wait_ge(elu_exp, u + 1)
                    chain(dve.scalar_tensor_tensor(hidden[:, d % 2], bank[3 + d % 2][0:P, 0:C0], -1.0, hidden[:, d % 2], op0=ALU.add, op1=ALU.max))
                    settle(dve)
                    dve.drain().then_inc(hidden_ready, 1)
                    dve.drain().then_inc(agg_taken, 1)

                def part_a(u, d):
                    dve.wait_ge(part_made, unit(u))
                    for g in range(2):
                        v = node_a[:, d, g * HD:(g + 1) * HD]
                        ins = dve.tensor_tensor(v, v, bank[6 + g][0:P, 0:HD], op=ALU.add)
                    ins.then_inc(part_taken, 1)

                dve_units(dve, chain, h, score, s_row, leave_a, elu_a, part_a)
                chain.end(H0, A_STEPS)
            next_phase(dve)
            dve.wait_ge(att_loaded, (H0 + 1) * 32)
            dve.wait_ge(b1_loaded, (H0 + 1) * 16)
            for n in range(NT):
                for i, al in enumerate((al_s, al_d)):
                    chain(dve.tensor_tensor_reduce(out=node_b[:, i], in0=node_a[:, n], in1=wide_rows[:, i], scale=1.0, scalar=0.0,
                                                   op0=ALU.mult, op1=ALU.add, accum_out=al[:, n:n + 1]))
            chain(dve.tensor_scalar(al_d[:], al_d[:], 1.0 - SLOPE, None, op0=ALU.mult))
            dve_s_row(dve, H0, s_diag)

            def leave_b(u, d):
                r = dve_unit_rden(dve, chain, u, d, True)
                for g in range(2):
                    v = slice(g * HD, (g + 1) * HD)
                    chain.mark(dve.scalar_tensor_tensor(node_b[:, d, v], bank[3 + 2 * (d % 2) + g][0:P, 0:HD], r, b2_row[:, v], op0=ALU.mult, op1=ALU.add))
                chain.wait()
                settle(dve)
                dve.drain().then_inc(agg_taken, 1)
                dve.wait_ge(x_loaded[d % 2], 16 * (d // 2 + 1))
                dve.tensor_tensor(node_b[:, d], node_b[:, d], x_slot[:, d % 2], op=ALU.add).then_inc(x_used, 1)

            dve_units(dve, chain, H0, score, s_row, leave_b, None, None)
            dve.wait_ge(x_used, NT)
            dve_norm(dve, chain, node_b, node_b)
            next_phase(dve)
            for c in range(2):
                dve.wait_ge(bias_loaded, 16 * (1 + c))
                for n in range(NT):
                    dve.wait_ge(root_made, c * NT + n + 1)
                    for g in range(2):
                        v = slice(g * HD, (g + 1) * HD)
                        ins = dve.tensor_tensor(node_a[:, n, v], bank[2 * (n % 4) + g][0:P, 0:HD], bias_row[:, v], op=ALU.add)
                    ins.then_inc(root_taken, 1)

                def take(d):
                    for g in range(2):
                        v = node_a[:, d, g * HD:(g + 1) * HD]
                        chain.mark(dve.tensor_tensor(v, v, bank[2 * (d % 2) + g][0:P, 0:HD], op=ALU.add))
                    chain.wait()
                    if c == 0:
                        return dve.tensor_scalar(node_a[:, d], node_a[:, d], 0.0, None, op0=ALU.max)
                    return dve.tensor_tensor(node_b[:, d], node_b[:, d], node_a[:, d], op=ALU.add)

                sum_dve(dve, c, idx_y, REL_W, take)
                if c == 1:
                    dve.wait_ge(sum_taken, 2 * NT)
                    dve_norm(dve, chain, node_b, node_b)
                next_phase(dve)
            dve.wait_ge(bulk_loaded, 16 * 7)
            for n in range(NT):
                dve.wait_ge(mm_made, n + 1)
                for g in range(2):
                    v = slice(g * HD, (g + 1) * HD)
                    chain.mark(dve.tensor_tensor(node_a[:, n, v], bank[2 * (n % 2) + g][0:P, 0:HD], bu_row[:, v], op=ALU.add))
                chain.wait()
                dve.tensor_tensor(node_a[:, n], node_a[:, n], node_b[:, n], op=ALU.add).then_inc(mm_taken, 1)
            for n in range(NT):
                dve.wait_ge(mm_made, NT + n + 1)
                dve.tensor_scalar(xs[:, n], bank[6 + n % 2][0:P, 0:G2], dinv[:, n:n + 1], None, op0=ALU.mult).then_inc(mm_taken, 1)
            dve.drain().then_inc(xs_ready, 1)

            def take_1(d):
                chain(dve.tensor_tensor(agg2[:, d], bank[2 * (d % 2)][0:P, 0:G2], xs[:, d], op=ALU.add))
                chain(dve.scalar_tensor_tensor(agg2[:, d], agg2[:, d], dinv[:, d:d + 1], gb1_row, op0=ALU.mult, op1=ALU.add))
                return dve.tensor_scalar(xs[:, d], agg2[:, d], 0.0, dinv[:, d:d + 1], op0=ALU.max, op1=ALU.mult)

            def take_2(d):
                chain(dve.tensor_tensor(agg2[:, d], bank[2 * (d % 2)][0:P, 0:G2], xs[:, d], op=ALU.add))
                return dve.tensor_scalar(agg2[:, d], agg2[:, d], dinv[:, d:d + 1], None, op0=ALU.mult)

            sum_dve(dve, 2, idx_src, EW, take_1)
            dve.drain().then_inc(xs_ready, 1)
            sum_dve(dve, 3, idx_src, EW, take_2)
            next_phase(dve)
            dve.wait_ge(bulk_loaded, 16 * 9)
            for n in range(NT):
                dve.wait_ge(mm_made, 2 * NT + n + 1)
                for g in range(2):
                    v = slice(g * HD, (g + 1) * HD)
                    chain.mark(dve.tensor_tensor(node_a[:, n, v], bank[2 * (n % 2) + g][0:P, 0:HD], gb2_row[:, v], op=ALU.add))
                chain.wait()
                dve.tensor_tensor(node_b[:, n], node_b[:, n], node_a[:, n], op=ALU.add).then_inc(mm_taken, 1)
            dve.wait_ge(mm_taken, 3 * NT)
            dve_norm(dve, chain, node_b, node_b)
            next_phase(dve)
            dve.wait_ge(bulk_loaded, 16 * 16)
            dve_ln(dve, chain, 1, ln_tmp3)
            for n in range(NT):
                for g in range(3):
                    q = 3 * n + g
                    dve.wait_ge(f_made, q + 1)
                    dve.wait_ge(r_taken, q + 1)
                    dve.tensor_copy(node_a[:, n, g * 256:(g + 1) * 256].rearrange("p (c f) -> p c f", c=2),
                                    bank[q % 6][0:P, :].rearrange("p (c i f) -> p c i f", c=2, i=2)[:, :, 0]).then_inc(f_taken, 1)
                dve.wait_ge(f_taken, 3 * (n + 1))
                for i in range(2):
                    chain(dve.tensor_tensor(scratch3, node_a[:, n], att3[:, i], op=ALU.mult))
                    chain(dve.tensor_reduce(al3[:, i, n], scratch3.rearrange("p (h c) -> p h c", c=C3), axis=AX_X, op=ALU.add))
            next_phase(dve)
            with dve.Fori(0, H3) as h:
                C_STEPS = 4 * NT + 2
                chain.loop(h, C_STEPS)
                u0 = h + (H0 + 1)
                chain.mark(dve.tensor_copy(al_s[:], al3[:, 0, :, bass.ds(h, 1)].rearrange("p n o -> p (n o)")))
                chain(dve.tensor_scalar(al_d[:], al3[:, 1, :, bass.ds(h, 1)].rearrange("p n o -> p (n o)"), 1.0 - SLOPE, None, op0=ALU.mult))
                dve_s_row(dve, u0, s_diag3)

                def leave_c(u, d):
                    r = dve_unit_rden(dve, chain, u, d, False)
                    v = res3[:, d, bass.ds(h * C3, C3)]
                    dve.scalar_tensor_tensor(v, bank[3 + d % 2][0:P, 0:C3], r, v, op0=ALU.mult, op1=ALU.add).then_inc(agg_taken, 1)

                dve_units(dve, chain, u0, score3, s_row3, leave_c, None, None)
                chain.end(H3, C_STEPS)
            dve.wait_ge(agg_taken, unit((H0 + 1 + H3) * NT - 1))
            for d in range(NT):
                chain.mark(dve.scalar_tensor_tensor(node_b[:, d], res3[:, d], 0.0, node_b[:, d], op0=ALU.max, op1=ALU.add))
            chain.wait()
            dve_norm(dve, chain, node_b, node_b)


_INS = ['x', 'src', 'dst', 'edge_type_8', 'edge_weight', 'L0_gnn_W1', 'L0_gnn_att_src1', 'L0_gnn_att_dst1', 'L0_gnn_b1',
        'L0_gnn_W2', 'L0_gnn_att_src2', 'L0_gnn_att_dst2', 'L0_gnn_b2', 'L1_gnn_W1', 'L1_gnn_root1', 'L1_gnn_b1',
        'L1_gnn_W2', 'L1_gnn_root2', 'L1_gnn_b2', 'L2_gnn_Wd', 'L2_gnn_bd', 'L2_gnn_Wu', 'L2_gnn_bu', 'L2_gnn_W1',
        'L2_gnn_b1', 'L2_gnn_W2', 'L2_gnn_b2', 'L3_gnn_W', 'L3_gnn_attn_l', 'L3_gnn_attn_r', 'L3_gnn_W_res']


def kernel(**inputs):
    import numpy as _np
    import concourse.bacc as _bacc
    from concourse import mybir as _mybir
    from concourse.bass_utils import run_bass_kernel_spmd as _run

    nc = _bacc.Bacc("TRN2", target_bir_lowering=False, num_devices=1)
    arrays, args = {}, {}
    for name in _INS:
        v = _np.ascontiguousarray(inputs[name])
        arrays[f"in_{name}_dram"] = v
        args[name] = nc.dram_tensor(f"in_{name}_dram", v.shape, _mybir.dt.from_np(v.dtype), kind="ExternalInput").ap()
    out = nc.dram_tensor("out_0_dram", inputs["x"].shape, _mybir.dt.float32, kind="ExternalOutput").ap()
    build(nc, args, out)
    r = _run(nc, [arrays], core_ids=[0])
    return r.results[0]["out_0_dram"]
```

```python
from contextlib import ExitStack

import concourse.bass as bass
from concourse import mybir

F32 = mybir.dt.float32
F32R = mybir.dt.float32r
BF16 = mybir.dt.bfloat16
F16 = mybir.dt.float16
I32 = mybir.dt.int32
ALU = mybir.AluOpType
ACT = mybir.ActivationFunctionType
AX_X = mybir.AxisListType.X

P = 125
NEVER = 30000.0



class Chain:

    def __init__(self, eng, done):
        self.eng, self.done, self.base, self.k = eng, done, 0, 0

    def mark(self, ins):
        ins.then_inc(self.done, 1)
        self.k += 1

    def wait(self):
        self.eng.wait_ge(self.done, self.base + self.k)

    def __call__(self, ins):
        self.mark(ins)
        self.wait()

    def loop(self, i, per):
        self.before = self.base + self.k
        self.base, self.k = self.before + i * per, 0

    def end(self, trips, per):
        assert self.k == per, f"{self.k} signals an iteration, not {per}"
        self.base, self.k = self.before + trips * per, 0


def build(nc, a, out):
    N, D = a["x"].shape
    E, = a["src"].shape
    NT = N // P
    KD = D // 128
    HD = D // 2
    GT = 5
    ET = -(-E // 128)
    EP = ET + GT
    NG = -(-ET // GT)
    R = a["L1_gnn_W1"].shape[0]
    FULL = E // 128
    TAIL = E - FULL * 128
    ROWS1 = ET - 128
    assert TAIL and GT * NG <= EP
    CW = [417, 417, 416]
    CO = [0, 417, 834]
    H0, C0 = a["L0_gnn_att_src1"].shape
    KC0 = C0 // 128
    _, H3, C3 = a["L3_gnn_attn_l"].shape
    BOT = a["L2_gnn_Wd"].shape[1]
    G2 = a["L2_gnn_W1"].shape[1]
    KG2 = G2 // 128
    PRE = 4
    SLOPE = 0.2
    ABSENT = -1e30
    FLOOR = -1e29
    TINY = 1e-16
    EPS = 1e-5
    PARTS = [(0, 4), (4, 4), (8, NT - 8)]

    with ExitStack() as ctx:
        def sb(name, shape, dt=F32):
            return ctx.enter_context(nc.sbuf_tensor(name, shape, dt))

        def sem(name):
            return ctx.enter_context(nc.semaphore(name))

        def dram(name, shape, dt=F32):
            return nc.dram_tensor(name, shape, dt).ap()

        bank = [ctx.enter_context(nc.psum_tensor(f"bank{i}", [128, 512], F32)) for i in range(8)]

        ident = sb("ident", [128, 128])
        ones = sb("ones", [128, 128])
        zeros = sb("zeros", [128, 128])
        iota_row = sb("iota_row", [128, N])
        tile_start = sb("tile_start", [128, 1])
        start_i = sb("start_i", [128, 1], I32)[:]
        table = sb("table", [1, 2 * NT + 1], I32)
        edge = sb("edge", [128, 6, EP])
        DST, SRC, TYP, EW, REL_W, TMP = range(6)
        idx_y = sb("idx_y", [128, EP], I32)
        idx_src = sb("idx_src", [128, EP], I32)
        idx_cnt = sb("idx_cnt", [128, EP], I32)
        idx_slot = sb("idx_slot", [128, GT], I32)
        w_slot = sb("w_slot", [128, GT])
        degree = sb("degree", [P, NT, 16])
        inv_count = sb("inv_count", [P, NT, R])
        dinv = sb("dinv", [P, NT])
        stats = sb("stats", [P, NT, 2, 6])
        moments = sb("moments", [P, NT, 2])
        rstd = sb("rstd", [P, NT])

        node = N // P * D
        fixed = 2 * node + KD * N
        REST = 26300
        XW = -(-KD * N // 16) * 16

        def placed(name, at, *shape, dt=F32R):
            n = 1
            for k in shape:
                n *= k
            assert at % 16 == 0
            with nc.sbuf_tensor(name + "_before", [128, at], F32), nc.sbuf_tensor(name, [128, n], dt) as t:
                v = t[:, :]
            names = "abcd"[:len(shape)]
            return v.rearrange(f"p ({' '.join(names)}) -> p {' '.join(names)}", **dict(zip(names, shape)))

        xT_hi = placed("xT_hi", 2 * node, KD, N)
        xT_lo = placed("xT_lo", 2 * node + XW, KD, N)
        w_at = 2 * (node + XW)
        HW = KD * HD
        w_raw = placed("w_raw", w_at, 2, KD, HD, dt=F32)
        w_hi = placed("w_hi", w_at + 2 * HW, 2, KD, HD)
        w_lo = placed("w_lo", w_at + 4 * HW, 2, KD, HD)
        arena = sb("arena", [128, fixed + REST])

        def cut(at, *shape, dt=F32, parts=128):
            n = 1
            for k in shape:
                n *= k
            if dt in (BF16, F16):
                n //= 2
            v = arena[0:parts, at:at + n]
            if dt != F32:
                v = v.bitcast(dt)
            names = "abcd"[:len(shape)]
            if len(shape) > 1:
                v = v.rearrange(f"p ({' '.join(names)}) -> p {' '.join(names)}", **dict(zip(names, shape)))
            return v

        node_a = cut(0, NT, D, parts=P)
        node_b = cut(node, NT, D, parts=P)
        xT = cut(2 * node, KD, N)
        rest = fixed

        lncount = cut(rest, NT, N, parts=P)
        at = rest + NT * N
        raw = cut(at, 4, 2, 128, dt=I32)
        rows = cut(at + 1024, 4, 2, 128)
        dst_low = cut(at + 2048, 2, 128)
        diags = cut(at + 2304, 4, 128)
        iota_half = cut(at + 2816, N, dt=F16)
        at += 2816 + N
        span = cut(at, 4)
        touch = cut(at + 4, 4, ET, parts=NT)
        reach = cut(at + 4 + 4 * ET, 8, parts=NT)
        tri = cut(at + 12 + 4 * ET, NT + 1, parts=NT)
        ew_parts = cut(at + 24 + 4 * ET, 3, EP + EP % 2, dt=BF16)
        at += 24 + 4 * ET + 2 * EP
        hot_dst = cut(at, GT, P + 1, dt=BF16)[:, :, 0:P]
        hot_src = cut(at + GT * (P + 1) // 2 + 1, GT, N, dt=BF16)
        feat = cut(at + GT * (P + 1) // 2 + 1 + GT * N // 2, GT, 16, dt=BF16)

        at = rest + NT * N
        score = cut(at, 2, N, parts=P)
        turned_score = cut(at + 2 * N, 2, NT, P, parts=P)
        w_in = cut(at + 4 * N, KD, C0)
        w_out = cut(at + 4 * N + KD * C0, KC0, D)
        hT = cut(at + 4 * N + 2 * KD * C0, 2, KC0, P)
        at += 4 * N + 2 * KD * C0 + 2 * KC0 * P
        s_row = cut(at, N, parts=P)
        s_diag = cut(at + N, 2, P + 3, parts=P)[:, :, 0:P]
        assert at + N + 256 <= rest + REST, at + N + 256 - rest
        h_head = cut(node, NT, C0, parts=P)
        hidden = cut(node + NT * C0, 2, C0, parts=P)
        att_rows = cut(node + NT * C0 + 2 * C0, 2, C0, parts=P)
        b1_row = cut(node + NT * C0 + 4 * C0, C0, parts=P)
        wide_rows = cut(rest + NT * N + 4 * N, 2, D, parts=P)
        b2_row = cut(rest + NT * N + 4 * N + 2 * D, D, parts=P)
        x_slot = cut(rest + NT * N + 4 * N + 3 * D, 2, D, parts=P)
        res3 = cut(rest + NT * N, NT, D, parts=P)
        score3 = cut(2 * node, 2, N, parts=P)
        turned3 = cut(2 * node + 2 * N, 2, NT, P, parts=P)
        s_row3 = cut(2 * node + 4 * N, N, parts=P)
        s_diag3 = cut(2 * node + 5 * N, 2, P + 3, parts=P)[:, :, 0:P]
        al3 = cut(rest + NT * N + node, 2, NT, H3, parts=P)
        att3 = cut(rest + NT * N + node + 2 * NT * H3, 2, D, parts=P)
        w3 = cut(rest + NT * N + node + 2 * NT * H3 + 2 * D, 2, 128)
        w3T = cut(rest + NT * N + node + 2 * NT * H3 + 2 * D + 256, 2, 128)
        scratch3 = cut(rest + NT * N + node + 2 * NT * H3 + 2 * D + 512, D, parts=P)
        ln_tmp3 = cut(rest + NT * N + node + 2 * NT * H3 + 3 * D + 512, 2, N, parts=P)
        s_row_low = iota_row[0:P, :]
        mx = sb("mx", [P, 4])
        neg_mx = sb("neg_mx", [P, 4])
        den = sb("den", [P, 4])
        rden = sb("rden", [P, 4])
        al_s = sb("al_s", [P, NT])
        al_d = sb("al_d", [P, NT])

        gathered = cut(w_at, GT, D)
        pick = cut(w_at + GT * D, GT, P + 3)[:, :, 0:P]
        y_stage = cut(w_at + 6 * HW, 4, HD, parts=P)
        bias_row = cut(w_at + 6 * HW + 4 * HD, D, parts=P)
        assert w_at + 6 * HW + 4 * HD + D <= rest + REST
        wd = cut(rest, KD, BOT)
        wu = cut(rest + 256, D, parts=BOT)
        bd_col = cut(rest + 256 + D, 1, parts=BOT)
        bu_row = cut(rest + 260 + D, D, parts=P)
        tT = cut(rest + 260 + 2 * D, N, parts=BOT)
        gw1 = cut(rest + 260 + 2 * D + N, KD, G2)
        gb1_row = cut(rest + 260 + 2 * D + N + KD * G2, G2, parts=P)
        gcn_at = rest + 260 + 2 * D + N + KD * G2 + G2
        assert gcn_at <= w_at and GT * (D + 128) <= 6 * HW
        gw2 = cut(rest, KG2, D)
        zT = cut(rest + KG2 * D, KG2, N)
        gb2_row = cut(rest + KG2 * D + KG2 * N, D, parts=P)
        at = w_at + 6 * HW
        xs = cut(at, NT, G2, parts=P)
        assert at + NT * G2 <= rest + REST, at + NT * G2 - rest
        agg2 = cut(2 * node, NT, G2, parts=P)

        count_d = dram("count_d", [N, N])
        inv_d = dram("inv_d", [N * R, 1])
        y_d = dram("y_d", [R * N, D])
        xs_d = dram("xs_d", [N, G2])

        consts = sem("consts")
        phase_end, gate = sem("phase_end"), sem("gate")
        loaded = sem("loaded")
        dve_step = sem("dve_step")
        rows_ready, diag_ready, spans_spread = sem("rows_ready"), sem("diag_ready"), sem("spans_spread")
        reach_ready, table_made, table_ready = sem("reach_ready"), sem("table_made"), sem("table_ready")
        edges_turned, edges_taken = sem("edges_turned"), sem("edges_taken")
        hot_ready = [sem(f"hot_ready{i}") for i in range(GT)]
        hot_used = [sem(f"hot_used{i}") for i in range(GT)]
        tile_counted, tile_taken = sem("tile_counted"), sem("tile_taken")
        count_stored, inv_ready, inv_stored = sem("count_stored"), sem("inv_ready"), sem("inv_stored")
        pool_step, w_landed = sem("pool_step"), sem("w_landed")
        piece_made, piece_taken = sem("piece_made"), sem("piece_taken")
        score_masked, weight_made = sem("score_masked"), sem("weight_made")
        score_turned, turned_taken = sem("score_turned"), sem("turned_taken")
        agg_made, agg_taken = sem("agg_made"), sem("agg_taken")
        elu_in, elu_exp, hidden_ready = sem("elu_in"), sem("elu_exp"), sem("hidden_ready")
        hidden_turned, hT_ready, part_made, part_taken = sem("hidden_turned"), sem("hT_ready"), sem("part_made"), sem("part_taken")
        h_made, h_ready = sem("h_made"), sem("h_ready")
        diag_made, s_spread, s_row_ready = sem("diag_made"), sem("s_spread"), sem("s_row_ready")
        w3_cleared, w3_turned, w3T_ready = sem("w3_cleared"), sem("w3_turned"), sem("w3T_ready")
        iota_ready, bias_loaded = sem("iota_ready"), sem("bias_loaded")
        acc_cleared, ln_in, ln_out = sem("acc_cleared"), sem("ln_in"), sem("ln_out")
        f_made, f_taken, r_taken = sem("f_made"), sem("f_taken"), sem("r_taken")
        t_made, t_taken = sem("t_made"), sem("t_taken")
        w_in_loaded, w_out_loaded = sem("w_in_loaded"), sem("w_out_loaded")
        att_loaded, b1_loaded = sem("att_loaded"), sem("b1_loaded")
        x_loaded = [sem(f"x_loaded{i}") for i in range(2)]
        x_used = sem("x_used")
        bulk_loaded = sem("bulk_loaded")
        raw_loaded = [sem(f"raw_loaded{i}") for i in range(2)]
        w_ready, prod_made, prod_taken = sem("w_ready"), sem("prod_made"), sem("prod_taken")
        piece_high = sem("piece_high")
        y_stored = [sem(f"y_stored{i}") for i in range(4)]
        pick_ready = [sem(f"pick_ready{i}") for i in range(GT)]
        row_landed = [sem(f"row_landed{i}") for i in range(GT)]
        slot_used = [sem(f"slot_used{i}") for i in range(GT)]
        sum_made, sum_taken = sem("sum_made"), sem("sum_taken")
        mm_made, mm_taken = sem("mm_made"), sem("mm_taken")
        sqrt_in, sqrt_done = sem("sqrt_in"), sem("sqrt_done")
        xs_ready, xs_stored = sem("xs_ready"), sem("xs_stored")
        stored = [sem(f"stored{i}") for i in range(2)]
        ln_done = sem("ln_done")

        def spread(v, n):
            return v.partition_broadcast(n)

        def settle(eng):
            eng.sem_inc(gate, 1)

        phases = {}

        def next_phase(eng):
            n = phases[eng] = phases.get(eng, 0) + 1
            eng.drain().then_inc(phase_end, 1)
            eng.wait_ge(phase_end, 5 * n)

        def unit(u):
            return u + 1 + PRE

        counts = {}

        def tick(name, by=1):
            counts[name] = counts.get(name, 0) + by
            return counts[name]

        PIECES = [(k, c) for k in range(KD) for c in range(3)]

        def pe_turn(pe, name, src, kd):
            for k in range(kd):
                for c, (t0, nt) in enumerate(PARTS):
                    q = tick(name) - 1
                    if q >= 6:
                        pe.wait_ge(piece_taken, q - 5)
                    for t in range(nt):
                        ins = pe.transpose(bank[q % 6][:, t * P:(t + 1) * P], src[:, t0 + t, k * 128:(k + 1) * 128], ident[0:P, 0:P])
                    ins.then_inc(piece_made, 1)

        def act_turn(act, name, dst, kd, done=None):
            for k in range(kd):
                for c, (t0, nt) in enumerate(PARTS):
                    q = tick(name) - 1
                    act.wait_ge(piece_made, q + 1)
                    act.copy(dst[:, k, t0 * P:(t0 + nt) * P], bank[q % 6][:, 0:nt * P]).then_inc(done or piece_taken, 1)

        def dve_turn_low(dve, c):
            for q in range(3 * KD):
                k, (t0, nt) = q // 3, PARTS[q % 3]
                v = slice(t0 * P, (t0 + nt) * P)
                dve.wait_ge(piece_high, 3 * KD * c + q + 1)
                b = (3 * KD * (c + 1) + q) % 6
                dve.tensor_tensor(xT_lo[:, k, v], bank[b][:, 0:nt * P], xT_hi[:, k, v].bitcast(F32), op=ALU.subtract).then_inc(piece_taken, 1)

        def dve_norm(dve, chain, t, to):
            for d in range(NT):
                for h in range(2):
                    chain.mark(dve.bn_stats(stats[:, d, h], t[:, d, h * HD:(h + 1) * HD]))
            chain.wait()
            for d in range(NT):
                chain.mark(dve.bn_aggr(moments[:, d], stats[:, d].rearrange("p a b -> p (a b)")))
            chain.wait()
            dve.tensor_scalar(rstd[:], moments[:, :, 1], EPS, None, op0=ALU.add).then_inc(sqrt_in, 1)
            dve.wait_ge(sqrt_done, tick("sqrt_dve"))
            chain(dve.reciprocal(rstd[:], rstd[:]))
            for d in range(NT):
                dve.tensor_scalar(to[:, d], t[:, d], moments[:, d, 0:1], rstd[:, d:d + 1], op0=ALU.subtract, op1=ALU.mult).then_inc(ln_done, 1)

        def act_sqrt(act, name, v):
            act.wait_ge(sqrt_in, tick(name))
            act.activation(v, v, ACT.Sqrt).then_inc(sqrt_done, 1)

        def act_units(act, uh, sc, tsc, elu):
            for s in range(0, NT + 3):
                if s < NT:
                    act_unit_exp(act, uh * NT + s, s, sc)
                if 0 <= s - 1 < NT:
                    act_unit_take(act, uh * NT + (s - 1), s - 1, tsc)
                if elu and 0 <= s - 3:
                    u, d = uh * NT + (s - 3), s - 3
                    act.wait_ge(elu_in, u + 1)
                    b = bank[3 + d % 2][0:P, 0:C0]
                    act.activation(b, b, ACT.Exp).then_inc(elu_exp, 1)
                    act.wait_ge(hidden_turned, unit(u))
                    act.wait_ge(part_made, unit(u - 2))
                    act.copy(hT[:, d % 2].rearrange("p k n -> p (k n)"), bank[5][:, 0:KC0 * P]).then_inc(hT_ready, 1)

        def pe_units(pe, uh, sc, tsc, banks, feats, elu):
            for s in range(0, NT + 2):
                if s < NT:
                    pe_unit_turn(pe, uh * NT + s, s, sc)
                if 0 <= s - 1 < NT:
                    pe_unit_sum(pe, uh * NT + (s - 1), s - 1, tsc, banks(s - 1), feats)
                if elu and 0 <= s - 2:
                    u, d = uh * NT + (s - 2), s - 2
                    pe.wait_ge(hidden_ready, unit(u))
                    pe.wait_ge(hT_ready, unit(u - 1))
                    for k in range(KC0):
                        ins = pe.transpose(bank[5][:, k * P:(k + 1) * P], hidden[:, d % 2, k * 128:(k + 1) * 128], ident[0:P, 0:P])
                    ins.then_inc(hidden_turned, 1)
                    pe.wait_ge(hT_ready, unit(u))
                    pe.wait_ge(part_taken, unit(u - 1))
                    for g in range(2):
                        for k in range(KC0):
                            ins = pe.matmul(bank[6 + g][0:P, 0:HD], hT[:, d % 2, k], w_out[:, k, g * HD:(g + 1) * HD],
                                            start=(k == 0), stop=(k == KC0 - 1))
                    ins.then_inc(part_made, 1)

        def dve_units(dve, chain, uh, sc, srow, leave, late, part):
            dve.wait_ge(s_row_ready, uh + 1)
            for s in range(-1, NT + 3):
                if s + 1 < NT:
                    dve_unit_mask(dve, chain, uh * NT + (s + 1), s + 1, sc, srow)
                if 0 <= s - 2 < NT:
                    leave(uh * NT + (s - 2), s - 2)
                if late and 0 <= s - 2 < NT:
                    late(uh * NT + (s - 2), s - 2)
                if part and 0 <= s - 3:
                    part(uh * NT + (s - 3), s - 3)

        def act_ln(act, which, tmp):
            for d in range(NT):
                act.wait_ge(ln_in, which * NT + d + 1)
                act.activation(tmp[:, d % 2], tmp[:, d % 2], ACT.Ln).then_inc(ln_out, 1)

        def dve_ln(dve, chain, which, tmp):
            for d in range(NT + 1):
                if d < NT:
                    chain(dve.tensor_scalar(tmp[:, d % 2], lncount[:, d], 1.0, None, op0=ALU.max))
                    dve.tensor_scalar(lncount[:, d], lncount[:, d], 0.5, ABSENT, op0=ALU.is_lt, op1=ALU.mult).then_inc(ln_in, 1)
                if d:
                    dve.wait_ge(ln_out, which * NT + d)
                    chain(dve.tensor_tensor(lncount[:, d - 1], lncount[:, d - 1], tmp[:, (d - 1) % 2], op=ALU.add))

        def act_unit_exp(act, u, d, sc):
            act.wait_ge(score_masked, unit(u))
            act.activation(sc[:, d % 2], sc[:, d % 2], ACT.Exp, bias=neg_mx[:, d % 4:d % 4 + 1],
                           accum_out=den[:, d % 4:d % 4 + 1]).then_inc(weight_made, 1)

        def dve_unit_mask(dve, chain, u, d, sc, srow):
            dve.wait_ge(score_turned, unit(u - 2))
            chain(dve.scalar_tensor_tensor(sc[:, d % 2], srow, al_d[:, d:d + 1], s_row_low, op0=ALU.add, op1=ALU.max))
            settle(dve)
            chain(dve.tensor_tensor_reduce(out=sc[:, d % 2], in0=sc[:, d % 2], in1=lncount[:, d], scale=1.0, scalar=FLOOR,
                                           op0=ALU.add, op1=ALU.max, accum_out=mx[:, d % 4:d % 4 + 1]))
            dve.tensor_scalar(neg_mx[:, d % 4:d % 4 + 1], mx[:, d % 4:d % 4 + 1], -1.0, None, op0=ALU.mult).then_inc(score_masked, 1)

        def pe_unit_turn(pe, u, d, sc):
            pe.wait_ge(weight_made, unit(u))
            pe.wait_ge(turned_taken, unit(u - 1))
            for c, (t0, nt) in enumerate(PARTS):
                for t in range(nt):
                    ins = pe.transpose(bank[c][0:P, t * P:(t + 1) * P], sc[:, d % 2, (t0 + t) * P:(t0 + t + 1) * P], ident[0:P, 0:P])
            ins.then_inc(score_turned, 1)

        def act_unit_take(act, u, d, tsc):
            act.wait_ge(score_turned, unit(u))
            act.wait_ge(agg_made, unit(u - 2))
            for c, (t0, nt) in enumerate(PARTS):
                ins = act.copy(tsc[:, d % 2, t0:t0 + nt], bank[c][0:P, 0:nt * P].rearrange("p (t n) -> p t n", n=P))
            ins.then_inc(turned_taken, 1)

        def pe_unit_sum(pe, u, d, tsc, banks, feats):
            pe.wait_ge(turned_taken, unit(u))
            pe.wait_ge(agg_taken, unit(u - 2))
            for t in range(NT):
                for b, f in zip(banks, feats(t)):
                    w = f.shape[-1]
                    ins = pe.matmul(bank[b][0:P, 0:w], tsc[:, d % 2, t], f, start=(t == 0), stop=(t == NT - 1))
            ins.then_inc(agg_made, 1)

        def dve_unit_rden(dve, chain, u, d, add):
            dve.wait_ge(agg_made, unit(u))
            q = slice(d % 4, d % 4 + 1)
            chain(dve.tensor_scalar(rden[:, q], den[:, q], TINY, None, op0=ALU.add if add else ALU.max))
            chain(dve.reciprocal(rden[:, q], rden[:, q]))
            return rden[:, q]

        def dve_s_row(dve, uh, sd):
            for t in range(NT):
                dve.wait_ge(s_spread, unit(uh * NT + (t - 2)))
                dve.tensor_scalar(sd[:, t % 2], ident[0:P, 0:P], al_s[:, t:t + 1], None, op0=ALU.mult).then_inc(diag_made, 1)

        def pe_s_row(pe, uh, sd):
            pe.wait_ge(turned_taken, unit(uh * NT - 1))
            for t in range(NT):
                pe.wait_ge(diag_made, uh * NT + (t + 1))
                pe.matmul(bank[t // 4][0:P, (t % 4) * P:(t % 4 + 1) * P], ones[0:P, 0:P], sd[:, t % 2], start=True, stop=True).then_inc(s_spread, 1)

        def act_s_row(act, uh, srow):
            act.wait_ge(s_spread, unit(uh * NT + (NT - 1)))
            for c, (t0, nt) in enumerate(PARTS):
                v = slice(t0 * P, (t0 + nt) * P)
                act.copy(srow[:, v], bank[c][0:P, 0:nt * P])
                ins = act.activation(s_row_low[:, v], bank[c][0:P, 0:nt * P], ACT.Copy, scale=SLOPE)
            ins.then_inc(s_row_ready, 1)
        def run_of(eng, d):
            first = eng.value_load(table[0:1, d:d + 1], min_val=0, max_val=NT * NG)
            end = eng.value_load(table[0:1, d + 1:d + 2], min_val=0, max_val=NT * NG)
            return first, end

        def done_before(eng, p):
            return eng.value_load(table[0:1, NT:NT + 1], min_val=1, max_val=NT * NG) * p if p else 0

        def sum_pool(pool, p, src_d, width):
            past = done_before(pool, p)
            for d in range(NT):
                first, end = run_of(pool, d)
                with pool.Fori(first, end) as j:
                    for k in range(GT):
                        pool.wait_ge(pick_ready[k], j + past + 1)
                        settle(pool)
                        pool.indirect_dma_start(gathered[:, k, 0:width], None, src_d,
                                                bass.IndirectOffsetOnAxis(ap=idx_slot[:, k:k + 1], axis=0)).then_inc(row_landed[k], 16)

        def sum_dve(dve, p, idx, weight, take):
            past = done_before(dve, p)
            dve.wait_ge(iota_ready, 1)
            for d in range(NT):
                first, end = run_of(dve, d)
                shift = dve.value_load(table[0:1, NT + 1 + d:NT + 2 + d], min_val=-NT * NG * GT, max_val=ET)
                with dve.Fori(first, end) as j:
                    tile = nc.s_assert_within(j * GT + shift, 0, ET - 1)
                    for k in range(GT):
                        t = tile + k
                        dve.wait_ge(slot_used[k], j + past + 1)
                        dve.tensor_copy(idx_slot[:, k:k + 1], idx[:, bass.ds(t, 1)])
                        dve.tensor_scalar(pick[:, k], iota_row[:, d * P:(d + 1) * P], edge[:, DST, bass.ds(t, 1)],
                                          edge[:, weight, bass.ds(t, 1)], op0=ALU.is_equal, op1=ALU.mult).then_inc(pick_ready[k], 1)
                q = tick("sum_dve")
                dve.wait_ge(sum_made, q)
                take(d).then_inc(sum_taken, 1)

        def sum_pe(pe, p, width):
            halves = [(h * HD, HD) for h in range(2)] if width == D else [(0, width)]
            past = done_before(pe, p)
            pe.wait_ge(iota_ready, 1)
            for d in range(NT):
                first, end = run_of(pe, d)
                acc = bank[2 * (d % 2):2 * (d % 2) + 2]
                q = tick("sum_pe")
                if q > 2:
                    pe.wait_ge(sum_taken, q - 2)
                for (o, w), b in zip(halves, acc):
                    pe.matmul(b[0:P, 0:w], zeros[0:1, 0:P], iota_row[0:1, 0:w], start=True, stop=False)
                with pe.Fori(first, end) as j:
                    for k in range(GT):
                        pe.wait_ge(pick_ready[k], j + past + 1)
                        pe.wait_ge(row_landed[k], (j + past + 1) * 16)
                        for (o, w), b in zip(halves, acc):
                            ins = pe.matmul(b[0:P, 0:w], pick[:, k], gathered[:, k, o:o + w], start=False, stop=False)
                        ins.then_inc(slot_used[k], 1)
                for (o, w), b in zip(halves, acc):
                    ins = pe.matmul(b[0:P, 0:w], zeros[0:1, 0:P], iota_row[0:1, 0:w], start=False, stop=True)
                ins.then_inc(sum_made, 1)

        block = ctx.enter_context(nc.Block())

        @block.sync
        def _(sp):
            for s in y_stored:
                sp.sem_inc(s, 16)
            sp.dma_start(node_a, a["x"].rearrange("(n p) d -> p n d", p=P)).then_inc(bulk_loaded, 16)
            sp.wait_ge(rows_ready, 1)
            for i, v in enumerate([a["dst"], a["src"], a["edge_type_8"], a["edge_weight"]]):
                to = raw[:, i] if i < 3 else rows[:, i]
                sp.dma_start(to[0:128, 0, :], v[0:128 * 128].rearrange("(t e) -> t e", e=128)).then_inc(loaded, 16)
                sp.dma_start(to[0:FULL - 128, 1, :], v[128 * 128:FULL * 128].rearrange("(t e) -> t e", e=128)).then_inc(loaded, 16)
                sp.dma_start(to[FULL - 128:FULL - 127, 1, 0:TAIL], v[FULL * 128:E].rearrange("(t e) -> t e", e=TAIL)).then_inc(loaded, 16)
            sp.wait_ge(tile_taken, NT)
            sp.dma_start(count_d.rearrange("(n p) s -> p n s", p=P), lncount).then_inc(count_stored, 16)
            sp.wait_ge(inv_ready, 1)
            sp.dma_start(inv_d.rearrange("(n p r) o -> p n (r o)", p=P, r=R), inv_count[:]).then_inc(inv_stored, 16)
            sp.wait_ge(count_stored, 16)
            next_phase(sp)
            with sp.Fori(0, H0) as h:
                sp.wait_ge(h_made, unit(h * NT - 1))
                sp.dma_start(w_in, a["L0_gnn_W1"].rearrange("(k p) c -> p k c", p=128)[:, :, bass.ds(h * C0, C0)]).then_inc(w_in_loaded, 16)
                sp.wait_ge(agg_taken, unit(h * NT - 1))
                sp.dma_start(att_rows[:, 0], spread(a["L0_gnn_att_src1"][bass.ds(h, 1), :].rearrange("o c -> (o c)"), P)).then_inc(att_loaded, 16)
                sp.dma_start(att_rows[:, 1], spread(a["L0_gnn_att_dst1"][bass.ds(h, 1), :].rearrange("o c -> (o c)"), P)).then_inc(att_loaded, 16)
                sp.dma_start(b1_row, spread(a["L0_gnn_b1"][bass.ds(h * C0, C0)], P)).then_inc(b1_loaded, 16)
                sp.wait_ge(part_made, unit(h * NT - 1))
                sp.dma_start(w_out, a["L0_gnn_W2"][bass.ds(h * C0, C0), :].rearrange("(k p) c -> p k c", p=128)).then_inc(w_out_loaded, 16)
            next_phase(sp)
            sp.dma_start(wide_rows[:, 0], spread(a["L0_gnn_att_src2"][0, :], P)).then_inc(att_loaded, 16)
            sp.dma_start(wide_rows[:, 1], spread(a["L0_gnn_att_dst2"][0, :], P)).then_inc(att_loaded, 16)
            sp.dma_start(b2_row, spread(a["L0_gnn_b2"], P)).then_inc(b1_loaded, 16)
            for d in range(NT):
                if d >= 2:
                    sp.wait_ge(x_used, d - 1)
                sp.dma_start(x_slot[:, d % 2], a["x"][d * P:(d + 1) * P, :]).then_inc(x_loaded[d % 2], 16)
            next_phase(sp)
            for c in range(2):
                with sp.Fori(0, R) as r:
                    for h in range(2):
                        for n in range(NT):
                            i = (h * NT + n) % 4
                            sp.wait_ge(prod_taken, unit(r * (2 * NT) + ((c * (R + 1) + 1) * 2 + h) * NT + n))
                            sp.dma_start(y_d[bass.ds(r * N + n * P, P), h * HD:(h + 1) * HD], y_stage[:, i]).then_inc(y_stored[i], 16)
                next_phase(sp)
            for v, t in ((wd, a["L2_gnn_Wd"].rearrange("(k p) c -> p k c", p=128)), (wu, a["L2_gnn_Wu"]),
                         (bd_col, a["L2_gnn_bd"].rearrange("(p o) -> p o", o=1)), (bu_row, spread(a["L2_gnn_bu"], P)),
                         (gw1, a["L2_gnn_W1"].rearrange("(k p) c -> p k c", p=128)), (gb1_row, spread(a["L2_gnn_b1"], P))):
                sp.dma_start(v, t).then_inc(bulk_loaded, 16)
            for c in range(2):
                sp.wait_ge(xs_ready, c + 1)
                sp.dma_start(xs_d.rearrange("(n p) c -> p n c", p=P), xs).then_inc(xs_stored, 16)
            next_phase(sp)
            sp.dma_start(gw2, a["L2_gnn_W2"].rearrange("(k p) c -> p k c", p=128)).then_inc(bulk_loaded, 16)
            sp.dma_start(gb2_row, spread(a["L2_gnn_b2"], P)).then_inc(bulk_loaded, 16)
            next_phase(sp)
            sp.dma_start(lncount, count_d.rearrange("(n p) s -> p n s", p=P)).then_inc(bulk_loaded, 16)
            sp.dma_start(att3[:, 0], spread(a["L3_gnn_attn_l"][0].rearrange("h c -> (h c)"), P)).then_inc(bulk_loaded, 16)
            sp.dma_start(att3[:, 1], spread(a["L3_gnn_attn_r"][0].rearrange("h c -> (h c)"), P)).then_inc(bulk_loaded, 16)
            sp.wait_ge(w3_cleared, 1)
            for i, w in enumerate((a["L3_gnn_W"], a["L3_gnn_W_res"])):
                for q in range(2):
                    sp.dma_start(w3[q * C3:(q + 1) * C3, i, q * C3:(q + 1) * C3], w).then_inc(bulk_loaded, 16)
            next_phase(sp)
            for d in range(NT):
                sp.wait_ge(ln_done, 3 * NT + d + 1)
                sp.dma_start(out[d * P:(d + 1) * P, :], node_b[:, d]).then_inc(stored[d % 2], 16)
            for i in range(2):
                sp.wait_ge(stored[i], 16 * NT // 2)

        @block.gpsimd
        def _(pool):
            pool.memset(ident[:], 0.0).then_inc(consts, 1)
            pool.memset(ones[:], 1.0).then_inc(consts, 1)
            pool.memset(zeros[:], 0.0).then_inc(consts, 1)
            pool.memset(tri, 0.0).then_inc(consts, 1)
            pool.wait_ge(consts, 4)
            pool.affine_select(out=ident[:], in_=ident[:], compare_op=ALU.not_equal, fill=1.0, base=0,
                               pattern=[[-1, 128]], channel_multiplier=1).then_inc(consts, 1)
            pool.affine_select(out=tri, in_=tri, compare_op=ALU.is_ge, fill=1.0, base=0,
                               pattern=[[-1, NT + 1]], channel_multiplier=1).then_inc(consts, 1)
            pool.iota(iota_row[:], pattern=[[1, N]], base=0, channel_multiplier=0, allow_small_or_imprecise_dtypes=True).then_inc(consts, 1)
            pool.iota(start_i, pattern=[[1, 1]], base=0, channel_multiplier=P).then_inc(consts, 1)
            next_phase(pool)
            pool.memset(node_a, 0.0).then_inc(acc_cleared, 1)
            pool.wait_ge(inv_stored, 16)
            with pool.Fori(0, NG) as g:
                pool.tensor_copy(idx_slot[:], idx_cnt[:, bass.ds(g * GT, GT)]).then_inc(pool_step, 1)
                pool.wait_ge(pool_step, g * 2 + 1)
                settle(pool)
                for k in range(GT):
                    pool.indirect_dma_start(w_slot[:, k:k + 1], None, inv_d,
                                            bass.IndirectOffsetOnAxis(ap=idx_slot[:, k:k + 1], axis=0)).then_inc(w_landed, 16)
                pool.wait_ge(w_landed, (g + 1) * 16 * GT)
                pool.tensor_copy(edge[:, REL_W, bass.ds(g * GT, GT)], w_slot[:]).then_inc(pool_step, 1)
                pool.wait_ge(pool_step, g * 2 + 2)
            next_phase(pool)
            next_phase(pool)
            pool.iota(iota_row[:], pattern=[[1, N]], base=0, channel_multiplier=0, allow_small_or_imprecise_dtypes=True).then_inc(iota_ready, 1)
            for c in range(2):
                W, root, b = (a[f"L1_gnn_{n}{c + 1}"] for n in ("W", "root", "b"))
                pool.dma_start(bias_row, spread(b, P)).then_inc(bias_loaded, 16)
                for h in range(2):
                    if c:
                        pool.wait_ge(w_ready, unit(2 * (R + 1) * c + h - 2))
                    pool.dma_start(w_raw[:, h], root.rearrange("(k p) c -> p k c", p=128)[:, :, h * HD:(h + 1) * HD]).then_inc(raw_loaded[h], 16)
                with pool.Fori(0, R) as r:
                    for h in range(2):
                        pool.wait_ge(w_ready, unit(r * 2 + ((c * (R + 1) + 1) * 2 + h - 2)))
                        pool.dma_start(w_raw[:, h], W[bass.ds(r, 1), :, h * HD:(h + 1) * HD].rearrange("o (k p) c -> p (o k) c", p=128)).then_inc(raw_loaded[h], 16)
                for i in range(4):
                    pool.wait_ge(y_stored[i], 16 * (R * 2 * NT // 4 * (c + 1) + 1))
                sum_pool(pool, c, y_d, D)
                next_phase(pool)
            for c in range(2):
                pool.wait_ge(xs_stored, 16 * (c + 1))
                sum_pool(pool, 2 + c, xs_d, G2)
            next_phase(pool)
            next_phase(pool)
            pool.memset(w3, 0.0).then_inc(w3_cleared, 1)
            next_phase(pool)

        @block.scalar
        def _(act):
            for s in (prod_taken, turned_taken, weight_made, hT_ready):
                act.sem_inc(s, PRE)
            act_turn(act, "turn_act", xT, KD)
            act_ln(act, 0, score)
            act_sqrt(act, "sqrt_act", dinv[:])
            next_phase(act)
            with act.Fori(0, H0) as h:
                for n in range(NT):
                    act.wait_ge(h_made, unit(h * NT + n))
                    if n == 0:
                        act.wait_ge(agg_made, unit(h * NT - 1))
                    act.copy(h_head[:, n], bank[5 + n % 2][0:P, 0:C0]).then_inc(h_ready, 1)
                act_s_row(act, h, s_row)
                act_units(act, h, score, turned_score, True)
            next_phase(act)
            act_s_row(act, H0, s_row)
            act_units(act, H0, score, turned_score, False)
            act_sqrt(act, "sqrt_act", rstd[:])
            next_phase(act)
            for c in range(2):
                act_turn(act, "turn_act", xT_hi, KD, piece_high)
                for h in range(2):
                    for n in range(NT):
                        act.wait_ge(prod_made, unit((c * (R + 1) * 2 + h) * NT + n))
                        act.copy(node_a[:, n, h * HD:(h + 1) * HD], bank[(h * NT + n) % 4][0:P, 0:HD]).then_inc(prod_taken, 1)
                with act.Fori(0, R) as r:
                    for h in range(2):
                        for n in range(NT):
                            i = (h * NT + n) % 4
                            act.wait_ge(prod_made, unit(r * (2 * NT) + ((c * (R + 1) + 1) * 2 + h) * NT + n))
                            act.wait_ge(y_stored[i], (r * 5 + (c * 5 * R + (h * NT + n) // 4 + 1)) * 16)
                            act.copy(y_stage[:, i], bank[i][0:P, 0:HD]).then_inc(prod_taken, 1)
                if c == 1:
                    act_sqrt(act, "sqrt_act", rstd[:])
                next_phase(act)
            act_turn(act, "turn_act", xT, KD)
            act.wait_ge(bulk_loaded, 16 * 7)
            for c, (t0, nt) in enumerate(PARTS):
                act.wait_ge(t_made, c + 1)
                act.activation(tT[:, t0 * P:(t0 + nt) * P], bank[6][0:BOT, 0:nt * P], ACT.Relu, bias=bd_col).then_inc(t_taken, 1)
            act_turn(act, "turn_act", xT, KD)
            next_phase(act)
            act_turn(act, "turn_act", zT, KG2)
            act_sqrt(act, "sqrt_act", rstd[:])
            next_phase(act)
            act_ln(act, 1, ln_tmp3)
            act_turn(act, "turn_act", xT, KD)
            act.wait_ge(w3_turned, 1)
            act.copy(w3T.rearrange("p a b -> p (a b)"), bank[6][:, 0:256]).then_inc(w3T_ready, 1)
            for n in range(NT):
                for g in range(3):
                    q = 3 * n + g
                    act.wait_ge(f_made, q + 1)
                    act.copy(res3[:, n, g * 256:(g + 1) * 256].rearrange("p (c f) -> p c f", c=2),
                             bank[q % 6][0:P, :].rearrange("p (c i f) -> p c i f", c=2, i=2)[:, :, 1]).then_inc(r_taken, 1)
            next_phase(act)
            with act.Fori(0, H3) as h:
                act_s_row(act, h + (H0 + 1), s_row3)
                act_units(act, h + (H0 + 1), score3, turned3, False)
            act_sqrt(act, "sqrt_act", rstd[:])

        @block.tensor
        def _(pe):
            for s in (s_spread, score_turned, agg_made, h_made, part_made, prod_made, hidden_turned):
                pe.sem_inc(s, PRE)
            for s in hot_used + slot_used:
                pe.sem_inc(s, 1)
            pe.wait_ge(consts, 8)
            pe.wait_ge(diag_ready, 1)
            for i in range(4):
                w = 128 if i % 2 == 0 else ROWS1
                o = 256 * (i // 2) + 128 * (i % 2)
                ins = pe.matmul(bank[7][0:NT, o:o + w], ones[:, 0:NT], diags[:, i, 0:w], start=True, stop=True)
            ins.then_inc(spans_spread, 1)
            pe.wait_ge(reach_ready, 1)
            pe.matmul(bank[7][0:1, 448:448 + NT + 1], reach[:, 4:5], tri, start=True, stop=True)
            pe.matmul(bank[7][0:1, 449 + NT:449 + 2 * NT], reach[:, 2:3], ident[0:NT, 0:NT], start=True, stop=True).then_inc(table_made, 1)
            for i in range(4):
                pe.matmul(bank[i][:, 0:128], rows[:, i, 0, :], ident[:], start=True, stop=True)
                ins = pe.matmul(bank[i][:, 128:ET], rows[0:ROWS1, i, 1, :], ident[0:ROWS1, 0:ROWS1], start=True, stop=True)
            ins.then_inc(edges_turned, 1)
            pe.wait_ge(edges_taken, 1)
            pe.wait_ge(bulk_loaded, 16)
            pe_turn(pe, "turn_pe", node_a, KD)
            pe.wait_ge(piece_taken, counts["turn_pe"])
            pe.wait_ge(table_ready, 1)
            for d in range(NT):
                first, end = run_of(pe, d)
                acc = bank[4 * (d % 2):4 * (d % 2) + 4]
                widths = CW + [16]
                if d >= 2:
                    pe.wait_ge(tile_taken, d - 1)
                for b, w in zip(acc, widths):
                    pe.matmul(b[0:P, 0:w], zeros[0:1, 0:P], iota_row[0:1, 0:w], start=True, stop=False)
                with pe.Fori(first, end) as j:
                    for k in range(GT):
                        pe.wait_ge(hot_ready[k], j + 1)
                        for c in range(3):
                            pe.matmul(acc[c][0:P, 0:CW[c]], hot_dst[:, k], hot_src[:, k, CO[c]:CO[c] + CW[c]], start=False, stop=False)
                        ins = pe.matmul(acc[3][0:P, 0:16], hot_dst[:, k], feat[:, k], start=False, stop=False)
                        ins.then_inc(hot_used[k], 1)
                for b, w in zip(acc, widths):
                    ins = pe.matmul(b[0:P, 0:w], zeros[0:1, 0:P], iota_row[0:1, 0:w], start=False, stop=True)
                ins.then_inc(tile_counted, 1)
            next_phase(pe)
            with pe.Fori(0, H0) as h:
                pe.wait_ge(w_in_loaded, (h + 1) * 16)
                for n in range(NT):
                    if n < 2:
                        pe.wait_ge(hT_ready, unit(h * NT - 1))
                        pe.wait_ge(part_taken, unit(h * NT - 1))
                    else:
                        pe.wait_ge(h_ready, h * NT + (n - 1))
                    for k in range(KD):
                        ins = pe.matmul(bank[5 + n % 2][0:P, 0:C0], xT[:, k, n * P:(n + 1) * P], w_in[:, k], start=(k == 0), stop=(k == KD - 1))
                    ins.then_inc(h_made, 1)
                pe_s_row(pe, h, s_diag)
                pe.wait_ge(w_out_loaded, (h + 1) * 16)
                pe_units(pe, h, score, turned_score, lambda d: [3 + d % 2], lambda t: [h_head[:, t]], True)
            next_phase(pe)
            pe_s_row(pe, H0, s_diag)
            pe_units(pe, H0, score, turned_score, lambda d: [3 + 2 * (d % 2), 4 + 2 * (d % 2)],
                     lambda t: [node_a[:, t, 0:HD], node_a[:, t, HD:D]], False)
            next_phase(pe)
            for c in range(2):
                pe_turn(pe, "turn_pe", node_a if c else node_b, KD)
                pe.wait_ge(piece_taken, counts["turn_pe"])

                def half_product(m, p, h):
                    pe.wait_ge(w_ready, unit(m))
                    for n in range(NT):
                        pe.wait_ge(prod_taken, unit(p + (n - 4)))
                        b, v = bank[(h * NT + n) % 4][0:P, 0:HD], slice(n * P, (n + 1) * P)
                        for k in range(KD):
                            pe.matmul(b, xT_hi[:, k, v], w_hi[:, h, k], start=(k == 0), stop=False)
                            pe.matmul(b, xT_hi[:, k, v], w_lo[:, h, k], start=False, stop=False)
                            ins = pe.matmul(b, xT_lo[:, k, v], w_hi[:, h, k], start=False, stop=(k == KD - 1))
                        ins.then_inc(prod_made, 1)

                m0 = c * (R + 1) * 2
                for h in range(2):
                    half_product(m0 + h, (m0 + h) * NT, h)
                with pe.Fori(0, R) as r:
                    for h in range(2):
                        half_product(r * 2 + (m0 + 2 + h), r * (2 * NT) + (m0 + 2 + h) * NT, h)
                pe.wait_ge(prod_taken, unit((m0 + 2 * (R + 1)) * NT - 1))
                sum_pe(pe, c, D)
                next_phase(pe)
            pe_turn(pe, "turn_pe", node_b, KD)
            pe.wait_ge(piece_taken, counts["turn_pe"])
            pe.wait_ge(bulk_loaded, 16 * 7)
            for c, (t0, nt) in enumerate(PARTS):
                if c:
                    pe.wait_ge(t_taken, c)
                for k in range(KD):
                    ins = pe.matmul(bank[6][0:BOT, 0:nt * P], wd[:, k], xT[:, k, t0 * P:(t0 + nt) * P], start=(k == 0), stop=(k == KD - 1))
                ins.then_inc(t_made, 1)
            pe.wait_ge(t_taken, 3)
            for n in range(NT):
                if n >= 2:
                    pe.wait_ge(mm_taken, n - 1)
                for h in range(2):
                    ins = pe.matmul(bank[2 * (n % 2) + h][0:P, 0:HD], tT[:, n * P:(n + 1) * P], wu[:, h * HD:(h + 1) * HD], start=True, stop=True)
                ins.then_inc(mm_made, 1)
            pe.wait_ge(mm_taken, NT)
            pe_turn(pe, "turn_pe", node_a, KD)
            pe.wait_ge(piece_taken, counts["turn_pe"])
            for n in range(NT):
                if n >= 2:
                    pe.wait_ge(mm_taken, NT + n - 1)
                for k in range(KD):
                    ins = pe.matmul(bank[6 + n % 2][0:P, 0:G2], xT[:, k, n * P:(n + 1) * P], gw1[:, k], start=(k == 0), stop=(k == KD - 1))
                ins.then_inc(mm_made, 1)
            sum_pe(pe, 2, G2)
            sum_pe(pe, 3, G2)
            next_phase(pe)
            pe_turn(pe, "turn_pe", agg2, KG2)
            pe.wait_ge(piece_taken, counts["turn_pe"])
            pe.wait_ge(bulk_loaded, 16 * 9)
            for n in range(NT):
                if n >= 2:
                    pe.wait_ge(mm_taken, 2 * NT + n - 1)
                for h in range(2):
                    for k in range(KG2):
                        ins = pe.matmul(bank[2 * (n % 2) + h][0:P, 0:HD], zT[:, k, n * P:(n + 1) * P], gw2[:, k, h * HD:(h + 1) * HD],
                                        start=(k == 0), stop=(k == KG2 - 1))
                ins.then_inc(mm_made, 1)
            next_phase(pe)
            pe_turn(pe, "turn_pe", node_b, KD)
            pe.wait_ge(bulk_loaded, 16 * 16)
            for i in range(2):
                ins = pe.transpose(bank[6][:, i * 128:(i + 1) * 128], w3[:, i], ident[:])
            ins.then_inc(w3_turned, 1)
            pe.wait_ge(w3T_ready, 1)
            pe.wait_ge(piece_taken, counts["turn_pe"])
            for n in range(NT):
                for g in range(3):
                    q = 3 * n + g
                    if q >= 6:
                        pe.wait_ge(f_taken, q - 5)
                        pe.wait_ge(r_taken, q - 5)
                    for c in range(2):
                        ins = pe.matmul(bank[q % 6][0:P, c * 256:(c + 1) * 256], xT[:, 2 * g + c, n * P:(n + 1) * P],
                                        w3T.rearrange("p a b -> p (a b)"), start=True, stop=True)
                    ins.then_inc(f_made, 1)
            next_phase(pe)
            with pe.Fori(0, H3) as h:
                pe_s_row(pe, h + (H0 + 1), s_diag3)
                pe_units(pe, h + (H0 + 1), score3, turned3, lambda d: [3 + d % 2], lambda t: [node_a[:, t, bass.ds(h * C3, C3)]], False)

        @block.vector
        def _(dve):
            chain = Chain(dve, dve_step)
            for s in (w_ready, score_masked, agg_taken, hidden_ready, part_taken):
                dve.sem_inc(s, PRE)
            chain.mark(dve.memset(raw[:, 0], int(NEVER)))
            chain.mark(dve.memset(raw[:, 1:3], 0))
            chain.mark(dve.memset(rows[:, 3], 0.0))
            chain.mark(dve.memset(edge[:, DST, ET:EP], NEVER))
            chain.mark(dve.memset(edge[:, SRC:EW + 1, ET:EP], 0.0))
            chain.mark(dve.memset(edge[:, REL_W], 0.0))
            chain.wait()
            dve.memset(feat, 0.0).then_inc(rows_ready, 1)
            dve.wait_ge(consts, 8)
            chain.mark(dve.tensor_copy(iota_half, iota_row[:]))
            chain(dve.tensor_copy(tile_start[:], start_i))
            dve.wait_ge(loaded, 16 * 12)
            chain(dve.tensor_copy(rows[:, 0:3], raw[:, 0:3]))
            chain.mark(dve.tensor_reduce(span[:, 0:2], rows[:, 0], axis=AX_X, op=ALU.min))
            chain(dve.scalar_tensor_tensor(dst_low, rows[:, 0], NEVER, rows[:, 0], op0=ALU.is_lt, op1=ALU.mult))
            chain(dve.tensor_reduce(span[:, 2:4], dst_low, axis=AX_X, op=ALU.max))
            for i in range(4):
                ins = dve.tensor_scalar(diags[:, i], ident[:], span[:, i:i + 1], None, op0=ALU.mult)
            ins.then_inc(diag_ready, 1)
            dve.wait_ge(spans_spread, 1)
            chain.mark(dve.tensor_scalar(touch[:, 0], bank[7][0:NT, 0:ET], tile_start[0:NT], float(P), op0=ALU.subtract, op1=ALU.is_lt))
            chain(dve.tensor_scalar(touch[:, 1], bank[7][0:NT, 256:256 + ET], tile_start[0:NT], None, op0=ALU.is_ge))
            chain(dve.tensor_tensor(touch[:, 2], touch[:, 0], touch[:, 1], op=ALU.mult))
            chain.mark(dve.scalar_tensor_tensor(touch[:, 0], iota_row[0:NT, 0:ET], 1.0, touch[:, 2], op0=ALU.add, op1=ALU.mult))
            chain(dve.tensor_scalar(touch[:, 3], iota_row[0:NT, 0:ET], -1.0, float(ET), op0=ALU.mult, op1=ALU.add))
            chain.mark(dve.tensor_tensor(touch[:, 1], touch[:, 3], touch[:, 2], op=ALU.mult))
            chain(dve.tensor_reduce(reach[:, 0:1], touch[:, 0], axis=AX_X, op=ALU.max))
            chain(dve.tensor_reduce(reach[:, 1:2], touch[:, 1], axis=AX_X, op=ALU.max))
            chain(dve.tensor_scalar(reach[:, 5:6], reach[:, 1:2], 1.0, -1.0, op0=ALU.max, op1=ALU.mult))
            chain(dve.tensor_scalar(reach[:, 2:3], reach[:, 5:6], float(ET), None, op0=ALU.add))
            chain(dve.tensor_tensor(reach[:, 3:4], reach[:, 0:1], reach[:, 2:3], op=ALU.subtract))
            chain(dve.tensor_scalar(reach[:, 6:7], reach[:, 3:4], 1.0, None, op0=ALU.max))
            chain(dve.tensor_scalar(touch[:, 3, 0:NG], iota_row[0:NT, 0:NG], float(GT), reach[:, 6:7], op0=ALU.mult, op1=ALU.is_lt))
            dve.tensor_reduce(reach[:, 4:5], touch[:, 3, 0:NG], axis=AX_X, op=ALU.add).then_inc(reach_ready, 1)
            dve.wait_ge(table_made, 1)
            chain(dve.tensor_copy(diags[0:1, 0, 0:2 * NT + 1], bank[7][0:1, 448:448 + 2 * NT + 1]))
            chain.mark(dve.tensor_copy(table[:, 0:NT + 1], diags[0:1, 0, 0:NT + 1]))
            chain(dve.scalar_tensor_tensor(diags[0:1, 1, 0:NT], diags[0:1, 0, 0:NT], -float(GT), diags[0:1, 0, NT + 1:2 * NT + 1], op0=ALU.mult, op1=ALU.add))
            dve.tensor_copy(table[:, NT + 1:], diags[0:1, 1, 0:NT]).then_inc(table_ready, 1)
            dve.wait_ge(edges_turned, 1)
            for i in range(4):
                chain.mark(dve.tensor_copy(edge[:, i, 0:ET], bank[i][:, 0:ET]))
            chain.wait()
            chain(dve.scalar_tensor_tensor(edge[:, TMP], edge[:, TYP], float(N), edge[:, SRC], op0=ALU.mult, op1=ALU.add))
            chain.mark(dve.tensor_copy(idx_y[:], edge[:, TMP]))
            chain(dve.tensor_copy(idx_src[:], edge[:, SRC]))
            chain(dve.tensor_scalar(edge[:, TMP], edge[:, DST], float(N - 1), float(R), op0=ALU.min, op1=ALU.mult))
            chain(dve.tensor_tensor(edge[:, TMP], edge[:, TMP], edge[:, TYP], op=ALU.add))
            chain.mark(dve.tensor_copy(idx_cnt[:], edge[:, TMP]))
            chain(dve.tensor_copy(ew_parts[:, 0, 0:EP], edge[:, EW]))
            chain(dve.tensor_tensor(edge[:, TMP], edge[:, EW], ew_parts[:, 0, 0:EP], op=ALU.subtract))
            chain(dve.tensor_copy(ew_parts[:, 1, 0:EP], edge[:, TMP]))
            chain(dve.tensor_tensor(edge[:, TMP], edge[:, TMP], ew_parts[:, 1, 0:EP], op=ALU.subtract))
            chain(dve.tensor_copy(ew_parts[:, 2, 0:EP], edge[:, TMP]))
            dve.drain().then_inc(edges_taken, 1)
            dve.wait_ge(table_ready, 1)
            for d in range(NT):
                first, end = run_of(dve, d)
                shift = dve.value_load(table[0:1, NT + 1 + d:NT + 2 + d], min_val=-NT * NG * GT, max_val=ET)
                with dve.Fori(first, end) as j:
                    tile = nc.s_assert_within(j * GT + shift, 0, ET - 1)
                    for k in range(GT):
                        t = tile + k
                        dve.wait_ge(hot_used[k], j + 1)
                        dve.tensor_scalar(hot_dst[:, k], iota_row[:, d * P:(d + 1) * P], edge[:, DST, bass.ds(t, 1)], None, op0=ALU.is_equal)
                        dve.tensor_scalar(hot_src[:, k], iota_half, edge[:, SRC, bass.ds(t, 1)], None, op0=ALU.is_equal)
                        dve.tensor_scalar(feat[:, k, 0:R], iota_row[:, 0:R], edge[:, TYP, bass.ds(t, 1)], None, op0=ALU.is_equal)
                        ins = dve.tensor_copy(feat[:, k, R:R + 3], ew_parts[:, :, bass.ds(t, 1)].rearrange("p c o -> p (c o)"))
                        ins.then_inc(hot_ready[k], 1)
                dve.wait_ge(tile_counted, d + 1)
                for c in range(3):
                    dve.tensor_copy(lncount[:, d, CO[c]:CO[c] + CW[c]], bank[4 * (d % 2) + c][0:P, 0:CW[c]])
                chain.mark(dve.tensor_copy(degree[:, d], bank[4 * (d % 2) + 3][0:P, 0:16]))
                chain.wait()
                dve.drain().then_inc(tile_taken, 1)
            chain(dve.tensor_scalar(inv_count[:], degree[:, :, 0:R], 1.0, None, op0=ALU.max))
            dve.reciprocal(inv_count[:], inv_count[:]).then_inc(inv_ready, 1)
            chain(dve.tensor_tensor(dinv[:], degree[:, :, R], degree[:, :, R + 1], op=ALU.add))
            chain(dve.scalar_tensor_tensor(dinv[:], dinv[:], 1.0, degree[:, :, R + 2], op0=ALU.add, op1=ALU.add))
            dve.wait_ge(count_stored, 16)
            for d in range(NT):
                chain.mark(dve.tensor_tensor(lncount[:, d, d * P:(d + 1) * P], lncount[:, d, d * P:(d + 1) * P], ident[0:P, 0:P], op=ALU.add))
            chain.wait()
            dve_ln(dve, chain, 0, score)
            dve.drain().then_inc(sqrt_in, 1)
            dve.wait_ge(sqrt_done, tick("sqrt_dve"))
            chain(dve.reciprocal(dinv[:], dinv[:]))
            next_phase(dve)
            dve.wait_ge(acc_cleared, 1)
            A_STEPS = 8 * NT + 1
            with dve.Fori(0, H0) as h:
                chain.loop(h, A_STEPS)
                dve.wait_ge(att_loaded, (h + 1) * 32)
                dve.wait_ge(b1_loaded, (h + 1) * 16)
                for n in range(NT):
                    dve.wait_ge(h_ready, h * NT + (n + 1))
                    for i, al in enumerate((al_s, al_d)):
                        chain(dve.tensor_tensor_reduce(out=hidden[:, i], in0=h_head[:, n], in1=att_rows[:, i], scale=1.0, scalar=0.0,
                                                       op0=ALU.mult, op1=ALU.add, accum_out=al[:, n:n + 1]))
                chain(dve.tensor_scalar(al_d[:], al_d[:], 1.0 - SLOPE, None, op0=ALU.mult))
                dve_s_row(dve, h, s_diag)

                def leave_a(u, d):
                    r = dve_unit_rden(dve, chain, u, d, True)
                    dve.wait_ge(hidden_turned, unit(u - 2))
                    b = bank[3 + d % 2][0:P, 0:C0]
                    chain(dve.scalar_tensor_tensor(hidden[:, d % 2], b, r, b1_row, op0=ALU.mult, op1=ALU.add))
                    dve.tensor_scalar(b, hidden[:, d % 2], 0.0, None, op0=ALU.min).then_inc(elu_in, 1)

                def elu_a(u, d):
                    dve.wait_ge(elu_exp, u + 1)
                    chain(dve.scalar_tensor_tensor(hidden[:, d % 2], bank[3 + d % 2][0:P, 0:C0], -1.0, hidden[:, d % 2], op0=ALU.add, op1=ALU.max))
                    settle(dve)
                    dve.drain().then_inc(hidden_ready, 1)
                    dve.drain().then_inc(agg_taken, 1)

                def part_a(u, d):
                    dve.wait_ge(part_made, unit(u))
                    for g in range(2):
                        v = node_a[:, d, g * HD:(g + 1) * HD]
                        ins = dve.tensor_tensor(v, v, bank[6 + g][0:P, 0:HD], op=ALU.add)
                    ins.then_inc(part_taken, 1)

                dve_units(dve, chain, h, score, s_row, leave_a, elu_a, part_a)
                chain.end(H0, A_STEPS)
            next_phase(dve)
            dve.wait_ge(att_loaded, (H0 + 1) * 32)
            dve.wait_ge(b1_loaded, (H0 + 1) * 16)
            for n in range(NT):
                for i, al in enumerate((al_s, al_d)):
                    chain(dve.tensor_tensor_reduce(out=node_b[:, i], in0=node_a[:, n], in1=wide_rows[:, i], scale=1.0, scalar=0.0,
                                                   op0=ALU.mult, op1=ALU.add, accum_out=al[:, n:n + 1]))
            chain(dve.tensor_scalar(al_d[:], al_d[:], 1.0 - SLOPE, None, op0=ALU.mult))
            dve_s_row(dve, H0, s_diag)

            def leave_b(u, d):
                r = dve_unit_rden(dve, chain, u, d, True)
                for g in range(2):
                    v = slice(g * HD, (g + 1) * HD)
                    chain.mark(dve.scalar_tensor_tensor(node_b[:, d, v], bank[3 + 2 * (d % 2) + g][0:P, 0:HD], r, b2_row[:, v], op0=ALU.mult, op1=ALU.add))
                chain.wait()
                settle(dve)
                dve.drain().then_inc(agg_taken, 1)
                dve.wait_ge(x_loaded[d % 2], 16 * (d // 2 + 1))
                dve.tensor_tensor(node_b[:, d], node_b[:, d], x_slot[:, d % 2], op=ALU.add).then_inc(x_used, 1)

            dve_units(dve, chain, H0, score, s_row, leave_b, None, None)
            dve.wait_ge(x_used, NT)
            dve_norm(dve, chain, node_b, node_b)
            next_phase(dve)
            for c in range(2):
                dve_turn_low(dve, c)

                def split(m, i, h):
                    dve.wait_ge(raw_loaded[h], (i + 1) * 16)
                    dve.wait_ge(prod_made, unit(m * NT + (-NT - 1)))
                    chain(dve.tensor_copy(w_hi[:, h], w_raw[:, h]))
                    dve.tensor_tensor(w_lo[:, h], w_raw[:, h], w_hi[:, h].bitcast(F32), op=ALU.subtract).then_inc(w_ready, 1)

                m0 = c * (R + 1) * 2
                for h in range(2):
                    if m0 + h >= 2:
                        split(m0 + h, c * (R + 1), h)
                    else:
                        dve.wait_ge(raw_loaded[h], 16)
                        chain(dve.tensor_copy(w_hi[:, h], w_raw[:, h]))
                        dve.tensor_tensor(w_lo[:, h], w_raw[:, h], w_hi[:, h].bitcast(F32), op=ALU.subtract).then_inc(w_ready, 1)
                with dve.Fori(0, R) as r:
                    chain.loop(r, 2)
                    for h in range(2):
                        split(r * 2 + (m0 + 2 + h), r + (c * (R + 1) + 1), h)
                    chain.end(R, 2)
                dve.wait_ge(w_ready, unit(m0 + 2 * (R + 1) - 1))
                dve.wait_ge(bias_loaded, 16 * (1 + c))

                def take(d):
                    chain(dve.tensor_tensor(node_a[:, d], node_a[:, d], bias_row, op=ALU.add))
                    for g in range(2):
                        v = node_a[:, d, g * HD:(g + 1) * HD]
                        chain.mark(dve.tensor_tensor(v, v, bank[2 * (d % 2) + g][0:P, 0:HD], op=ALU.add))
                    chain.wait()
                    if c == 0:
                        return dve.tensor_scalar(node_a[:, d], node_a[:, d], 0.0, None, op0=ALU.max)
                    return dve.tensor_tensor(node_b[:, d], node_b[:, d], node_a[:, d], op=ALU.add)

                sum_dve(dve, c, idx_y, REL_W, take)
                if c == 1:
                    dve.wait_ge(sum_taken, 2 * NT)
                    dve_norm(dve, chain, node_b, node_b)
                next_phase(dve)
            dve.wait_ge(bulk_loaded, 16 * 7)
            for n in range(NT):
                dve.wait_ge(mm_made, n + 1)
                for g in range(2):
                    v = slice(g * HD, (g + 1) * HD)
                    chain.mark(dve.tensor_tensor(node_a[:, n, v], bank[2 * (n % 2) + g][0:P, 0:HD], bu_row[:, v], op=ALU.add))
                chain.wait()
                dve.tensor_tensor(node_a[:, n], node_a[:, n], node_b[:, n], op=ALU.add).then_inc(mm_taken, 1)
            for n in range(NT):
                dve.wait_ge(mm_made, NT + n + 1)
                dve.tensor_scalar(xs[:, n], bank[6 + n % 2][0:P, 0:G2], dinv[:, n:n + 1], None, op0=ALU.mult).then_inc(mm_taken, 1)
            dve.drain().then_inc(xs_ready, 1)

            def take_1(d):
                chain(dve.tensor_tensor(agg2[:, d], bank[2 * (d % 2)][0:P, 0:G2], xs[:, d], op=ALU.add))
                chain(dve.scalar_tensor_tensor(agg2[:, d], agg2[:, d], dinv[:, d:d + 1], gb1_row, op0=ALU.mult, op1=ALU.add))
                return dve.tensor_scalar(xs[:, d], agg2[:, d], 0.0, dinv[:, d:d + 1], op0=ALU.max, op1=ALU.mult)

            def take_2(d):
                chain(dve.tensor_tensor(agg2[:, d], bank[2 * (d % 2)][0:P, 0:G2], xs[:, d], op=ALU.add))
                return dve.tensor_scalar(agg2[:, d], agg2[:, d], dinv[:, d:d + 1], None, op0=ALU.mult)

            sum_dve(dve, 2, idx_src, EW, take_1)
            dve.drain().then_inc(xs_ready, 1)
            sum_dve(dve, 3, idx_src, EW, take_2)
            next_phase(dve)
            dve.wait_ge(bulk_loaded, 16 * 9)
            for n in range(NT):
                dve.wait_ge(mm_made, 2 * NT + n + 1)
                for g in range(2):
                    v = slice(g * HD, (g + 1) * HD)
                    chain.mark(dve.tensor_tensor(node_a[:, n, v], bank[2 * (n % 2) + g][0:P, 0:HD], gb2_row[:, v], op=ALU.add))
                chain.wait()
                dve.tensor_tensor(node_b[:, n], node_b[:, n], node_a[:, n], op=ALU.add).then_inc(mm_taken, 1)
            dve.wait_ge(mm_taken, 3 * NT)
            dve_norm(dve, chain, node_b, node_b)
            next_phase(dve)
            dve.wait_ge(bulk_loaded, 16 * 16)
            dve_ln(dve, chain, 1, ln_tmp3)
            for n in range(NT):
                for g in range(3):
                    q = 3 * n + g
                    dve.wait_ge(f_made, q + 1)
                    dve.wait_ge(r_taken, q + 1)
                    dve.tensor_copy(node_a[:, n, g * 256:(g + 1) * 256].rearrange("p (c f) -> p c f", c=2),
                                    bank[q % 6][0:P, :].rearrange("p (c i f) -> p c i f", c=2, i=2)[:, :, 0]).then_inc(f_taken, 1)
                dve.wait_ge(f_taken, 3 * (n + 1))
                for i in range(2):
                    chain(dve.tensor_tensor(scratch3, node_a[:, n], att3[:, i], op=ALU.mult))
                    chain(dve.tensor_reduce(al3[:, i, n], scratch3.rearrange("p (h c) -> p h c", c=C3), axis=AX_X, op=ALU.add))
            next_phase(dve)
            with dve.Fori(0, H3) as h:
                C_STEPS = 4 * NT + 2
                chain.loop(h, C_STEPS)
                u0 = h + (H0 + 1)
                chain.mark(dve.tensor_copy(al_s[:], al3[:, 0, :, bass.ds(h, 1)].rearrange("p n o -> p (n o)")))
                chain(dve.tensor_scalar(al_d[:], al3[:, 1, :, bass.ds(h, 1)].rearrange("p n o -> p (n o)"), 1.0 - SLOPE, None, op0=ALU.mult))
                dve_s_row(dve, u0, s_diag3)

                def leave_c(u, d):
                    r = dve_unit_rden(dve, chain, u, d, False)
                    v = res3[:, d, bass.ds(h * C3, C3)]
                    dve.scalar_tensor_tensor(v, bank[3 + d % 2][0:P, 0:C3], r, v, op0=ALU.mult, op1=ALU.add).then_inc(agg_taken, 1)

                dve_units(dve, chain, u0, score3, s_row3, leave_c, None, None)
                chain.end(H3, C_STEPS)
            dve.wait_ge(agg_taken, unit((H0 + 1 + H3) * NT - 1))
            for d in range(NT):
                chain.mark(dve.scalar_tensor_tensor(node_b[:, d], res3[:, d], 0.0, node_b[:, d], op0=ALU.max, op1=ALU.add))
            chain.wait()
            dve_norm(dve, chain, node_b, node_b)


_INS = ['x', 'src', 'dst', 'edge_type_8', 'edge_weight', 'L0_gnn_W1', 'L0_gnn_att_src1', 'L0_gnn_att_dst1', 'L0_gnn_b1',
        'L0_gnn_W2', 'L0_gnn_att_src2', 'L0_gnn_att_dst2', 'L0_gnn_b2', 'L1_gnn_W1', 'L1_gnn_root1', 'L1_gnn_b1',
        'L1_gnn_W2', 'L1_gnn_root2', 'L1_gnn_b2', 'L2_gnn_Wd', 'L2_gnn_bd', 'L2_gnn_Wu', 'L2_gnn_bu', 'L2_gnn_W1',
        'L2_gnn_b1', 'L2_gnn_W2', 'L2_gnn_b2', 'L3_gnn_W', 'L3_gnn_attn_l', 'L3_gnn_attn_r', 'L3_gnn_W_res']


def kernel(**inputs):
    import numpy as _np
    import concourse.bacc as _bacc
    from concourse import mybir as _mybir
    from concourse.bass_utils import run_bass_kernel_spmd as _run

    nc = _bacc.Bacc("TRN2", target_bir_lowering=False, num_devices=1)
    arrays, args = {}, {}
    for name in _INS:
        v = _np.ascontiguousarray(inputs[name])
        arrays[f"in_{name}_dram"] = v
        args[name] = nc.dram_tensor(f"in_{name}_dram", v.shape, _mybir.dt.from_np(v.dtype), kind="ExternalInput").ap()
    out = nc.dram_tensor("out_0_dram", inputs["x"].shape, _mybir.dt.float32, kind="ExternalOutput").ap()
    build(nc, args, out)
    r = _run(nc, [arrays], core_ids=[0])
    return r.results[0]["out_0_dram"]
```

```python
from contextlib import ExitStack

import concourse.bass as bass
from concourse import mybir

F32 = mybir.dt.float32
F32R = mybir.dt.float32r
BF16 = mybir.dt.bfloat16
F16 = mybir.dt.float16
I32 = mybir.dt.int32
ALU = mybir.AluOpType
ACT = mybir.ActivationFunctionType
AX_X = mybir.AxisListType.X

P = 125
NEVER = 30000.0


class Chain:

    def __init__(self, eng, done):
        self.eng, self.done, self.base, self.k = eng, done, 0, 0

    def mark(self, ins):
        ins.then_inc(self.done, 1)
        self.k += 1

    def wait(self):
        self.eng.wait_ge(self.done, self.base + self.k)

    def __call__(self, ins):
        self.mark(ins)
        self.wait()

    def loop(self, i, per):
        self.before = self.base + self.k
        self.base, self.k = self.before + i * per, 0

    def end(self, trips, per):
        assert self.k == per, f"{self.k} signals an iteration, not {per}"
        self.base, self.k = self.before + trips * per, 0


def build(nc, a, out):
    N, D = a["x"].shape
    E, = a["src"].shape
    NT = N // P
    KD = D // 128
    HD = D // 2
    GT = 5
    ET = -(-E // 128)
    EP = ET + GT
    NG = -(-ET // GT)
    R = a["L1_gnn_W1"].shape[0]
    FULL = E // 128
    TAIL = E - FULL * 128
    ROWS1 = ET - 128
    assert TAIL and GT * NG <= EP
    CW = [417, 417, 416]
    CO = [0, 417, 834]
    H0, C0 = a["L0_gnn_att_src1"].shape
    KC0 = C0 // 128
    _, H3, C3 = a["L3_gnn_attn_l"].shape
    BOT = a["L2_gnn_Wd"].shape[1]
    G2 = a["L2_gnn_W1"].shape[1]
    KG2 = G2 // 128
    PRE = 4
    V3 = (H0 + 1) * NT
    PAIR = 2 * NT
    SLOPE = 0.2
    ABSENT = 1e30
    CEILING = 1e29
    TINY = 1e-16
    EPS = 1e-5
    PARTS = [(0, 4), (4, 4), (8, NT - 8)]

    with ExitStack() as ctx:
        def sb(name, shape, dt=F32):
            return ctx.enter_context(nc.sbuf_tensor(name, shape, dt))

        def sem(name):
            return ctx.enter_context(nc.semaphore(name))

        def dram(name, shape, dt=F32):
            return nc.dram_tensor(name, shape, dt).ap()

        bank = [ctx.enter_context(nc.psum_tensor(f"bank{i}", [128, 512], F32)) for i in range(8)]

        ident = sb("ident", [128, 128])
        ones = sb("ones", [128, 128])
        zeros = sb("zeros", [1, 512], BF16)
        minus_one = sb("minus_one", [128, 1])
        iota_row = sb("iota_row", [128, N])
        tile_start = sb("tile_start", [128, 1])
        start_i = sb("start_i", [128, 1], I32)[:]
        table = sb("table", [1, 2 * NT + 1], I32)
        edge = sb("edge", [128, 6, EP])
        DST, SRC, TYP, EW, REL_W, TMP = range(6)
        idx_y = sb("idx_y", [128, EP], I32)
        idx_src = sb("idx_src", [128, EP], I32)
        idx_cnt = sb("idx_cnt", [128, EP], I32)
        idx_slot = sb("idx_slot", [128, GT], I32)
        w_slot = sb("w_slot", [128, GT])
        degree = sb("degree", [P, NT, 16])
        inv_count = sb("inv_count", [P, NT, R])
        dinv = sb("dinv", [P, NT])
        stats = sb("stats", [P, NT, 2, 6])
        moments = sb("moments", [P, NT, 2])
        rstd = sb("rstd", [P, NT])

        node = N // P * D
        fixed = 2 * node + KD * N
        REST = 26300
        XW = -(-KD * N // 16) * 16

        def placed(name, at, *shape, dt=F32R):
            n = 1
            for k in shape:
                n *= k
            assert at % 16 == 0
            with nc.sbuf_tensor(name + "_before", [128, at], F32), nc.sbuf_tensor(name, [128, n], dt) as t:
                v = t[:, :]
            names = "abcd"[:len(shape)]
            return v.rearrange(f"p ({' '.join(names)}) -> p {' '.join(names)}", **dict(zip(names, shape)))

        xT_hi = placed("xT_hi", 2 * node, KD, N)
        xT_lo = placed("xT_lo", 2 * node + XW, KD, N)
        w_at = 2 * (node + XW)
        HW = KD * HD
        w_raw = placed("w_raw", w_at, 2, KD, HD, dt=F32)
        w_hi = placed("w_hi", w_at + 2 * HW, 2, KD, HD)
        w_lo = placed("w_lo", w_at + 4 * HW, 2, KD, HD)
        arena = sb("arena", [128, fixed + REST])

        def cut(at, *shape, dt=F32, parts=128):
            n = 1
            for k in shape:
                n *= k
            if dt in (BF16, F16):
                n //= 2
            v = arena[0:parts, at:at + n]
            if dt != F32:
                v = v.bitcast(dt)
            names = "abcd"[:len(shape)]
            if len(shape) > 1:
                v = v.rearrange(f"p ({' '.join(names)}) -> p {' '.join(names)}", **dict(zip(names, shape)))
            return v

        node_a = cut(0, NT, D, parts=P)
        node_b = cut(node, NT, D, parts=P)
        xT = cut(2 * node, KD, N)
        rest = fixed

        mask = cut(rest, NT, N, parts=P)
        at = rest + NT * N
        raw = cut(at, 4, 2, 128, dt=I32)
        rows = cut(at + 1024, 4, 2, 128)
        dst_low = cut(at + 2048, 2, 128)
        diags = cut(at + 2304, 4, 128)
        iota_half = cut(at + 2816, N, dt=F16)
        at += 2816 + N
        span = cut(at, 4)
        touch = cut(at + 4, 4, ET, parts=NT)
        reach = cut(at + 4 + 4 * ET, 8, parts=NT)
        tri = cut(at + 12 + 4 * ET, NT + 1, parts=NT)
        assert at + 24 + 4 * ET <= rest + NT * N + 4 * N
        ew_parts = cut(node, 3, EP + EP % 2, dt=BF16)
        feat = cut(node + 2 * EP, EP, 16, dt=BF16)
        hot_dst = cut(node + 10 * EP, GT, P + 1, dt=BF16)[:, :, 0:P]
        hot_src = cut(node + 10 * EP + GT * (P + 1) // 2 + 1, GT, N, dt=BF16)
        assert 10 * EP + GT * (P + 1) // 2 + 1 + GT * N // 2 <= NT * C0 + 2 * C0

        at = rest + NT * N
        score = cut(at, 2, N, parts=P)
        turned_score = cut(at + 2 * N, 2, NT, P, parts=P)
        w_in = cut(at + 4 * N, KD, C0)
        w_out = cut(at + 4 * N + KD * C0, KC0, D)
        hT = cut(at + 4 * N + 2 * KD * C0, 2, KC0, P)
        at += 4 * N + 2 * KD * C0 + 2 * KC0 * P
        s_row = cut(at, N, parts=P)
        ln_row = cut(at, N, parts=P)
        ln_own = cut(at - 2 * P, P, parts=P)
        absent = cut(at - P, P, parts=P)
        s_diag = cut(at + N, 2, P + 3, parts=P)[:, :, 0:P]
        assert at + N + 256 <= rest + REST, at + N + 256 - rest
        h_head = cut(node, NT, C0, parts=P)
        hidden = cut(node + NT * C0, 2, C0, parts=P)
        att_rows = cut(node + NT * C0 + 2 * C0, 2, C0, parts=P)
        b1_row = cut(node + NT * C0 + 4 * C0, C0, parts=P)
        wide_rows = cut(rest + NT * N + 4 * N, 2, D, parts=P)
        b2_row = cut(rest + NT * N + 4 * N + 2 * D, D, parts=P)
        x_slot = cut(rest + NT * N + 4 * N + 3 * D, 2, D, parts=P)
        logit_out = cut(2 * node, 2, D, parts=P)
        res3 = cut(rest + NT * N, NT, D, parts=P)
        score3 = cut(2 * node, 4, N, parts=P)
        turned3 = cut(2 * node + 4 * N, 2, NT, P, parts=P)
        assert 6 * N <= KD * N
        al3 = cut(rest + NT * N + node, 2, NT, H3, parts=P)
        att3 = cut(rest + NT * N + node + 2 * NT * H3, 2, D, parts=P)
        w3 = cut(rest + NT * N + node + 2 * NT * H3 + 2 * D, 2, 128)
        w3T = cut(rest + NT * N + node + 2 * NT * H3 + 2 * D + 256, 2, 128)
        scratch3 = cut(rest + NT * N + node + 2 * NT * H3 + 2 * D + 512, D, parts=P)
        s_row3 = cut(rest + NT * N + node + 2 * NT * H3, 2, N, parts=P)
        s_low3 = cut(rest + NT * N + node + 2 * NT * H3 + 2 * N, 2, N, parts=P)
        s_diag3 = cut(rest + NT * N + node + 2 * NT * H3 + 4 * N, 4, P + 3, parts=P)[:, :, 0:P]
        s_row_low = iota_row[0:P, :]
        low = sb("low", [P, 4])
        den = sb("den", [P, 4])
        rden = sb("rden", [P, 4])
        al_s = sb("al_s", [P, NT])
        al_d = sb("al_d", [P, NT])

        gathered = cut(w_at, GT, D)
        pick = cut(w_at + GT * D, GT, P + 3)[:, :, 0:P]
        y_stage = cut(w_at + 6 * HW, 4, HD, parts=P)
        bias_row = cut(w_at + 6 * HW + 4 * HD, D, parts=P)
        assert w_at + 6 * HW + 4 * HD + D <= rest + REST
        wd = cut(rest, KD, BOT)
        wu = cut(rest + 256, D, parts=BOT)
        bd_col = cut(rest + 256 + D, 1, parts=BOT)
        bu_row = cut(rest + 260 + D, D, parts=P)
        tT = cut(rest + 260 + 2 * D, N, parts=BOT)
        gw1 = cut(rest + 260 + 2 * D + N, KD, G2)
        gb1_row = cut(rest + 260 + 2 * D + N + KD * G2, G2, parts=P)
        gcn_at = rest + 260 + 2 * D + N + KD * G2 + G2
        assert gcn_at <= w_at and GT * (D + 128) <= 6 * HW
        gw2 = cut(rest, KG2, D)
        zT = cut(rest + KG2 * D, KG2, N)
        gb2_row = cut(rest + KG2 * D + KG2 * N, D, parts=P)
        at = w_at + 6 * HW
        xs = cut(at, NT, G2, parts=P)
        assert at + NT * G2 <= rest + REST, at + NT * G2 - rest
        agg2 = cut(2 * node, NT, G2, parts=P)

        mask_d = dram("mask_d", [N, N])
        inv_d = dram("inv_d", [N * R, 1])
        y_d = dram("y_d", [R * N, D])
        xs_d = dram("xs_d", [N, G2])

        consts = sem("consts")
        phase_end, gate = sem("phase_end"), sem("gate")
        loaded = sem("loaded")
        dve_step = sem("dve_step")
        rows_ready, diag_ready, spans_spread = sem("rows_ready"), sem("diag_ready"), sem("spans_spread")
        reach_ready, table_made, table_ready = sem("reach_ready"), sem("table_made"), sem("table_ready")
        edges_turned, edges_taken = sem("edges_turned"), sem("edges_taken")
        hot_ready = [sem(f"hot_ready{i}") for i in range(GT)]
        hot_used = [sem(f"hot_used{i}") for i in range(GT)]
        tile_counted, tile_taken = sem("tile_counted"), sem("tile_taken")
        inv_ready, inv_stored = sem("inv_ready"), sem("inv_stored")
        pool_step, w_landed = sem("pool_step"), sem("w_landed")
        piece_made, piece_taken = sem("piece_made"), sem("piece_taken")
        score_masked, weight_made = sem("score_masked"), sem("weight_made")
        score_turned, turned_taken = sem("score_turned"), sem("turned_taken")
        agg_made, agg_taken = sem("agg_made"), sem("agg_taken")
        elu_in, elu_exp, hidden_ready = sem("elu_in"), sem("elu_exp"), sem("hidden_ready")
        hidden_turned, hT_ready, part_made, part_taken = sem("hidden_turned"), sem("hT_ready"), sem("part_made"), sem("part_taken")
        h_made, h_ready = sem("h_made"), sem("h_ready")
        diag_made, s_spread, s_row_ready = sem("diag_made"), sem("s_spread"), sem("s_row_ready")
        w3_cleared, w3_loaded, w3_turned, w3T_ready = sem("w3_cleared"), sem("w3_loaded"), sem("w3_turned"), sem("w3T_ready")
        iota_ready, bias_loaded = sem("iota_ready"), sem("bias_loaded")
        absent_marked = sem("absent_marked")
        acc_cleared, ln_shifted, ln_in, ln_out = sem("acc_cleared"), sem("ln_shifted"), sem("ln_in"), sem("ln_out")
        mask_step, mask_stored, mask_loaded = sem("mask_step"), sem("mask_stored"), sem("mask_loaded")
        f_made, f_taken, r_taken = sem("f_made"), sem("f_taken"), sem("r_taken")
        t_made, t_taken = sem("t_made"), sem("t_taken")
        w_in_loaded, w_out_loaded = sem("w_in_loaded"), sem("w_out_loaded")
        att_loaded, b1_loaded = sem("att_loaded"), sem("b1_loaded")
        x_loaded = [sem(f"x_loaded{i}") for i in range(2)]
        x_used = sem("x_used")
        bulk_loaded = sem("bulk_loaded")
        raw_loaded = [sem(f"raw_loaded{i}") for i in range(2)]
        w_ready, prod_made, prod_taken = sem("w_ready"), sem("prod_made"), sem("prod_taken")
        piece_high = sem("piece_high")
        y_stored = [sem(f"y_stored{i}") for i in range(4)]
        pick_ready = [sem(f"pick_ready{i}") for i in range(GT)]
        row_landed = [sem(f"row_landed{i}") for i in range(GT)]
        slot_used = [sem(f"slot_used{i}") for i in range(GT)]
        sum_made, sum_taken = sem("sum_made"), sem("sum_taken")
        mm_made, mm_taken = sem("mm_made"), sem("mm_taken")
        sqrt_in, sqrt_done = sem("sqrt_in"), sem("sqrt_done")
        xs_ready, xs_stored = sem("xs_ready"), sem("xs_stored")
        stored = [sem(f"stored{i}") for i in range(2)]
        ln_done = sem("ln_done")

        def spread(v, n):
            return v.partition_broadcast(n)

        def settle(eng):
            eng.sem_inc(gate, 1)

        phases = {}

        def next_phase(eng):
            n = phases[eng] = phases.get(eng, 0) + 1
            eng.drain().then_inc(phase_end, 1)
            eng.wait_ge(phase_end, 5 * n)

        def unit(u):
            return u + 1 + PRE

        def piece(u, c):
            return 3 * u + c + 1 + 3 * PRE

        counts = {}

        def tick(name, by=1):
            counts[name] = counts.get(name, 0) + by
            return counts[name]

        PIECES = [(k, c) for k in range(KD) for c in range(3)]

        def pe_turn(pe, name, src, kd):
            for k in range(kd):
                for c, (t0, nt) in enumerate(PARTS):
                    q = tick(name) - 1
                    if q >= 6:
                        pe.wait_ge(piece_taken, q - 5)
                    for t in range(nt):
                        ins = pe.transpose(bank[q % 6][:, t * P:(t + 1) * P], src[:, t0 + t, k * 128:(k + 1) * 128], ident[0:P, 0:P])
                    ins.then_inc(piece_made, 1)

        def act_turn(act, name, dst, kd, done=None):
            for k in range(kd):
                for c, (t0, nt) in enumerate(PARTS):
                    q = tick(name) - 1
                    act.wait_ge(piece_made, q + 1)
                    act.copy(dst[:, k, t0 * P:(t0 + nt) * P], bank[q % 6][:, 0:nt * P]).then_inc(done or piece_taken, 1)

        def dve_turn_low(dve, c):
            for q in range(3 * KD):
                k, (t0, nt) = q // 3, PARTS[q % 3]
                v = slice(t0 * P, (t0 + nt) * P)
                dve.wait_ge(piece_high, 3 * KD * c + q + 1)
                b = (3 * KD * (c + 1) + q) % 6
                dve.tensor_tensor(xT_lo[:, k, v], bank[b][:, 0:nt * P], xT_hi[:, k, v].bitcast(F32), op=ALU.subtract).then_inc(piece_taken, 1)

        def dve_stats(dve, chain, t, d):
            for h in range(2):
                chain.mark(dve.bn_stats(stats[:, d, h], t[:, d, h * HD:(h + 1) * HD]))

        def dve_norm(dve, chain, t, to):
            chain.wait()
            for d in range(NT):
                chain.mark(dve.bn_aggr(moments[:, d], stats[:, d].rearrange("p a b -> p (a b)")))
            chain.wait()
            dve.tensor_scalar(rstd[:], moments[:, :, 1], EPS, None, op0=ALU.add).then_inc(sqrt_in, 1)
            dve.wait_ge(sqrt_done, tick("sqrt_dve"))
            chain(dve.reciprocal(rstd[:], rstd[:]))
            for d in range(NT):
                dve.tensor_scalar(to[:, d], t[:, d], moments[:, d, 0:1], rstd[:, d:d + 1], op0=ALU.subtract, op1=ALU.mult).then_inc(ln_done, 1)

        def act_sqrt(act, name, v):
            act.wait_ge(sqrt_in, tick(name))
            act.activation(v, v, ACT.Sqrt).then_inc(sqrt_done, 1)

        def act_units(act, uh, sc, tsc, elu):
            for s in range(0, NT + 3):
                if s < NT:
                    act_unit_exp(act, uh * NT + s, s, sc[:, s % 2])
                if 0 <= s - 1 < NT:
                    act_unit_take(act, uh * NT + (s - 1), tsc[:, (s - 1) % 2])
                if elu and 0 <= s - 3:
                    u, d = uh * NT + (s - 3), s - 3
                    act.wait_ge(elu_in, u + 1)
                    b = bank[3 + d % 2][0:P, 0:C0]
                    act.activation(b, b, ACT.Exp).then_inc(elu_exp, 1)
                    act.wait_ge(hidden_turned, unit(u))
                    act.wait_ge(part_made, unit(u - 2))
                    act.copy(hT[:, d % 2].rearrange("p k n -> p (k n)"), bank[5][:, 0:KC0 * P]).then_inc(hT_ready, 1)

        def pe_units(pe, uh, sc, tsc, banks, feats, elu):
            for s in range(0, NT + 2):
                if s < NT:
                    pe_unit_turn(pe, uh * NT + s, sc[:, s % 2])
                if 0 <= s - 1 < NT:
                    pe_unit_sum(pe, uh * NT + (s - 1), tsc[:, (s - 1) % 2], banks(s - 1), feats)
                if elu and 0 <= s - 2:
                    u, d = uh * NT + (s - 2), s - 2
                    pe.wait_ge(hidden_ready, unit(u))
                    pe.wait_ge(hT_ready, unit(u - 1))
                    for k in range(KC0):
                        ins = pe.transpose(bank[5][:, k * P:(k + 1) * P], hidden[:, d % 2, k * 128:(k + 1) * 128], ident[0:P, 0:P])
                    ins.then_inc(hidden_turned, 1)
                    pe.wait_ge(hT_ready, unit(u))
                    pe.wait_ge(part_taken, unit(u - 1))
                    for g in range(2):
                        for k in range(KC0):
                            ins = pe.matmul(bank[6 + g][0:P, 0:HD], hT[:, d % 2, k], w_out[:, k, g * HD:(g + 1) * HD],
                                            start=(k == 0), stop=(k == KC0 - 1))
                    ins.then_inc(part_made, 1)

        def dve_units(dve, chain, uh, sc, srow, leave, late, part, before=None):
            dve.wait_ge(s_row_ready, uh + 1)
            for s in range(-1, NT + 3):
                if s + 1 < NT:
                    d = s + 1
                    if before:
                        before(d)
                    dve_unit_mask(dve, chain, uh * NT + d, 2, d, sc[:, d % 2], mask[:, d], srow, s_row_low, al_d[:, d:d + 1])
                if 0 <= s - 2 < NT:
                    leave(uh * NT + (s - 2), s - 2)
                if late and 0 <= s - 2 < NT:
                    late(uh * NT + (s - 2), s - 2)
                if part and 0 <= s - 3:
                    part(uh * NT + (s - 3), s - 3)

        def act_unit_exp(act, u, d, sc):
            act.wait_ge(score_masked, unit(u))
            act.activation(sc, sc, ACT.Exp, scale=-1.0, bias=low[:, d % 4:d % 4 + 1], accum_out=den[:, d % 4:d % 4 + 1]).then_inc(weight_made, 1)

        def dve_unit_mask(dve, chain, u, lag, d, sc, mask_row, srow, srow_low, ald, between=None):
            dve.wait_ge(score_turned, piece(u - lag, 2))
            chain.mark(dve.scalar_tensor_tensor(sc, srow, ald, srow_low, op0=ALU.add, op1=ALU.min))
            then = between() if between else None
            chain.wait()
            settle(dve)
            if then:
                then()
            dve.tensor_tensor_reduce(out=sc, in0=sc, in1=mask_row, scale=1.0, scalar=CEILING,
                                     op0=ALU.add, op1=ALU.min, accum_out=low[:, d % 4:d % 4 + 1]).then_inc(score_masked, 1)

        def pe_unit_turn(pe, u, sc):
            pe.wait_ge(weight_made, unit(u))
            for c, (t0, nt) in enumerate(PARTS):
                pe.wait_ge(turned_taken, piece(u - 1, c))
                for t in range(nt):
                    ins = pe.transpose(bank[c][0:P, t * P:(t + 1) * P], sc[:, (t0 + t) * P:(t0 + t + 1) * P], ident[0:P, 0:P])
                ins.then_inc(score_turned, 1)

        def act_unit_take(act, u, tsc):
            act.wait_ge(agg_made, unit(u - 2))
            for c, (t0, nt) in enumerate(PARTS):
                act.wait_ge(score_turned, piece(u, c))
                act.copy(tsc[:, t0:t0 + nt], bank[c][0:P, 0:nt * P].rearrange("p (t n) -> p t n", n=P)).then_inc(turned_taken, 1)

        def pe_unit_sum(pe, u, tsc, banks, feats):
            pe.wait_ge(agg_taken, unit(u - 2))
            for c, (t0, nt) in enumerate(PARTS):
                pe.wait_ge(turned_taken, piece(u, c))
                for t in range(t0, t0 + nt):
                    for b, f in zip(banks, feats(t)):
                        w = f.shape[-1]
                        ins = pe.matmul(bank[b][0:P, 0:w], tsc[:, t], f, start=(t == 0), stop=(t == NT - 1))
            ins.then_inc(agg_made, 1)

        def dve_unit_rden(dve, chain, u, d):
            dve.wait_ge(agg_made, unit(u))
            q = slice(d % 4, d % 4 + 1)
            chain(dve.tensor_scalar(rden[:, q], den[:, q], TINY, None, op0=ALU.add))
            chain(dve.reciprocal(rden[:, q], rden[:, q]))
            return rden[:, q]

        def dve_diag(dve, v, ring, sd, als):
            dve.wait_ge(s_spread, unit(v - ring))
            dve.tensor_scalar(sd, ident[0:P, 0:P], als, -1.0, op0=ALU.mult, op1=ALU.mult).then_inc(diag_made, 1)

        def pe_spread(pe, v, t, b0, sd):
            pe.wait_ge(diag_made, v + 1)
            pe.matmul(bank[b0 + t // 4][0:P, (t % 4) * P:(t % 4 + 1) * P], ones[0:P, 0:P], sd, start=True, stop=True).then_inc(s_spread, 1)

        def act_spread(act, v, c, b0, srow, low):
            t0, nt = PARTS[c]
            act.wait_ge(s_spread, unit(v + (t0 + nt - 1)))
            w = slice(t0 * P, (t0 + nt) * P)
            act.copy(srow[:, w], bank[b0 + c][0:P, 0:nt * P])
            return act.activation(low[:, w], bank[b0 + c][0:P, 0:nt * P], ACT.Copy, scale=SLOPE)

        def dve_s_row(dve, uh, sd):
            for t in range(NT):
                dve_diag(dve, uh * NT + t, 2, sd[:, t % 2], al_s[:, t:t + 1])

        def pe_s_row(pe, uh, sd):
            pe.wait_ge(turned_taken, piece(uh * NT - 1, 2))
            for t in range(NT):
                pe_spread(pe, uh * NT + t, t, 0, sd[:, t % 2])

        def act_s_row(act, uh, srow):
            for c in range(3):
                ins = act_spread(act, uh * NT, c, 0, srow, s_row_low)
            ins.then_inc(s_row_ready, 1)

        def runs_of(eng):
            return [eng.value_load(table[0:1, d:d + 1], min_val=0, max_val=NT * NG) for d in range(NT + 1)]

        def done_before(eng, p):
            return eng.value_load(table[0:1, NT:NT + 1], min_val=1, max_val=NT * NG) * p if p else 0

        def sum_pool(pool, p, src_d, width):
            past = done_before(pool, p)
            runs = runs_of(pool)
            for d in range(NT):
                with pool.Fori(runs[d], runs[d + 1]) as j:
                    for k in range(GT):
                        pool.wait_ge(pick_ready[k], j + past + 1)
                        settle(pool)
                        pool.indirect_dma_start(gathered[:, k, 0:width], None, src_d,
                                                bass.IndirectOffsetOnAxis(ap=idx_slot[:, k:k + 1], axis=0)).then_inc(row_landed[k], 16)

        def sum_dve(dve, p, idx, weight, take):
            past = done_before(dve, p)
            dve.wait_ge(iota_ready, 1)
            runs = runs_of(dve)
            for d in range(NT):
                first, end = runs[d], runs[d + 1]
                shift = dve.value_load(table[0:1, NT + 1 + d:NT + 2 + d], min_val=-NT * NG * GT, max_val=ET)
                with dve.Fori(first, end) as j:
                    tile = nc.s_assert_within(j * GT + shift, 0, ET - 1)
                    for k in range(GT):
                        t = tile + k
                        dve.wait_ge(slot_used[k], j + past + 1)
                        dve.tensor_copy(idx_slot[:, k:k + 1], idx[:, bass.ds(t, 1)])
                        dve.tensor_scalar(pick[:, k], iota_row[:, d * P:(d + 1) * P], edge[:, DST, bass.ds(t, 1)],
                                          edge[:, weight, bass.ds(t, 1)], op0=ALU.is_equal, op1=ALU.mult).then_inc(pick_ready[k], 1)
                if d:
                    dve.wait_ge(sum_made, p * NT + d)
                    take(d - 1).then_inc(sum_taken, 1)
            dve.wait_ge(sum_made, (p + 1) * NT)
            take(NT - 1).then_inc(sum_taken, 1)

        def sum_pe(pe, p, width):
            halves = [(h * HD, HD) for h in range(2)] if width == D else [(0, width)]
            past = done_before(pe, p)
            pe.wait_ge(iota_ready, 1)
            runs = runs_of(pe)
            for d in range(NT):
                first, end = runs[d], runs[d + 1]
                acc = bank[2 * (d % 2):2 * (d % 2) + 2]
                q = tick("sum_pe")
                if q > 2:
                    pe.wait_ge(sum_taken, q - 2)
                for (o, w), b in zip(halves, acc):
                    pe.matmul(b[0:P, 0:w], zeros[0:1, 0:P], zeros[0:1, 0:w], start=True, stop=False)
                with pe.Fori(first, end) as j:
                    for k in range(GT):
                        pe.wait_ge(pick_ready[k], j + past + 1)
                        pe.wait_ge(row_landed[k], (j + past + 1) * 16)
                        for (o, w), b in zip(halves, acc):
                            ins = pe.matmul(b[0:P, 0:w], pick[:, k], gathered[:, k, o:o + w], start=False, stop=False)
                        ins.then_inc(slot_used[k], 1)
                for (o, w), b in zip(halves, acc):
                    ins = pe.matmul(b[0:P, 0:w], zeros[0:1, 0:P], zeros[0:1, 0:w], start=False, stop=True)
                ins.then_inc(sum_made, 1)

        block = ctx.enter_context(nc.Block())

        @block.sync
        def _(sp):
            for s in y_stored:
                sp.sem_inc(s, 16)
            sp.dma_start(node_a, a["x"].rearrange("(n p) d -> p n d", p=P)).then_inc(bulk_loaded, 16)
            sp.wait_ge(rows_ready, 1)
            for i, v in enumerate([a["dst"], a["src"], a["edge_type_8"], a["edge_weight"]]):
                to = raw[:, i] if i < 3 else rows[:, i]
                sp.dma_start(to[0:128, 0, :], v[0:128 * 128].rearrange("(t e) -> t e", e=128)).then_inc(loaded, 16)
                sp.dma_start(to[0:FULL - 128, 1, :], v[128 * 128:FULL * 128].rearrange("(t e) -> t e", e=128)).then_inc(loaded, 16)
                sp.dma_start(to[FULL - 128:FULL - 127, 1, 0:TAIL], v[FULL * 128:E].rearrange("(t e) -> t e", e=TAIL)).then_inc(loaded, 16)
            sp.wait_ge(inv_ready, 1)
            sp.dma_start(inv_d.rearrange("(n p r) o -> p n (r o)", p=P, r=R), inv_count[:]).then_inc(inv_stored, 16)
            sp.dma_start(w_in, a["L0_gnn_W1"].rearrange("(k p) c -> p k c", p=128)[:, :, 0:C0]).then_inc(w_in_loaded, 16)
            sp.dma_start(att_rows[:, 0], spread(a["L0_gnn_att_src1"][0, :], P)).then_inc(att_loaded, 16)
            sp.dma_start(att_rows[:, 1], spread(a["L0_gnn_att_dst1"][0, :], P)).then_inc(att_loaded, 16)
            sp.dma_start(b1_row, spread(a["L0_gnn_b1"][0:C0], P)).then_inc(b1_loaded, 16)
            sp.dma_start(w_out, a["L0_gnn_W2"][0:C0, :].rearrange("(k p) c -> p k c", p=128)).then_inc(w_out_loaded, 16)
            next_phase(sp)
            with sp.Fori(1, H0) as h:
                sp.wait_ge(h_made, unit(h * NT - 1))
                sp.dma_start(w_in, a["L0_gnn_W1"].rearrange("(k p) c -> p k c", p=128)[:, :, bass.ds(h * C0, C0)]).then_inc(w_in_loaded, 16)
                sp.wait_ge(agg_taken, unit(h * NT - 1))
                sp.dma_start(att_rows[:, 0], spread(a["L0_gnn_att_src1"][bass.ds(h, 1), :].rearrange("o c -> (o c)"), P)).then_inc(att_loaded, 16)
                sp.dma_start(att_rows[:, 1], spread(a["L0_gnn_att_dst1"][bass.ds(h, 1), :].rearrange("o c -> (o c)"), P)).then_inc(att_loaded, 16)
                sp.dma_start(b1_row, spread(a["L0_gnn_b1"][bass.ds(h * C0, C0)], P)).then_inc(b1_loaded, 16)
                sp.wait_ge(part_made, unit(h * NT - 1))
                sp.dma_start(w_out, a["L0_gnn_W2"][bass.ds(h * C0, C0), :].rearrange("(k p) c -> p k c", p=128)).then_inc(w_out_loaded, 16)
            next_phase(sp)
            sp.dma_start(wide_rows[:, 0], spread(a["L0_gnn_att_src2"][0, :], P)).then_inc(att_loaded, 16)
            sp.dma_start(wide_rows[:, 1], spread(a["L0_gnn_att_dst2"][0, :], P)).then_inc(att_loaded, 16)
            sp.dma_start(b2_row, spread(a["L0_gnn_b2"], P)).then_inc(b1_loaded, 16)
            for d in range(NT):
                if d >= 2:
                    sp.wait_ge(x_used, d - 1)
                sp.dma_start(x_slot[:, d % 2], a["x"][d * P:(d + 1) * P, :]).then_inc(x_loaded[d % 2], 16)
            next_phase(sp)
            for c in range(2):
                with sp.Fori(0, R) as r:
                    for h in range(2):
                        for n in range(NT):
                            i = (h * NT + n) % 4
                            sp.wait_ge(prod_taken, unit(r * (2 * NT) + ((c * (R + 1) + 1) * 2 + h) * NT + n))
                            sp.dma_start(y_d[bass.ds(r * N + n * P, P), h * HD:(h + 1) * HD], y_stage[:, i]).then_inc(y_stored[i], 16)
                next_phase(sp)
            for v, t in ((wd, a["L2_gnn_Wd"].rearrange("(k p) c -> p k c", p=128)), (wu, a["L2_gnn_Wu"]),
                         (bd_col, a["L2_gnn_bd"].rearrange("(p o) -> p o", o=1)), (bu_row, spread(a["L2_gnn_bu"], P)),
                         (gw1, a["L2_gnn_W1"].rearrange("(k p) c -> p k c", p=128)), (gb1_row, spread(a["L2_gnn_b1"], P))):
                sp.dma_start(v, t).then_inc(bulk_loaded, 16)
            for c in range(2):
                sp.wait_ge(xs_ready, c + 1)
                sp.dma_start(xs_d.rearrange("(n p) c -> p n c", p=P), xs).then_inc(xs_stored, 16)
            next_phase(sp)
            sp.dma_start(gw2, a["L2_gnn_W2"].rearrange("(k p) c -> p k c", p=128)).then_inc(bulk_loaded, 16)
            sp.dma_start(gb2_row, spread(a["L2_gnn_b2"], P)).then_inc(bulk_loaded, 16)
            sp.dma_start(att3[:, 0], spread(a["L3_gnn_attn_l"][0].rearrange("h c -> (h c)"), P)).then_inc(w3_loaded, 16)
            sp.dma_start(att3[:, 1], spread(a["L3_gnn_attn_r"][0].rearrange("h c -> (h c)"), P)).then_inc(w3_loaded, 16)
            sp.wait_ge(w3_cleared, 1)
            for i, w in enumerate((a["L3_gnn_W"], a["L3_gnn_W_res"])):
                for q in range(2):
                    sp.dma_start(w3[q * C3:(q + 1) * C3, i, q * C3:(q + 1) * C3], w).then_inc(w3_loaded, 16)
            next_phase(sp)
            sp.dma_start(mask, mask_d.rearrange("(n p) s -> p n s", p=P)).then_inc(mask_loaded, 16)
            next_phase(sp)
            for d in range(NT):
                sp.wait_ge(ln_done, 3 * NT + d + 1)
                sp.dma_start(out[d * P:(d + 1) * P, :], node_b[:, d]).then_inc(stored[d % 2], 16)
            for i in range(2):
                sp.wait_ge(stored[i], 16 * NT // 2)

        @block.gpsimd
        def _(pool):
            pool.memset(ident[:], 0.0).then_inc(consts, 1)
            pool.memset(ones[:], 1.0).then_inc(consts, 1)
            pool.memset(zeros[:], 0.0).then_inc(consts, 1)
            pool.memset(minus_one[:], -1.0).then_inc(consts, 1)
            pool.memset(tri, 0.0).then_inc(consts, 1)
            pool.wait_ge(consts, 5)
            pool.affine_select(out=ident[:], in_=ident[:], compare_op=ALU.not_equal, fill=1.0, base=0,
                               pattern=[[-1, 128]], channel_multiplier=1).then_inc(consts, 1)
            pool.affine_select(out=tri, in_=tri, compare_op=ALU.is_ge, fill=1.0, base=0,
                               pattern=[[-1, NT + 1]], channel_multiplier=1).then_inc(consts, 1)
            pool.iota(iota_row[:], pattern=[[1, N]], base=0, channel_multiplier=0, allow_small_or_imprecise_dtypes=True).then_inc(consts, 1)
            pool.iota(start_i, pattern=[[1, 1]], base=0, channel_multiplier=P).then_inc(consts, 1)
            chain = Chain(pool, mask_step)
            for d in range(NT):
                own = mask[:, d, d * P:(d + 1) * P]
                pool.wait_ge(tile_taken, 4 * (d + 1))
                chain(pool.tensor_tensor(ln_own, own, ident[0:P, 0:P], op=ALU.add))
                chain(pool.tensor_scalar(absent, ln_own, 0.5, ABSENT, op0=ALU.is_lt, op1=ALU.mult))
                pool.tensor_scalar(ln_own, ln_own, 1.0, None, op0=ALU.max).then_inc(ln_in, 1)
                if d == NT - 1:
                    next_phase(pool)
                pool.wait_ge(absent_marked, d + 1)
                pool.wait_ge(ln_out, 2 * (d + 1))
                chain(pool.tensor_tensor(mask[:, d], mask[:, d], ln_row, op=ALU.subtract))
                pool.dma_start(mask_d[d * P:(d + 1) * P, :], mask[:, d]).then_inc(mask_stored, 16)
                pool.wait_ge(mask_stored, 16 * (d + 1))
                chain(pool.tensor_tensor(own, absent, ln_own, op=ALU.subtract))
            pool.memset(node_a, 0.0).then_inc(acc_cleared, 1)
            pool.wait_ge(inv_stored, 16)
            with pool.Fori(0, NG) as g:
                pool.tensor_copy(idx_slot[:], idx_cnt[:, bass.ds(g * GT, GT)]).then_inc(pool_step, 1)
                pool.wait_ge(pool_step, g * 2 + 1)
                settle(pool)
                for k in range(GT):
                    pool.indirect_dma_start(w_slot[:, k:k + 1], None, inv_d,
                                            bass.IndirectOffsetOnAxis(ap=idx_slot[:, k:k + 1], axis=0)).then_inc(w_landed, 16)
                pool.wait_ge(w_landed, (g + 1) * 16 * GT)
                pool.tensor_copy(edge[:, REL_W, bass.ds(g * GT, GT)], w_slot[:]).then_inc(pool_step, 1)
                pool.wait_ge(pool_step, g * 2 + 2)
            next_phase(pool)
            next_phase(pool)
            pool.iota(iota_row[:], pattern=[[1, N]], base=0, channel_multiplier=0, allow_small_or_imprecise_dtypes=True).then_inc(iota_ready, 1)
            for c in range(2):
                W, root, b = (a[f"L1_gnn_{n}{c + 1}"] for n in ("W", "root", "b"))
                pool.dma_start(bias_row, spread(b, P)).then_inc(bias_loaded, 16)
                for h in range(2):
                    if c:
                        pool.wait_ge(w_ready, unit(2 * (R + 1) * c + h - 2))
                    pool.dma_start(w_raw[:, h], root.rearrange("(k p) c -> p k c", p=128)[:, :, h * HD:(h + 1) * HD]).then_inc(raw_loaded[h], 16)
                with pool.Fori(0, R) as r:
                    for h in range(2):
                        pool.wait_ge(w_ready, unit(r * 2 + ((c * (R + 1) + 1) * 2 + h - 2)))
                        pool.dma_start(w_raw[:, h], W[bass.ds(r, 1), :, h * HD:(h + 1) * HD].rearrange("o (k p) c -> p (o k) c", p=128)).then_inc(raw_loaded[h], 16)
                for i in range(4):
                    pool.wait_ge(y_stored[i], 16 * (R * 2 * NT // 4 * (c + 1) + 1))
                sum_pool(pool, c, y_d, D)
                next_phase(pool)
            for c in range(2):
                pool.wait_ge(xs_stored, 16 * (c + 1))
                sum_pool(pool, 2 + c, xs_d, G2)
            next_phase(pool)
            pool.memset(w3, 0.0).then_inc(w3_cleared, 1)
            next_phase(pool)
            next_phase(pool)

        @block.scalar
        def _(act):
            for s in (prod_taken, weight_made, hT_ready):
                act.sem_inc(s, PRE)
            act.sem_inc(turned_taken, 3 * PRE)
            act_turn(act, "turn_act", xT, KD)
            def act_logs(d):
                act.wait_ge(tile_taken, 4 * (d + 1))
                if d:
                    act.wait_ge(mask_stored, 16 * d)
                act.activation(ln_row, mask[:, d], ACT.Relu, bias=minus_one[0:P, 0:1]).then_inc(ln_shifted, 1)
                act.wait_ge(ln_shifted, d + 1)
                act.activation(ln_row, ln_row, ACT.Ln, bias=ones[0:P, 0:1]).then_inc(ln_out, 1)
                act.wait_ge(ln_in, d + 1)
                act.activation(ln_own, ln_own, ACT.Ln).then_inc(ln_out, 1)

            for d in range(NT):
                act.wait_ge(tile_counted, d + 1)
                for c in range(3):
                    act.copy(mask[:, d, CO[c]:CO[c] + CW[c]], bank[4 * (d % 2) + c][0:P, 0:CW[c]]).then_inc(tile_taken, 1)
                act.copy(degree[:, d], bank[4 * (d % 2) + 3][0:P, 0:16]).then_inc(tile_taken, 1)
                act_logs(d)
            act_sqrt(act, "sqrt_act", dinv[:])
            next_phase(act)
            with act.Fori(0, H0) as h:
                for n in range(NT):
                    act.wait_ge(h_made, unit(h * NT + n))
                    if n == 0:
                        act.wait_ge(agg_made, unit(h * NT - 1))
                    act.copy(h_head[:, n], bank[5 + n % 2][0:P, 0:C0]).then_inc(h_ready, 1)
                act.wait_ge(acc_cleared, 1)
                act_s_row(act, h, s_row)
                act_units(act, h, score, turned_score, True)
            next_phase(act)
            act_s_row(act, H0, s_row)
            act_units(act, H0, score, turned_score, False)
            act_sqrt(act, "sqrt_act", rstd[:])
            next_phase(act)
            for c in range(2):
                act_turn(act, "turn_act", xT_hi, KD, piece_high)
                for h in range(2):
                    for n in range(NT):
                        act.wait_ge(prod_made, unit((c * (R + 1) * 2 + h) * NT + n))
                        act.copy(node_a[:, n, h * HD:(h + 1) * HD], bank[(h * NT + n) % 4][0:P, 0:HD]).then_inc(prod_taken, 1)
                with act.Fori(0, R) as r:
                    for h in range(2):
                        for n in range(NT):
                            i = (h * NT + n) % 4
                            act.wait_ge(prod_made, unit(r * (2 * NT) + ((c * (R + 1) + 1) * 2 + h) * NT + n))
                            act.wait_ge(y_stored[i], (r * 5 + (c * 5 * R + (h * NT + n) // 4 + 1)) * 16)
                            act.copy(y_stage[:, i], bank[i][0:P, 0:HD]).then_inc(prod_taken, 1)
                if c == 0:
                    for d in range(NT):
                        act.wait_ge(sum_taken, d + 1)
                        act.activation(node_a[:, d], node_a[:, d], ACT.Relu)
                if c == 1:
                    act_sqrt(act, "sqrt_act", rstd[:])
                next_phase(act)
            act_turn(act, "turn_act", xT, KD)
            act.wait_ge(bulk_loaded, 16 * 7)
            for c, (t0, nt) in enumerate(PARTS):
                act.wait_ge(t_made, c + 1)
                act.activation(tT[:, t0 * P:(t0 + nt) * P], bank[6][0:BOT, 0:nt * P], ACT.Relu, bias=bd_col).then_inc(t_taken, 1)
            act_turn(act, "turn_act", xT, KD)
            next_phase(act)
            act_turn(act, "turn_act", zT, KG2)
            act_sqrt(act, "sqrt_act", rstd[:])
            next_phase(act)
            act_turn(act, "turn_act", xT, KD)
            act.wait_ge(w3_turned, 1)
            act.copy(w3T.rearrange("p a b -> p (a b)"), bank[6][:, 0:256]).then_inc(w3T_ready, 1)
            for n in range(NT):
                for g in range(3):
                    q = 3 * n + g
                    act.wait_ge(f_made, q + 1)
                    act.copy(res3[:, n, g * 256:(g + 1) * 256].rearrange("p (c f) -> p c f", c=2),
                             bank[q % 6][0:P, :].rearrange("p (c i f) -> p c i f", c=2, i=2)[:, :, 1]).then_inc(r_taken, 1)
            next_phase(act)
            for c in range(3):
                ins = act_spread(act, V3, c, 5, s_row3[:, 0], s_low3[:, 0])
            ins.then_inc(s_row_ready, 1)

            def act_3(u, k):
                if k + 2 >= 0:
                    act_unit_exp(act, u + (k + 2), k + 2, score3[:, (k + 2) % 4])
                if k + 1 >= 0:
                    act_unit_take(act, u + (k + 1), turned3[:, (k + 1) % 2])

            def act_pair(i, last):
                for k in range(PAIR):
                    u = i * PAIR + V3
                    if k + 2 < PAIR or not last:
                        act_3(u, k)
                    elif k + 1 < PAIR:
                        act_unit_take(act, u + (k + 1), turned3[:, (k + 1) % 2])
                    q, d = k // NT + 1, k % NT
                    if 3 <= d < 6 and (q == 1 or not last):
                        ins = act_spread(act, u + q * NT, d - 3, 5, s_row3[:, q % 2], s_low3[:, q % 2])
                        if d == 5:
                            ins.then_inc(s_row_ready, 1)

            for k in (-2, -1):
                act_3(V3, k)
            with act.Fori(0, H3 // 2 - 1) as i:
                act_pair(i, False)
            act_pair(H3 // 2 - 1, True)
            act_sqrt(act, "sqrt_act", rstd[:])

        @block.tensor
        def _(pe):
            for s in (s_spread, agg_made, h_made, part_made, prod_made, hidden_turned):
                pe.sem_inc(s, PRE)
            pe.sem_inc(score_turned, 3 * PRE)
            for s in hot_used + slot_used:
                pe.sem_inc(s, 1)
            pe.wait_ge(consts, 9)
            pe.wait_ge(diag_ready, 1)
            for i in range(4):
                w = 128 if i % 2 == 0 else ROWS1
                o = 256 * (i // 2) + 128 * (i % 2)
                ins = pe.matmul(bank[7][0:NT, o:o + w], ones[:, 0:NT], diags[:, i, 0:w], start=True, stop=True)
            ins.then_inc(spans_spread, 1)
            pe.wait_ge(reach_ready, 1)
            pe.matmul(bank[7][0:1, 448:448 + NT + 1], reach[:, 4:5], tri, start=True, stop=True)
            pe.matmul(bank[7][0:1, 449 + NT:449 + 2 * NT], reach[:, 2:3], ident[0:NT, 0:NT], start=True, stop=True).then_inc(table_made, 1)
            for i in range(4):
                pe.matmul(bank[i][:, 0:128], rows[:, i, 0, :], ident[:], start=True, stop=True)
                ins = pe.matmul(bank[i][:, 128:ET], rows[0:ROWS1, i, 1, :], ident[0:ROWS1, 0:ROWS1], start=True, stop=True)
            ins.then_inc(edges_turned, 1)
            pe.wait_ge(edges_taken, 1)
            pe.wait_ge(bulk_loaded, 16)
            pe_turn(pe, "turn_pe", node_a, KD)
            pe.wait_ge(piece_taken, counts["turn_pe"])
            pe.wait_ge(table_ready, 1)
            runs = runs_of(pe)
            for d in range(NT):
                first, end = runs[d], runs[d + 1]
                acc = bank[4 * (d % 2):4 * (d % 2) + 4]
                widths = CW + [16]
                if d >= 2:
                    pe.wait_ge(tile_taken, 4 * (d - 1))
                for b, w in zip(acc, widths):
                    pe.matmul(b[0:P, 0:w], zeros[0:1, 0:P], zeros[0:1, 0:w], start=True, stop=False)
                shift = pe.value_load(table[0:1, NT + 1 + d:NT + 2 + d], min_val=-NT * NG * GT, max_val=ET)
                with pe.Fori(first, end) as j:
                    tile = nc.s_assert_within(j * GT + shift, 0, ET - 1)
                    for k in range(GT):
                        pe.wait_ge(hot_ready[k], j + 1)
                        for c in range(3):
                            pe.matmul(acc[c][0:P, 0:CW[c]], hot_dst[:, k], hot_src[:, k, CO[c]:CO[c] + CW[c]], start=False, stop=False)
                        ins = pe.matmul(acc[3][0:P, 0:16], hot_dst[:, k], feat[:, bass.ds(tile + k, 1)].rearrange("p o c -> p (o c)"), start=False, stop=False)
                        ins.then_inc(hot_used[k], 1)
                for b, w in zip(acc, widths):
                    ins = pe.matmul(b[0:P, 0:w], zeros[0:1, 0:P], zeros[0:1, 0:w], start=False, stop=True)
                ins.then_inc(tile_counted, 1)
            next_phase(pe)
            with pe.Fori(0, H0) as h:
                pe.wait_ge(w_in_loaded, (h + 1) * 16)
                for n in range(NT):
                    if n < 2:
                        pe.wait_ge(hT_ready, unit(h * NT - 1))
                        pe.wait_ge(part_taken, unit(h * NT - 1))
                    else:
                        pe.wait_ge(h_ready, h * NT + (n - 1))
                    for k in range(KD):
                        ins = pe.matmul(bank[5 + n % 2][0:P, 0:C0], xT[:, k, n * P:(n + 1) * P], w_in[:, k], start=(k == 0), stop=(k == KD - 1))
                    ins.then_inc(h_made, 1)
                pe_s_row(pe, h, s_diag)
                pe.wait_ge(w_out_loaded, (h + 1) * 16)
                pe_units(pe, h, score, turned_score, lambda d: [3 + d % 2], lambda t: [h_head[:, t]], True)
            next_phase(pe)
            pe_s_row(pe, H0, s_diag)
            pe_units(pe, H0, score, turned_score, lambda d: [3 + 2 * (d % 2), 4 + 2 * (d % 2)],
                     lambda t: [node_a[:, t, 0:HD], node_a[:, t, HD:D]], False)
            next_phase(pe)
            for c in range(2):
                pe_turn(pe, "turn_pe", node_a if c else node_b, KD)
                pe.wait_ge(piece_taken, counts["turn_pe"])

                def half_product(m, p, h):
                    pe.wait_ge(w_ready, unit(m))
                    for n in range(NT):
                        pe.wait_ge(prod_taken, unit(p + (n - 4)))
                        b, v = bank[(h * NT + n) % 4][0:P, 0:HD], slice(n * P, (n + 1) * P)
                        for k in range(KD):
                            pe.matmul(b, xT_hi[:, k, v], w_hi[:, h, k], start=(k == 0), stop=False)
                            pe.matmul(b, xT_hi[:, k, v], w_lo[:, h, k], start=False, stop=False)
                            ins = pe.matmul(b, xT_lo[:, k, v], w_hi[:, h, k], start=False, stop=(k == KD - 1))
                        ins.then_inc(prod_made, 1)

                m0 = c * (R + 1) * 2
                for h in range(2):
                    half_product(m0 + h, (m0 + h) * NT, h)
                with pe.Fori(0, R) as r:
                    for h in range(2):
                        half_product(r * 2 + (m0 + 2 + h), r * (2 * NT) + (m0 + 2 + h) * NT, h)
                pe.wait_ge(prod_taken, unit((m0 + 2 * (R + 1)) * NT - 1))
                sum_pe(pe, c, D)
                next_phase(pe)
            pe_turn(pe, "turn_pe", node_b, KD)
            pe.wait_ge(piece_taken, counts["turn_pe"])
            pe.wait_ge(bulk_loaded, 16 * 7)
            for c, (t0, nt) in enumerate(PARTS):
                if c:
                    pe.wait_ge(t_taken, c)
                for k in range(KD):
                    ins = pe.matmul(bank[6][0:BOT, 0:nt * P], wd[:, k], xT[:, k, t0 * P:(t0 + nt) * P], start=(k == 0), stop=(k == KD - 1))
                ins.then_inc(t_made, 1)
            pe.wait_ge(t_taken, 3)
            for n in range(NT):
                if n >= 2:
                    pe.wait_ge(mm_taken, n - 1)
                for h in range(2):
                    ins = pe.matmul(bank[2 * (n % 2) + h][0:P, 0:HD], tT[:, n * P:(n + 1) * P], wu[:, h * HD:(h + 1) * HD], start=True, stop=True)
                ins.then_inc(mm_made, 1)
            pe.wait_ge(mm_taken, NT)
            pe_turn(pe, "turn_pe", node_a, KD)
            pe.wait_ge(piece_taken, counts["turn_pe"])
            for n in range(NT):
                if n >= 2:
                    pe.wait_ge(mm_taken, NT + n - 1)
                for k in range(KD):
                    ins = pe.matmul(bank[6 + n % 2][0:P, 0:G2], xT[:, k, n * P:(n + 1) * P], gw1[:, k], start=(k == 0), stop=(k == KD - 1))
                ins.then_inc(mm_made, 1)
            sum_pe(pe, 2, G2)
            sum_pe(pe, 3, G2)
            next_phase(pe)
            pe_turn(pe, "turn_pe", agg2, KG2)
            pe.wait_ge(piece_taken, counts["turn_pe"])
            pe.wait_ge(bulk_loaded, 16 * 9)
            for n in range(NT):
                if n >= 2:
                    pe.wait_ge(mm_taken, 2 * NT + n - 1)
                for h in range(2):
                    for k in range(KG2):
                        ins = pe.matmul(bank[2 * (n % 2) + h][0:P, 0:HD], zT[:, k, n * P:(n + 1) * P], gw2[:, k, h * HD:(h + 1) * HD],
                                        start=(k == 0), stop=(k == KG2 - 1))
                ins.then_inc(mm_made, 1)
            next_phase(pe)
            pe_turn(pe, "turn_pe", node_b, KD)
            pe.wait_ge(w3_loaded, 16 * 6)
            for i in range(2):
                ins = pe.transpose(bank[6][:, i * 128:(i + 1) * 128], w3[:, i], ident[:])
            ins.then_inc(w3_turned, 1)
            pe.wait_ge(w3T_ready, 1)
            pe.wait_ge(piece_taken, counts["turn_pe"])
            for n in range(NT):
                for g in range(3):
                    q = 3 * n + g
                    if q >= 6:
                        pe.wait_ge(f_taken, q - 5)
                        pe.wait_ge(r_taken, q - 5)
                    for c in range(2):
                        ins = pe.matmul(bank[q % 6][0:P, c * 256:(c + 1) * 256], xT[:, 2 * g + c, n * P:(n + 1) * P],
                                        w3T.rearrange("p a b -> p (a b)"), start=True, stop=True)
                    ins.then_inc(f_made, 1)
            next_phase(pe)
            for t in range(NT):
                pe_spread(pe, V3 + t, t, 5, s_diag3[:, t % 4])
            pe_unit_turn(pe, V3, score3[:, 0])

            def pe_pair(i, last):
                for k in range(PAIR):
                    u, q, d = i * PAIR + V3, k // NT, k % NT
                    if k + 1 < PAIR or not last:
                        pe_unit_turn(pe, u + (k + 1), score3[:, (k + 1) % 4])
                    h = i * 2 + q
                    pe_unit_sum(pe, u + k, turned3[:, k % 2], [3 + k % 2], lambda t: [node_a[:, t, bass.ds(h * C3, C3)]])
                    if d < NT // 2 and (q == 0 or not last):
                        if d == 0:
                            pe.wait_ge(s_row_ready, h + (H0 + 2))
                        for t in (2 * d, 2 * d + 1):
                            pe_spread(pe, u + ((q + 1) * NT + t), t, 5, s_diag3[:, ((q + 1) * NT + t) % 4])

            with pe.Fori(0, H3 // 2 - 1) as i:
                pe_pair(i, False)
            pe_pair(H3 // 2 - 1, True)

        @block.vector
        def _(dve):
            chain = Chain(dve, dve_step)
            for s in (w_ready, score_masked, agg_taken, hidden_ready, part_taken):
                dve.sem_inc(s, PRE)
            chain.mark(dve.memset(raw[:, 0], int(NEVER)))
            chain.mark(dve.memset(raw[:, 1:3], 0))
            chain.mark(dve.memset(rows[:, 3], 0.0))
            chain.mark(dve.memset(edge[:, DST, ET:EP], NEVER))
            chain.mark(dve.memset(edge[:, SRC:EW + 1, ET:EP], 0.0))
            chain.mark(dve.memset(edge[:, REL_W], 0.0))
            chain.wait()
            dve.memset(feat, 0.0).then_inc(rows_ready, 1)
            dve.wait_ge(consts, 9)
            chain.mark(dve.tensor_copy(iota_half, iota_row[:]))
            chain(dve.tensor_copy(tile_start[:], start_i))
            dve.wait_ge(loaded, 16 * 12)
            chain(dve.tensor_copy(rows[:, 0:3], raw[:, 0:3]))
            chain.mark(dve.tensor_reduce(span[:, 0:2], rows[:, 0], axis=AX_X, op=ALU.min))
            chain(dve.scalar_tensor_tensor(dst_low, rows[:, 0], NEVER, rows[:, 0], op0=ALU.is_lt, op1=ALU.mult))
            chain(dve.tensor_reduce(span[:, 2:4], dst_low, axis=AX_X, op=ALU.max))
            for i in range(4):
                ins = dve.tensor_scalar(diags[:, i], ident[:], span[:, i:i + 1], None, op0=ALU.mult)
            ins.then_inc(diag_ready, 1)
            dve.wait_ge(spans_spread, 1)
            chain.mark(dve.tensor_scalar(touch[:, 0], bank[7][0:NT, 0:ET], tile_start[0:NT], float(P), op0=ALU.subtract, op1=ALU.is_lt))
            chain(dve.tensor_scalar(touch[:, 1], bank[7][0:NT, 256:256 + ET], tile_start[0:NT], None, op0=ALU.is_ge))
            chain(dve.tensor_tensor(touch[:, 2], touch[:, 0], touch[:, 1], op=ALU.mult))
            chain.mark(dve.scalar_tensor_tensor(touch[:, 0], iota_row[0:NT, 0:ET], 1.0, touch[:, 2], op0=ALU.add, op1=ALU.mult))
            chain(dve.tensor_scalar(touch[:, 3], iota_row[0:NT, 0:ET], -1.0, float(ET), op0=ALU.mult, op1=ALU.add))
            chain.mark(dve.tensor_tensor(touch[:, 1], touch[:, 3], touch[:, 2], op=ALU.mult))
            chain(dve.tensor_reduce(reach[:, 0:1], touch[:, 0], axis=AX_X, op=ALU.max))
            chain(dve.tensor_reduce(reach[:, 1:2], touch[:, 1], axis=AX_X, op=ALU.max))
            chain(dve.tensor_scalar(reach[:, 5:6], reach[:, 1:2], 1.0, -1.0, op0=ALU.max, op1=ALU.mult))
            chain(dve.tensor_scalar(reach[:, 2:3], reach[:, 5:6], float(ET), None, op0=ALU.add))
            chain(dve.tensor_tensor(reach[:, 3:4], reach[:, 0:1], reach[:, 2:3], op=ALU.subtract))
            chain(dve.tensor_scalar(reach[:, 6:7], reach[:, 3:4], 1.0, None, op0=ALU.max))
            chain(dve.tensor_scalar(touch[:, 3, 0:NG], iota_row[0:NT, 0:NG], float(GT), reach[:, 6:7], op0=ALU.mult, op1=ALU.is_lt))
            dve.tensor_reduce(reach[:, 4:5], touch[:, 3, 0:NG], axis=AX_X, op=ALU.add).then_inc(reach_ready, 1)
            dve.wait_ge(table_made, 1)
            chain(dve.tensor_copy(diags[0:1, 0, 0:2 * NT + 1], bank[7][0:1, 448:448 + 2 * NT + 1]))
            chain.mark(dve.tensor_copy(table[:, 0:NT + 1], diags[0:1, 0, 0:NT + 1]))
            chain(dve.scalar_tensor_tensor(diags[0:1, 1, 0:NT], diags[0:1, 0, 0:NT], -float(GT), diags[0:1, 0, NT + 1:2 * NT + 1], op0=ALU.mult, op1=ALU.add))
            dve.tensor_copy(table[:, NT + 1:], diags[0:1, 1, 0:NT]).then_inc(table_ready, 1)
            dve.wait_ge(edges_turned, 1)
            for i in range(4):
                chain.mark(dve.tensor_copy(edge[:, i, 0:ET], bank[i][:, 0:ET]))
            chain.wait()
            chain(dve.scalar_tensor_tensor(edge[:, TMP], edge[:, TYP], float(N), edge[:, SRC], op0=ALU.mult, op1=ALU.add))
            chain.mark(dve.tensor_copy(idx_y[:], edge[:, TMP]))
            chain(dve.tensor_copy(idx_src[:], edge[:, SRC]))
            chain(dve.tensor_scalar(edge[:, TMP], edge[:, DST], float(N - 1), float(R), op0=ALU.min, op1=ALU.mult))
            chain(dve.tensor_tensor(edge[:, TMP], edge[:, TMP], edge[:, TYP], op=ALU.add))
            chain.mark(dve.tensor_copy(idx_cnt[:], edge[:, TMP]))
            chain(dve.tensor_copy(ew_parts[:, 0, 0:EP], edge[:, EW]))
            chain(dve.tensor_tensor(edge[:, TMP], edge[:, EW], ew_parts[:, 0, 0:EP], op=ALU.subtract))
            chain(dve.tensor_copy(ew_parts[:, 1, 0:EP], edge[:, TMP]))
            chain(dve.tensor_tensor(edge[:, TMP], edge[:, TMP], ew_parts[:, 1, 0:EP], op=ALU.subtract))
            chain(dve.tensor_copy(ew_parts[:, 2, 0:EP], edge[:, TMP]))
            for r in range(R):
                chain.mark(dve.tensor_scalar(feat[:, :, r], edge[:, TYP], float(r), None, op0=ALU.is_equal))
            for c in range(3):
                chain.mark(dve.tensor_copy(feat[:, :, R + c], ew_parts[:, c, 0:EP]))
            chain.wait()
            dve.drain().then_inc(edges_taken, 1)
            dve.wait_ge(table_ready, 1)

            def mark_absent(d):
                dve.wait_ge(ln_shifted, d + 1)
                dve.wait_ge(ln_in, d + 1)
                dve.tensor_scalar(mask[:, d], mask[:, d], 0.5, ABSENT, op0=ALU.is_lt, op1=ALU.mult).then_inc(absent_marked, 1)

            runs = runs_of(dve)
            for d in range(NT):
                first, end = runs[d], runs[d + 1]
                shift = dve.value_load(table[0:1, NT + 1 + d:NT + 2 + d], min_val=-NT * NG * GT, max_val=ET)
                if d >= 2:
                    mark_absent(d - 2)
                with dve.Fori(first, end) as j:
                    tile = nc.s_assert_within(j * GT + shift, 0, ET - 1)
                    for k in range(GT):
                        t = tile + k
                        dve.wait_ge(hot_used[k], j + 1)
                        dve.tensor_scalar(hot_dst[:, k], iota_row[:, d * P:(d + 1) * P], edge[:, DST, bass.ds(t, 1)], None, op0=ALU.is_equal)
                        ins = dve.tensor_scalar(hot_src[:, k], iota_half, edge[:, SRC, bass.ds(t, 1)], None, op0=ALU.is_equal)
                        ins.then_inc(hot_ready[k], 1)
            for d in (NT - 2, NT - 1):
                mark_absent(d)
            dve.wait_ge(tile_taken, 4 * NT)
            chain(dve.tensor_scalar(inv_count[:], degree[:, :, 0:R], 1.0, None, op0=ALU.max))
            dve.reciprocal(inv_count[:], inv_count[:]).then_inc(inv_ready, 1)
            chain(dve.tensor_tensor(dinv[:], degree[:, :, R], degree[:, :, R + 1], op=ALU.add))
            chain(dve.scalar_tensor_tensor(dinv[:], dinv[:], 1.0, degree[:, :, R + 2], op0=ALU.add, op1=ALU.add))
            dve.drain().then_inc(sqrt_in, 1)
            dve.wait_ge(sqrt_done, tick("sqrt_dve"))
            chain(dve.reciprocal(dinv[:], dinv[:]))
            next_phase(dve)
            A_STEPS = 7 * NT + 1
            with dve.Fori(0, H0) as h:
                chain.loop(h, A_STEPS)
                dve.wait_ge(att_loaded, (h + 1) * 32)
                dve.wait_ge(b1_loaded, (h + 1) * 16)
                for n in range(NT):
                    dve.wait_ge(h_ready, h * NT + (n + 1))
                    for i, al in enumerate((al_s, al_d)):
                        chain(dve.tensor_tensor_reduce(out=hidden[:, i], in0=h_head[:, n], in1=att_rows[:, i], scale=1.0, scalar=0.0,
                                                       op0=ALU.mult, op1=ALU.add, accum_out=al[:, n:n + 1]))
                chain(dve.tensor_scalar(al_d[:], al_d[:], SLOPE - 1.0, None, op0=ALU.mult))
                dve_s_row(dve, h, s_diag)

                def leave_a(u, d):
                    r = dve_unit_rden(dve, chain, u, d)
                    dve.wait_ge(hidden_turned, unit(u - 2))
                    b = bank[3 + d % 2][0:P, 0:C0]
                    chain(dve.scalar_tensor_tensor(hidden[:, d % 2], b, r, b1_row, op0=ALU.mult, op1=ALU.add))
                    dve.tensor_scalar(b, hidden[:, d % 2], 0.0, None, op0=ALU.min).then_inc(elu_in, 1)

                def elu_a(u, d):
                    dve.wait_ge(elu_exp, u + 1)
                    chain(dve.scalar_tensor_tensor(hidden[:, d % 2], bank[3 + d % 2][0:P, 0:C0], -1.0, hidden[:, d % 2], op0=ALU.add, op1=ALU.max))
                    settle(dve)
                    dve.drain().then_inc(hidden_ready, 1)
                    dve.drain().then_inc(agg_taken, 1)

                def part_a(u, d):
                    dve.wait_ge(part_made, unit(u))
                    for g in range(2):
                        v = node_a[:, d, g * HD:(g + 1) * HD]
                        ins = dve.tensor_tensor(v, v, bank[6 + g][0:P, 0:HD], op=ALU.add)
                    ins.then_inc(part_taken, 1)

                dve.wait_ge(acc_cleared, 1)
                dve_units(dve, chain, h, score, s_row, leave_a, elu_a, part_a)
                chain.end(H0, A_STEPS)
            next_phase(dve)
            dve.wait_ge(att_loaded, (H0 + 1) * 32)
            dve.wait_ge(b1_loaded, (H0 + 1) * 16)

            def wide_logit(n, i, al):
                return dve.tensor_tensor_reduce(out=logit_out[:, n % 2], in0=node_a[:, n], in1=wide_rows[:, i], scale=1.0, scalar=0.0,
                                                op0=ALU.mult, op1=ALU.add, accum_out=al[:, n:n + 1])

            def before_b(n):
                chain(wide_logit(n, 1, al_d))
                chain(dve.tensor_scalar(al_d[:, n:n + 1], al_d[:, n:n + 1], SLOPE - 1.0, None, op0=ALU.mult))

            for n in range(NT):
                if n >= 2:
                    chain.wait()
                chain.mark(wide_logit(n, 0, al_s))
            chain.wait()
            dve_s_row(dve, H0, s_diag)

            def leave_b(u, d):
                r = dve_unit_rden(dve, chain, u, d)
                for g in range(2):
                    v = slice(g * HD, (g + 1) * HD)
                    chain.mark(dve.scalar_tensor_tensor(node_b[:, d, v], bank[3 + 2 * (d % 2) + g][0:P, 0:HD], r, b2_row[:, v], op0=ALU.mult, op1=ALU.add))
                chain.wait()
                settle(dve)
                dve.drain().then_inc(agg_taken, 1)
                dve.wait_ge(x_loaded[d % 2], 16 * (d // 2 + 1))
                dve.tensor_tensor(node_b[:, d], node_b[:, d], x_slot[:, d % 2], op=ALU.add).then_inc(x_used, 1)
                dve.wait_ge(x_used, d + 1)
                dve_stats(dve, chain, node_b, d)

            dve_units(dve, chain, H0, score, s_row, leave_b, None, None, before_b)
            dve_norm(dve, chain, node_b, node_b)
            next_phase(dve)
            for c in range(2):
                dve_turn_low(dve, c)

                def split(m, i, h):
                    dve.wait_ge(raw_loaded[h], (i + 1) * 16)
                    dve.wait_ge(prod_made, unit(m * NT + (-NT - 1)))
                    chain(dve.tensor_copy(w_hi[:, h], w_raw[:, h]))
                    dve.tensor_tensor(w_lo[:, h], w_raw[:, h], w_hi[:, h].bitcast(F32), op=ALU.subtract).then_inc(w_ready, 1)

                m0 = c * (R + 1) * 2
                for h in range(2):
                    if m0 + h >= 2:
                        split(m0 + h, c * (R + 1), h)
                    else:
                        dve.wait_ge(raw_loaded[h], 16)
                        chain(dve.tensor_copy(w_hi[:, h], w_raw[:, h]))
                        dve.tensor_tensor(w_lo[:, h], w_raw[:, h], w_hi[:, h].bitcast(F32), op=ALU.subtract).then_inc(w_ready, 1)
                with dve.Fori(0, R) as r:
                    chain.loop(r, 2)
                    for h in range(2):
                        split(r * 2 + (m0 + 2 + h), r + (c * (R + 1) + 1), h)
                    chain.end(R, 2)
                dve.wait_ge(w_ready, unit(m0 + 2 * (R + 1) - 1))
                dve.wait_ge(bias_loaded, 16 * (1 + c))
                to = node_a if c == 0 else node_b
                dve.wait_ge(prod_taken, unit((m0 + 2) * NT - 1))
                for d in range(NT):
                    chain.mark(dve.tensor_tensor(node_a[:, d], node_a[:, d], bias_row, op=ALU.add))
                chain.wait()
                if c == 1:
                    for d in range(NT):
                        chain.mark(dve.tensor_tensor(node_b[:, d], node_b[:, d], node_a[:, d], op=ALU.add))
                    chain.wait()

                def take(d):
                    for g in range(2):
                        v = to[:, d, g * HD:(g + 1) * HD]
                        ins = dve.tensor_tensor(v, v, bank[2 * (d % 2) + g][0:P, 0:HD], op=ALU.add)
                    return ins

                sum_dve(dve, c, idx_y, REL_W, take)
                if c == 1:
                    for d in range(NT):
                        if d == 0:
                            dve.wait_ge(sum_taken, 2 * NT)
                        dve_stats(dve, chain, node_b, d)
                    dve_norm(dve, chain, node_b, node_b)
                next_phase(dve)
            dve.wait_ge(bulk_loaded, 16 * 7)
            for n in range(NT):
                dve.wait_ge(mm_made, n + 1)
                for g in range(2):
                    v = slice(g * HD, (g + 1) * HD)
                    chain.mark(dve.tensor_tensor(node_a[:, n, v], bank[2 * (n % 2) + g][0:P, 0:HD], bu_row[:, v], op=ALU.add))
                chain.wait()
                dve.tensor_tensor(node_a[:, n], node_a[:, n], node_b[:, n], op=ALU.add).then_inc(mm_taken, 1)
            for n in range(NT):
                dve.wait_ge(mm_made, NT + n + 1)
                dve.tensor_scalar(xs[:, n], bank[6 + n % 2][0:P, 0:G2], dinv[:, n:n + 1], None, op0=ALU.mult).then_inc(mm_taken, 1)
            dve.drain().then_inc(xs_ready, 1)

            def take_1(d):
                chain(dve.tensor_tensor(agg2[:, d], bank[2 * (d % 2)][0:P, 0:G2], xs[:, d], op=ALU.add))
                chain(dve.scalar_tensor_tensor(agg2[:, d], agg2[:, d], dinv[:, d:d + 1], gb1_row, op0=ALU.mult, op1=ALU.add))
                return dve.tensor_scalar(xs[:, d], agg2[:, d], 0.0, dinv[:, d:d + 1], op0=ALU.max, op1=ALU.mult)

            def take_2(d):
                chain(dve.tensor_tensor(agg2[:, d], bank[2 * (d % 2)][0:P, 0:G2], xs[:, d], op=ALU.add))
                return dve.tensor_scalar(agg2[:, d], agg2[:, d], dinv[:, d:d + 1], None, op0=ALU.mult)

            sum_dve(dve, 2, idx_src, EW, take_1)
            dve.drain().then_inc(xs_ready, 1)
            sum_dve(dve, 3, idx_src, EW, take_2)
            next_phase(dve)
            dve.wait_ge(bulk_loaded, 16 * 9)
            for n in range(NT):
                dve.wait_ge(mm_made, 2 * NT + n + 1)
                for g in range(2):
                    v = slice(g * HD, (g + 1) * HD)
                    chain.mark(dve.tensor_tensor(node_a[:, n, v], bank[2 * (n % 2) + g][0:P, 0:HD], gb2_row[:, v], op=ALU.add))
                chain.wait()
                dve.tensor_tensor(node_b[:, n], node_b[:, n], node_a[:, n], op=ALU.add).then_inc(mm_taken, 1)
                dve.wait_ge(mm_taken, 2 * NT + n + 1)
                dve_stats(dve, chain, node_b, n)
            dve_norm(dve, chain, node_b, node_b)
            next_phase(dve)
            dve.wait_ge(w3_loaded, 16 * 6)
            for n in range(NT):
                for g in range(3):
                    q = 3 * n + g
                    dve.wait_ge(f_made, q + 1)
                    dve.wait_ge(r_taken, q + 1)
                    dve.tensor_copy(node_a[:, n, g * 256:(g + 1) * 256].rearrange("p (c f) -> p c f", c=2),
                                    bank[q % 6][0:P, :].rearrange("p (c i f) -> p c i f", c=2, i=2)[:, :, 0]).then_inc(f_taken, 1)
                dve.wait_ge(f_taken, 3 * (n + 1))
                for i in range(2):
                    chain(dve.tensor_tensor(scratch3, node_a[:, n], att3[:, i], op=ALU.mult))
                    chain(dve.tensor_reduce(al3[:, i, n], scratch3.rearrange("p (h c) -> p h c", c=C3), axis=AX_X, op=ALU.add))
            next_phase(dve)
            dve.wait_ge(mask_loaded, 16)
            chain(dve.tensor_scalar(al3[:, 1], al3[:, 1], SLOPE - 1.0, None, op0=ALU.mult))

            def diag_3(v, k, h, t):
                dve_diag(dve, v, 4, s_diag3[:, k % 4], al3[:, 0, t, bass.ds(h, 1)])

            def mask_3(v, m, h, between=None):
                d = m % NT
                if d == 0:
                    dve.wait_ge(s_row_ready, h + (H0 + 2))
                q = (m // NT) % 2
                dve_unit_mask(dve, chain, v, 4, m, score3[:, m % 4], mask[:, d], s_row3[:, q], s_low3[:, q],
                              al3[:, 1, d, bass.ds(h, 1)], between)

            def rden_3(v, k):
                dve.wait_ge(weight_made, unit(v))
                r = rden[:, k % 4:k % 4 + 1]
                chain.mark(dve.tensor_scalar(r, den[:, k % 4:k % 4 + 1], TINY, None, op0=ALU.max))
                return lambda: chain.mark(dve.reciprocal(r, r))

            for t in range(NT):
                diag_3(V3 + t, t, 0, t)
            mask_3(V3, 0, 0)
            mask_3(V3 + 1, 1, 0)
            mask_3(V3 + 2, 2, 0, lambda: rden_3(V3, 0))

            def dve_pair(i, last):
                for k in range(PAIR):
                    u, q, d, m = i * PAIR + V3, k // NT, k % NT, k + 3

                    def between():
                        then = rden_3(u + (k + 1), k + 1) if k + 1 < PAIR or not last else None
                        if d < NT // 2 and (q == 0 or not last):
                            for t in (2 * d, 2 * d + 1):
                                n = (q + 1) * NT + t
                                diag_3(u + n, n, i * 2 + (q + 1), t)
                        return then

                    if m < PAIR or not last:
                        mask_3(u + m, m, i * 2 + m // NT, between)
                    else:
                        then = between()
                        if then:
                            chain.wait()
                            then()
                            chain.wait()
                    dve.wait_ge(agg_made, unit(u + k))
                    v = res3[:, d, bass.ds((i * 2 + q) * C3, C3)]
                    dve.scalar_tensor_tensor(v, bank[3 + k % 2][0:P, 0:C3], rden[:, k % 4:k % 4 + 1], v, op0=ALU.mult, op1=ALU.add).then_inc(agg_taken, 1)

            with dve.Fori(0, H3 // 2 - 1) as i:
                chain.loop(i, 3 * PAIR)
                dve_pair(i, False)
                chain.end(H3 // 2 - 1, 3 * PAIR)
            dve_pair(H3 // 2 - 1, True)
            dve.wait_ge(agg_taken, unit((H0 + 1 + H3) * NT - 1))
            for d in range(NT):
                chain.mark(dve.scalar_tensor_tensor(node_b[:, d], res3[:, d], 0.0, node_b[:, d], op0=ALU.max, op1=ALU.add))
            chain.wait()
            for d in range(NT):
                dve_stats(dve, chain, node_b, d)
            dve_norm(dve, chain, node_b, node_b)


_INS = ['x', 'src', 'dst', 'edge_type_8', 'edge_weight', 'L0_gnn_W1', 'L0_gnn_att_src1', 'L0_gnn_att_dst1', 'L0_gnn_b1',
        'L0_gnn_W2', 'L0_gnn_att_src2', 'L0_gnn_att_dst2', 'L0_gnn_b2', 'L1_gnn_W1', 'L1_gnn_root1', 'L1_gnn_b1',
        'L1_gnn_W2', 'L1_gnn_root2', 'L1_gnn_b2', 'L2_gnn_Wd', 'L2_gnn_bd', 'L2_gnn_Wu', 'L2_gnn_bu', 'L2_gnn_W1',
        'L2_gnn_b1', 'L2_gnn_W2', 'L2_gnn_b2', 'L3_gnn_W', 'L3_gnn_attn_l', 'L3_gnn_attn_r', 'L3_gnn_W_res']


def kernel(**inputs):
    import numpy as _np
    import concourse.bacc as _bacc
    from concourse import mybir as _mybir
    from concourse.bass_utils import run_bass_kernel_spmd as _run

    nc = _bacc.Bacc("TRN2", target_bir_lowering=False, num_devices=1)
    arrays, args = {}, {}
    for name in _INS:
        v = _np.ascontiguousarray(inputs[name])
        arrays[f"in_{name}_dram"] = v
        args[name] = nc.dram_tensor(f"in_{name}_dram", v.shape, _mybir.dt.from_np(v.dtype), kind="ExternalInput").ap()
    out = nc.dram_tensor("out_0_dram", inputs["x"].shape, _mybir.dt.float32, kind="ExternalOutput").ap()
    build(nc, args, out)
    r = _run(nc, [arrays], core_ids=[0])
    return r.results[0]["out_0_dram"]
```
